# Optimizing a Trainium2 kernel written in Bass

```python
import numpy as np
import jax
import jax.numpy as jnp

def _softmax(x, axis=-1):
    return jax.nn.softmax(x, axis=axis)

def _gelu(x):
    return jax.nn.gelu(x, approximate=True)

def _silu(x):
    return jax.nn.silu(x)

def _sigmoid(x):
    return jax.nn.sigmoid(x)

def _layernorm(x, axis=-1, eps=1e-05):
    m = jnp.mean(x, axis=axis, keepdims=True)
    v = jnp.var(x, axis=axis, keepdims=True)
    return (x - m) / jnp.sqrt(v + eps)

def _scatter_add(tgt, idx, src, axis=0):
    return tgt.at[idx].add(src)

def _segment_sum(src, seg, n):
    return jax.ops.segment_sum(src, seg, n)
kernel_name = 'mk_adaln_d2_jaxref_r8_3f3a02'

def setup_inputs(seed: int=0):
    np.random.seed(seed)
    _w = jnp.asarray

    def _L0_attn_setup():
        import jax, jax.numpy as jnp
        import numpy as np
        NUM_HEADS = 16
        LN_EPS = 1e-05

        def _gelu(x):
            return jax.nn.gelu(x, approximate=False)
        key = jax.random.key(seed)
        ks = jax.random.split(key, 12)
        B, S, E = (2, 256, 128)
        H = E // 2
        s = lambda fan_in: 1.0 / np.sqrt(fan_in)
        inp = {'x': jax.random.normal(ks[0], (B, S, E), jnp.float32), 'Wq': jax.random.normal(ks[1], (E, E), jnp.float32) * s(E), 'bq': jnp.zeros((E,), jnp.float32), 'Wk': jax.random.normal(ks[2], (E, E), jnp.float32) * s(E), 'bk': jnp.zeros((E,), jnp.float32), 'Wv': jax.random.normal(ks[3], (E, E), jnp.float32) * s(E), 'bv': jnp.zeros((E,), jnp.float32), 'Wo': jax.random.normal(ks[4], (E, E), jnp.float32) * s(E), 'bo': jnp.zeros((E,), jnp.float32), 'dp_w1': jax.random.normal(ks[5], (E, H), jnp.float32) * s(E), 'dp_b1': jnp.zeros((H,), jnp.float32), 'ln_g': jnp.ones((H,), jnp.float32), 'ln_b': jnp.zeros((H,), jnp.float32), 'dp_w2': jax.random.normal(ks[6], (H, 1), jnp.float32) * s(H), 'dp_b2': jnp.zeros((1,), jnp.float32), 'g_w1': jax.random.normal(ks[7], (1, 16), jnp.float32), 'g_b1': jnp.zeros((16,), jnp.float32), 'g_w2': jax.random.normal(ks[8], (16, 1), jnp.float32) * s(16), 'g_b2': jnp.zeros((1,), jnp.float32)}
        return inp
    _L0_attn_in = _L0_attn_setup()

    def _L0_ffn_setup():
        import jax, jax.numpy as jnp
        import numpy as np
        B, S, H, D, E = (4, 128, 128, 512, 8)
        key = jax.random.key(seed)
        ks = jax.random.split(key, 12)

        def init(k, shape, fan_in):
            return jax.random.normal(k, shape, jnp.float32) / np.float32(np.sqrt(fan_in))
        return {'x': jax.random.normal(ks[0], (B, S, H), jnp.float32), 'Wq': init(ks[1], (H, H), H), 'bq': jnp.zeros((H,), jnp.float32), 'Wk': init(ks[2], (H, H), H), 'bk': jnp.zeros((H,), jnp.float32), 'Wv': init(ks[3], (H, H), H), 'bv': jnp.zeros((H,), jnp.float32), 'Wo': init(ks[4], (H, H), H), 'bo': jnp.zeros((H,), jnp.float32), 'Wg': init(ks[5], (H, E), H), 'bg': jnp.zeros((E,), jnp.float32), 'W1': init(ks[6], (E, H, D), H), 'b1': jnp.zeros((E, D), jnp.float32), 'W2': init(ks[7], (E, D, H), D), 'b2': jnp.zeros((E, H), jnp.float32)}
    _L0_ffn_in = _L0_ffn_setup()
    _L0_c = _w((lambda *s: np.random.randn(*s).astype(np.float32) * 0.05)(16, 128))
    _L0_wmod = _w((lambda *s: np.random.randn(*s).astype(np.float32) * 0.05)(128, 6 * 128) * 128 ** (-0.5))

    def _L1_attn_setup():
        import jax, jax.numpy as jnp
        import numpy as np
        EPS = 1e-05

        def _layernorm(x, gamma, beta):
            m = jnp.mean(x, axis=-1, keepdims=True)
            v = jnp.mean(jnp.square(x - m), axis=-1, keepdims=True)
            return (x - m) * jax.lax.rsqrt(v + EPS) * gamma + beta
        key = jax.random.key(seed)
        B, Q, C, H = (4, 512, 128, 16)
        hd = C // H
        ks = jax.random.split(key, 8)
        s_in = 1.0 / np.sqrt(C)
        return {'x': jax.random.normal(ks[0], (B, Q, C), jnp.float32), 'qkv_w': jax.random.normal(ks[1], (3 * C, C), jnp.float32) * s_in, 'qkv_b': jnp.zeros((3 * C,), jnp.float32), 'kn_g': jnp.ones((hd,), jnp.float32), 'kn_b': jnp.zeros((hd,), jnp.float32), 'vn_g': jnp.ones((hd,), jnp.float32), 'vn_b': jnp.zeros((hd,), jnp.float32), 'temperature': jnp.ones((H, 1, 1), jnp.float32), 'attn_bias': jnp.zeros((H, hd, hd), jnp.float32), 'p1_w': jax.random.normal(ks[2], (C, C), jnp.float32) * s_in, 'p1_b': jnp.zeros((C,), jnp.float32), 'p2_w': jax.random.normal(ks[3], (C, C), jnp.float32) * s_in, 'p2_b': jnp.zeros((C,), jnp.float32)}
    _L1_attn_in = _L1_attn_setup()

    def _L1_ffn_setup():
        import jax, jax.numpy as jnp
        import numpy as np
        TOP_K = 2
        CAPACITY_FACTOR = 1.0
        key = jax.random.key(seed)
        ks = jax.random.split(key, 4)
        sl, bs, hs, ffn, E = (256, 8, 128, 512, 8)
        x = jax.random.normal(ks[0], (sl, bs, hs), dtype=jnp.float32)
        w_router = jax.random.normal(ks[1], (hs, E), dtype=jnp.float32) * 0.02
        w1 = jax.random.normal(ks[2], (E, hs, ffn), dtype=jnp.float32) * 0.02
        w2 = jax.random.normal(ks[3], (E, ffn, hs), dtype=jnp.float32) * 0.02
        bias = jnp.zeros((1, 1, hs), dtype=jnp.float32)
        return {'x': x, 'w_router': w_router, 'w1': w1, 'w2': w2, 'bias': bias}
    _L1_ffn_in = _L1_ffn_setup()
    _L1_c = _w((lambda *s: np.random.randn(*s).astype(np.float32) * 0.05)(16, 128))
    _L1_wmod = _w((lambda *s: np.random.randn(*s).astype(np.float32) * 0.05)(128, 6 * 128) * 128 ** (-0.5))
    _d = {'L0_attn_x': _L0_attn_in['x'], 'L0_attn_Wq': _L0_attn_in['Wq'], 'L0_attn_bq': _L0_attn_in['bq'], 'L0_attn_Wk': _L0_attn_in['Wk'], 'L0_attn_bk': _L0_attn_in['bk'], 'L0_attn_Wv': _L0_attn_in['Wv'], 'L0_attn_bv': _L0_attn_in['bv'], 'L0_attn_Wo': _L0_attn_in['Wo'], 'L0_attn_bo': _L0_attn_in['bo'], 'L0_attn_dp_w1': _L0_attn_in['dp_w1'], 'L0_attn_dp_b1': _L0_attn_in['dp_b1'], 'L0_attn_ln_g': _L0_attn_in['ln_g'], 'L0_attn_ln_b': _L0_attn_in['ln_b'], 'L0_attn_dp_w2': _L0_attn_in['dp_w2'], 'L0_attn_dp_b2': _L0_attn_in['dp_b2'], 'L0_attn_g_w1': _L0_attn_in['g_w1'], 'L0_attn_g_b1': _L0_attn_in['g_b1'], 'L0_attn_g_w2': _L0_attn_in['g_w2'], 'L0_attn_g_b2': _L0_attn_in['g_b2'], 'L0_ffn_Wq': _L0_ffn_in['Wq'], 'L0_ffn_bq': _L0_ffn_in['bq'], 'L0_ffn_Wk': _L0_ffn_in['Wk'], 'L0_ffn_bk': _L0_ffn_in['bk'], 'L0_ffn_Wv': _L0_ffn_in['Wv'], 'L0_ffn_bv': _L0_ffn_in['bv'], 'L0_ffn_Wo': _L0_ffn_in['Wo'], 'L0_ffn_bo': _L0_ffn_in['bo'], 'L0_ffn_Wg': _L0_ffn_in['Wg'], 'L0_ffn_bg': _L0_ffn_in['bg'], 'L0_ffn_W1': _L0_ffn_in['W1'], 'L0_ffn_b1': _L0_ffn_in['b1'], 'L0_ffn_W2': _L0_ffn_in['W2'], 'L0_ffn_b2': _L0_ffn_in['b2'], 'L0_c': _L0_c, 'L0_wmod': _L0_wmod, 'L1_attn_qkv_w': _L1_attn_in['qkv_w'], 'L1_attn_qkv_b': _L1_attn_in['qkv_b'], 'L1_attn_kn_g': _L1_attn_in['kn_g'], 'L1_attn_kn_b': _L1_attn_in['kn_b'], 'L1_attn_vn_g': _L1_attn_in['vn_g'], 'L1_attn_vn_b': _L1_attn_in['vn_b'], 'L1_attn_temperature': _L1_attn_in['temperature'], 'L1_attn_attn_bias': _L1_attn_in['attn_bias'], 'L1_attn_p1_w': _L1_attn_in['p1_w'], 'L1_attn_p1_b': _L1_attn_in['p1_b'], 'L1_attn_p2_w': _L1_attn_in['p2_w'], 'L1_attn_p2_b': _L1_attn_in['p2_b'], 'L1_ffn_w_router': _L1_ffn_in['w_router'], 'L1_ffn_w1': _L1_ffn_in['w1'], 'L1_ffn_w2': _L1_ffn_in['w2'], 'L1_ffn_bias': _L1_ffn_in['bias'], 'L1_c': _L1_c, 'L1_wmod': _L1_wmod}
    _x0 = _d['L0_attn_x']
    _d['L0_attn_x'] = jax.random.normal(jax.random.fold_in(jax.random.key(seed), 1), (16, 256, 128), dtype=_x0.dtype)
    del _x0
    return _d

def reference(L0_attn_x, L0_attn_Wq, L0_attn_bq, L0_attn_Wk, L0_attn_bk, L0_attn_Wv, L0_attn_bv, L0_attn_Wo, L0_attn_bo, L0_attn_dp_w1, L0_attn_dp_b1, L0_attn_ln_g, L0_attn_ln_b, L0_attn_dp_w2, L0_attn_dp_b2, L0_attn_g_w1, L0_attn_g_b1, L0_attn_g_w2, L0_attn_g_b2, L0_ffn_Wq, L0_ffn_bq, L0_ffn_Wk, L0_ffn_bk, L0_ffn_Wv, L0_ffn_bv, L0_ffn_Wo, L0_ffn_bo, L0_ffn_Wg, L0_ffn_bg, L0_ffn_W1, L0_ffn_b1, L0_ffn_W2, L0_ffn_b2, L0_c, L0_wmod, L1_attn_qkv_w, L1_attn_qkv_b, L1_attn_kn_g, L1_attn_kn_b, L1_attn_vn_g, L1_attn_vn_b, L1_attn_temperature, L1_attn_attn_bias, L1_attn_p1_w, L1_attn_p1_b, L1_attn_p2_w, L1_attn_p2_b, L1_ffn_w_router, L1_ffn_w1, L1_ffn_w2, L1_ffn_bias, L1_c, L1_wmod):

    def _L0_attn_ref(x, Wq, bq, Wk, bk, Wv, bv, Wo, bo, dp_w1, dp_b1, ln_g, ln_b, dp_w2, dp_b2, g_w1, g_b1, g_w2, g_b2):
        import jax, jax.numpy as jnp
        import numpy as np
        NUM_HEADS = 16
        LN_EPS = 1e-05

        def _gelu(x):
            return jax.nn.gelu(x, approximate=False)
        B, S, E = x.shape
        Hn = NUM_HEADS
        Dh = E // Hn
        scale = Dh ** (-0.5)
        Q = (x @ Wq + bq).reshape(B, S, Hn, Dh)
        K = (x @ Wk + bk).reshape(B, S, Hn, Dh)
        V = (x @ Wv + bv).reshape(B, S, Hn, Dh)
        logits = jnp.einsum('bqhd,bkhd->bhqk', Q, K) * scale
        causal = jnp.tril(jnp.ones((S, S), bool))
        logits = jnp.where(causal, logits, -jnp.inf)
        attn = jax.nn.softmax(logits, axis=-1)
        h = x @ dp_w1 + dp_b1
        mu = h.mean(-1, keepdims=True)
        var = ((h - mu) ** 2).mean(-1, keepdims=True)
        h = (h - mu) / jnp.sqrt(var + LN_EPS) * ln_g + ln_b
        drift = (_gelu(h) @ dp_w2 + dp_b2)[..., 0]
        g = _gelu(drift[..., None] * g_w1[0] + g_b1)
        gate = jnp.tanh(g @ g_w2 + g_b2)[..., 0]
        gated = attn * gate[:, None, None, :]
        out = jnp.einsum('bhqk,bkhd->bqhd', gated, V).reshape(B, S, E)
        return out @ Wo + bo

    def _L0_ffn_ref(x, Wq, bq, Wk, bk, Wv, bv, Wo, bo, Wg, bg, W1, b1, W2, b2):
        import jax, jax.numpy as jnp
        import numpy as np
        B, S, H, D, E = (4, 128, 128, 512, 8)
        q = x @ Wq + bq
        k = x @ Wk + bk
        v = x @ Wv + bv
        scale = jnp.asarray(1.0 / np.sqrt(H), x.dtype)
        scores = jnp.einsum('bqh,bkh->bqk', q, k) * scale
        attn = jax.nn.softmax(scores, axis=-1)
        a = jnp.einsum('bqk,bkh->bqh', attn, v) @ Wo + bo
        x = x + a
        gates = jax.nn.softmax(x @ Wg + bg, axis=-1)
        hmid = jax.nn.relu(jnp.einsum('bsh,ehd->bsed', x, W1) + b1)
        eout = jnp.einsum('bsed,edh->bseh', hmid, W2) + b2
        y = jnp.einsum('bse,bseh->bsh', gates, eout)
        return x + y

    def _L1_attn_ref(x, qkv_w, qkv_b, kn_g, kn_b, vn_g, vn_b, temperature, attn_bias, p1_w, p1_b, p2_w, p2_b):
        import jax, jax.numpy as jnp
        import numpy as np
        EPS = 1e-05

        def _layernorm(x, gamma, beta):
            m = jnp.mean(x, axis=-1, keepdims=True)
            v = jnp.mean(jnp.square(x - m), axis=-1, keepdims=True)
            return (x - m) * jax.lax.rsqrt(v + EPS) * gamma + beta
        B, Q, C = x.shape
        H = temperature.shape[0]
        hd = C // H
        qkv = (x @ qkv_w.T + qkv_b).reshape(B, Q, 3, H, hd)
        qkv = jnp.transpose(qkv, (2, 0, 3, 1, 4))
        q, k, v = (qkv[0], qkv[1], qkv[2])
        k = _layernorm(k, kn_g, kn_b)
        v = _layernorm(v, vn_g, vn_b)
        kv = jnp.einsum('bhqd,bhqe->bhde', k, v) / Q * temperature + attn_bias
        att = jnp.einsum('bhqd,bhde->bhqe', q, kv)
        att = jnp.transpose(att, (0, 2, 1, 3)).reshape(B, Q, C) + x
        h = jax.nn.gelu(att @ p1_w.T + p1_b, approximate=False)
        return h @ p2_w.T + p2_b + x

    def _L1_ffn_ref(x, w_router, w1, w2, bias):
        import jax, jax.numpy as jnp
        import numpy as np
        TOP_K = 2
        CAPACITY_FACTOR = 1.0
        sl, bs, hs = x.shape
        E = w_router.shape[1]
        xf = x.reshape(-1, hs)
        T = xf.shape[0]
        capacity = int(CAPACITY_FACTOR * TOP_K * T / E)
        scores = jax.nn.softmax(xf @ w_router, axis=-1)
        expert_weights, top_experts = jax.lax.top_k(scores, TOP_K)
        flat_e = top_experts.reshape(-1)
        flat_w = expert_weights.reshape(-1)
        N = flat_e.shape[0]
        order = jnp.argsort(flat_e, stable=True)
        bin_ids = flat_e[order]
        tpe = jnp.zeros((E,), jnp.int32).at[flat_e].add(1)
        starts = jnp.cumsum(tpe) - tpe
        offsets = jnp.arange(N) - starts[bin_ids]
        valid = offsets < capacity
        slot = jnp.where(valid, bin_ids * capacity + offsets, E * capacity)
        src = order // TOP_K
        xb = jnp.zeros((E * capacity + 1, hs), x.dtype).at[slot].set(xf[src])
        xb = xb[:-1].reshape(E, capacity, hs)
        h = jax.nn.gelu(jnp.einsum('ech,ehf->ecf', xb, w1))
        y = jnp.einsum('ecf,efh->ech', h, w2).reshape(E * capacity, hs)
        yv = jnp.where(valid[:, None], y[jnp.minimum(slot, E * capacity - 1)], 0.0)
        out = jnp.zeros((T, hs), x.dtype).at[src].add(flat_w[order][:, None] * yv)
        return out.reshape(sl, bs, hs) + bias
    x = L0_attn_x
    mod = (_silu(L0_c) @ L0_wmod).reshape(L0_c.shape[0], 6, 1, -1)
    sa, ca, ga, sb, cb, gb = (mod[:, 0], mod[:, 1], mod[:, 2], mod[:, 3], mod[:, 4], mod[:, 5])
    ga = (2 * (ga >= 0) - 1) * jnp.maximum(jnp.abs(ga), 0.25)
    gb = (2 * (gb >= 0) - 1) * jnp.maximum(jnp.abs(gb), 0.25)
    h = _layernorm(x, axis=-1) * (1 + ca) + sa
    x = x + ga * _L0_attn_ref(h, L0_attn_Wq, L0_attn_bq, L0_attn_Wk, L0_attn_bk, L0_attn_Wv, L0_attn_bv, L0_attn_Wo, L0_attn_bo, L0_attn_dp_w1, L0_attn_dp_b1, L0_attn_ln_g, L0_attn_ln_b, L0_attn_dp_w2, L0_attn_dp_b2, L0_attn_g_w1, L0_attn_g_b1, L0_attn_g_w2, L0_attn_g_b2)
    h = _layernorm(x, axis=-1) * (1 + cb) + sb
    x = x + gb * _L0_ffn_ref(h, L0_ffn_Wq, L0_ffn_bq, L0_ffn_Wk, L0_ffn_bk, L0_ffn_Wv, L0_ffn_bv, L0_ffn_Wo, L0_ffn_bo, L0_ffn_Wg, L0_ffn_bg, L0_ffn_W1, L0_ffn_b1, L0_ffn_W2, L0_ffn_b2)
    mod = (_silu(L1_c) @ L1_wmod).reshape(L1_c.shape[0], 6, 1, -1)
    sa, ca, ga, sb, cb, gb = (mod[:, 0], mod[:, 1], mod[:, 2], mod[:, 3], mod[:, 4], mod[:, 5])
    ga = (2 * (ga >= 0) - 1) * jnp.maximum(jnp.abs(ga), 0.25)
    gb = (2 * (gb >= 0) - 1) * jnp.maximum(jnp.abs(gb), 0.25)
    h = _layernorm(x, axis=-1) * (1 + ca) + sa
    x = x + ga * _L1_attn_ref(h, L1_attn_qkv_w, L1_attn_qkv_b, L1_attn_kn_g, L1_attn_kn_b, L1_attn_vn_g, L1_attn_vn_b, L1_attn_temperature, L1_attn_attn_bias, L1_attn_p1_w, L1_attn_p1_b, L1_attn_p2_w, L1_attn_p2_b)
    h = _layernorm(x, axis=-1) * (1 + cb) + sb
    x = x + gb * _L1_ffn_ref(h, L1_ffn_w_router, L1_ffn_w1, L1_ffn_w2, L1_ffn_bias)
    return x

_drawn_inputs = setup_inputs


def setup_inputs(seed=0):
    import zlib

    import numpy as np

    out = dict(_drawn_inputs(seed))
    spreads = {'L0_attn_bq': (0.0, 0.8),
     'L0_attn_bk': (0.0, 2.0),
     'L0_attn_bv': (0.0, 0.8),
     'L0_attn_bo': (0.0, 1.701),
     'L0_attn_dp_b1': (0.0, 0.8),
     'L0_attn_ln_g': (1.0, 0.6),
     'L0_attn_ln_b': (0.0, 0.8),
     'L0_attn_g_b1': (0.0, 0.8),
     'L0_ffn_bq': (0.0, 2.0),
     'L0_ffn_bk': (0.0, 2.0),
     'L0_ffn_bv': (0.0, 1.59),
     'L0_ffn_bo': (0.0, 1.607),
     'L0_ffn_bg': (0.0, 2.0),
     'L0_ffn_b1': (0.0, 2.0),
     'L0_ffn_b2': (0.0, 2.0),
     'L1_attn_qkv_b': (0.0, 0.69),
     'L1_attn_kn_g': (1.0, 0.6),
     'L1_attn_kn_b': (0.0, 0.8),
     'L1_attn_vn_g': (1.0, 0.6),
     'L1_attn_vn_b': (0.0, 0.8),
     'L1_attn_temperature': (1.0, 0.6),
     'L1_attn_attn_bias': (0.0, 0.745),
     'L1_attn_p1_b': (0.0, 2.0),
     'L1_attn_p2_b': (0.0, 1.569),
     'L1_ffn_bias': (0.0, 2.0)}
    factors = {'L0_attn_Wq': 7.675,
     'L0_attn_Wk': 7.538,
     'L0_attn_Wv': 5.129,
     'L0_attn_Wo': 4.979,
     'L0_attn_dp_w1': 5.608,
     'L0_attn_dp_w2': 5.517,
     'L0_attn_g_w1': 6.718,
     'L0_attn_g_w2': 4.005,
     'L1_ffn_w_router': 8.0,
     'L1_ffn_w1': 8.0,
     'L1_ffn_w2': 8.0,
     'L0_ffn_Wq': 6.944,
     'L0_ffn_Wk': 5.903,
     'L0_ffn_Wv': 4.387,
     'L0_ffn_Wo': 2.879,
     'L0_ffn_Wg': 2.772,
     'L0_ffn_W1': 3.481}
    for name, (base, spread) in spreads.items():
        noise = np.random.default_rng([zlib.crc32(name.encode()), seed]).standard_normal(out[name].shape)
        drawn = base * np.exp(spread * noise) if base else spread * noise
        out[name] = jnp.asarray(drawn.astype(out[name].dtype))
    for name, factor in factors.items():
        out[name] = (out[name] * factor).astype(out[name].dtype)
    return out
```

```python
from contextlib import ExitStack

import numpy as np
import concourse.bass as bass
from concourse import mybir

F32 = mybir.dt.float32
F32R = mybir.dt.float32r
BF16 = mybir.dt.bfloat16
I32 = mybir.dt.int32
ALU = mybir.AluOpType
ACT = mybir.ActivationFunctionType
X_AXIS = mybir.AxisListType.X

B, S, C = 16, 256, 128
P = 128
TOK = B * S
NT = TOK // P
TPB = S // P
HEADS, HD = 16, 8
HID = 64
GW = 16
NE, FF = 8, 512
FC = FF // P
CHUNK = 512
NCH = TOK // CHUNK
CT = CHUNK // P
TOPK = 2
CAP = TOPK * TOK // NE
SLOTS = NE * CAP
EPS = 1e-5
MASKED = -1e30
ROW = C + 2
MOD = 6


class Step:

    def __init__(self, engine, emit, after):
        self.engine, self.emit, self.after, self.signals, self.value = engine, emit, after, False, None


class Landed:

    def __init__(self, stream, value):
        self.stream, self.value = stream, value


class Stream:

    def __init__(self, sem):
        self.sem, self.count = sem, 0


class Queues:

    def __init__(self, nc, new_sem):
        self.nc = nc
        self.lists = {n: [] for n in ("tensor", "vector", "scalar", "gpsimd", "sync")}
        self.sems = {n: new_sem(f"done_{n}") for n in ("tensor", "vector", "scalar", "gpsimd")}

    def step(self, engine, emit, after=()):
        s = Step(engine, emit, list(after))
        for a in s.after:
            if isinstance(a, Step):
                a.signals = True
        self.lists[engine].append(s)
        return s

    def dma(self, engine, stream, emit, after=()):
        s = self.step(engine, emit, after)
        s.stream = stream
        stream.count += 16
        return Landed(stream, stream.count)

    def number(self):
        for name, steps in self.lists.items():
            n = 0
            for s in steps:
                if s.signals:
                    n += 1
                    s.value = n

    def play(self, name, eng):
        seen = {}
        for s in self.lists[name]:
            need = {}
            for a in s.after:
                if isinstance(a, Step):
                    sem, value = self.sems[a.engine], a.value
                else:
                    sem, value = a.stream.sem, a.value
                key = id(sem)
                if value > seen.get(key, 0) and value > need.get(key, (None, 0))[1]:
                    need[key] = (sem, value)
            for key, (sem, value) in need.items():
                eng.wait_ge(sem, value)
                seen[key] = value
            inst = s.emit(eng)
            if hasattr(s, "stream"):
                inst.then_inc(s.stream.sem, 16)
            elif s.signals:
                inst.then_inc(self.sems[name], 1)


class Ring:

    def __init__(self, n):
        self.n, self.i, self.left = n, -1, [[] for _ in range(n)]

    def take(self):
        self.i = (self.i + 1) % self.n
        return self.i, self.left[self.i]

    def leave(self, i, steps):
        self.left[i] = list(steps)


def build(nc, a, out):
    ctx = ExitStack()
    with ctx:
        def sb(name, shape, dt=F32):
            return ctx.enter_context(nc.sbuf_tensor(name, shape, dt))

        def new_sem(name):
            return ctx.enter_context(nc.semaphore(name))

        q = Queues(nc, new_sem)

        def pe(emit, after=()):
            return q.step("tensor", emit, after)

        def dve(emit, after=()):
            return q.step("vector", emit, after)

        def act(emit, after=()):
            return q.step("scalar", emit, after)

        def pool(emit, after=()):
            return q.step("gpsimd", emit, after)

        def mm(o, l, r, start=True, stop=True, after=(), skip=False):
            return pe(lambda e: e.matmul(o, l, r, start=start, stop=stop, skip_group_check=skip), after)

        def stream(name):
            return Stream(new_sem(name))

        def load(st, dst, src, after=(), engine="sync"):
            return q.dma(engine, st, lambda e: e.dma_start(dst, src), after)

        x = sb("x", [P, NT, C])
        hT = sb("hT", [P, TOK])
        hT3 = hT[:, :].rearrange("p (t c) -> p t c", c=C)
        big1 = sb("big1", [P, NT * (C + HID)])
        big2 = sb("big2", [P, NT * HEADS * (HD + 1)])
        tmp = sb("tmp", [P, 8, CHUNK])
        gb_tok = sb("gb_tok", [P, B, C])
        ew1 = sb("ew1", [P, NE, FF])
        ew2 = sb("ew2", [P, NE, FC, C])
        QR = 4
        q_stack = [sb(f"q_stack{i}", [P, 4, S], F32R) for i in range(QR)]
        k_stack = [sb(f"k_stack{i}", [P, 4, S], F32R) for i in range(QR)]
        parts = [sb(f"parts{i}", [P, CHUNK], F32R) for i in range(4)]
        ident = sb("ident", [P, P])
        ident_b = sb("ident_b", [P, P], BF16)
        mask_qk = sb("mask_qk", [P, 4, P], BF16)
        mask_kq = sb("mask_kq", [P, 4, P], BF16)
        before = sb("before", [P, P], BF16)
        ones_b = sb("ones_b", [P, P], BF16)
        const = big2[:, 0:CHUNK]
        psum = ctx.enter_context(nc.psum_tensor("psum", [P, 8, CHUNK], F32))

        def bank(i, n=CHUNK):
            return psum[:, i, 0:n]

        psum_ring = Ring(8)
        tmp_ring = Ring(8)

        q_parts = nc.dram_tensor("q_parts", [P, 4, TOK], F32, kind="Internal").ap()
        k_parts = nc.dram_tensor("k_parts", [P, 4, TOK], F32, kind="Internal").ap()
        routed = nc.dram_tensor("routed", [SLOTS, ROW], F32, kind="Internal").ap()
        answers = nc.dram_tensor("answers", [TOPK * TOK, C], F32, kind="Internal").ap()

        s_mod, s_w, s_col, s_rowp, s_ew = (stream(n) for n in ("mod", "weights", "cols", "rows", "experts"))
        s_x = [stream(f"x{i}") for i in range(4)]
        wmod = big1[:, 0:2 * MOD * C].rearrange("p (l n) -> p l n", l=2)
        for l in range(2):
            mod_in = load(s_mod, wmod[:, l, :], a[f"L{l}_wmod"])
        xd = a["L0_attn_x"].rearrange("b (t p) c -> p (b t) c", p=P)
        x_in = [load(s_x[i], x[:, 8 * i:8 * i + 8, :], xd[:, 8 * i:8 * i + 8, :]) for i in range(4)]

        wqk = sb("wqk", [P, 2, C])
        wvd = sb("wvd", [P, C + HID])
        wo = sb("wo", [P, C])
        fw = sb("fw", [P, 4, C])
        wg = sb("wg", [P, NE])
        w_raw = sb("w_raw", [P, 5, C])
        w_t = sb("w_t", [P, 5, C])
        wr = sb("wr", [P, NE])
        load(s_w, wqk[:, 0, :], a["L0_attn_Wq"])
        load(s_w, wqk[:, 1, :], a["L0_attn_Wk"])
        load(s_w, wvd[:, 0:C], a["L0_attn_Wv"])
        load(s_w, wvd[:, C:C + HID], a["L0_attn_dp_w1"])
        load(s_w, wo[:, :], a["L0_attn_Wo"])
        for i, n in enumerate("qkvo"):
            load(s_w, fw[:, i, :], a[f"L0_ffn_W{n}"])
        load(s_w, wg[:, :], a["L0_ffn_Wg"])
        load(s_w, w_raw[:, 0:3, :], a["L1_attn_qkv_w"].rearrange("(g p) c -> p g c", p=P))
        load(s_w, w_raw[:, 3, :], a["L1_attn_p1_w"])
        load(s_w, w_raw[:, 4, :], a["L1_attn_p2_w"])
        w_in = load(s_w, wr[:, :], a["L1_ffn_w_router"])

        COLS = {}
        n_cols = 0
        for name, n in (("L0_c", B), ("L1_c", B),
                        ("L0_attn_bq", 1), ("L0_attn_bk", 1), ("L0_attn_bo", 1), ("L0_ffn_bq", 1),
                        ("L0_ffn_bk", 1), ("L0_ffn_bo", 1), ("L1_attn_p1_b", 1), ("L1_attn_p2_b", 1),
                        ("L1_attn_qkv_b", 3), ("L0_ffn_b1", NE * FC)):
            COLS[name] = n_cols
            n_cols += n
        cols = sb("cols", [P, n_cols])
        col_rows = sb("col_rows", [n_cols, P])
        for name, at in COLS.items():
            v = a[name]
            if len(v.shape) == 2:
                v = v.rearrange("e f -> (e f)")
            n = v.shape[0] // P
            cols_loaded = load(s_col, col_rows[at:at + n, :], v.rearrange("(n p) -> n p", p=P))

        def col(name, i=0):
            return cols[:, COLS[name] + i:COLS[name] + i + 1]

        ROWS = {}
        n_rows = 0
        for name, n in (("L0_attn_bv", C), ("L0_attn_dp_b1", HID), ("L0_attn_ln_g", HID), ("L0_attn_ln_b", HID),
                        ("L0_attn_dp_w2", HID), ("L0_attn_dp_b2", 1), ("L0_attn_g_w1", GW), ("L0_attn_g_b1", GW),
                        ("L0_attn_g_w2", GW), ("L0_attn_g_b2", 1), ("L0_ffn_bv", C), ("L0_ffn_bg", NE),
                        ("L1_attn_qkv_b", 3 * C), ("L1_attn_kn_g", HD), ("L1_attn_vn_g", HD),
                        ("L1_attn_kn_b", HD), ("L1_attn_vn_b", HD), ("L1_ffn_bias", C)):
            ROWS[name] = (n_rows, n)
            n_rows += n
        rows = sb("rows", [P, n_rows])
        for name, (at, n) in ROWS.items():
            v = a[name]
            if len(v.shape) == 2:
                v = v.rearrange("a b -> (a b)")
            if len(v.shape) == 3:
                v = v.rearrange("a b c -> (a b c)")
            rows_in = load(s_rowp, rows[:, at:at + n], v.unsqueeze(0).to_broadcast([P, n]))

        def row(name):
            at, n = ROWS[name]
            return rows[:, at:at + n]

        b2 = sb("b2", [NE, C])
        load(s_ew, b2[:, :], a["L0_ffn_b2"])
        load(s_ew, ew1[:, :, :], a["L0_ffn_W1"].rearrange("e p f -> p e f"))
        ew_in = load(s_ew, ew2[:, :, :, :], a["L0_ffn_W2"].rearrange("e (k p) c -> p e k c", p=P))

        def select(t, pattern, mult, base, fill, cmp, after):
            return pool(lambda e: e.affine_select(out=t, in_=t, pattern=pattern, compare_op=cmp, fill=fill,
                                                  base=base, channel_multiplier=mult), after)

        z1 = pool(lambda e: e.memset(ident[:, :], 0.0))
        identity = select(ident[:, :], [[-1, P]], 1, 0, 1.0, ALU.not_equal, [z1])
        z2 = pool(lambda e: e.memset(ident_b[:, :], 0.0))
        identity_b = select(ident_b[:, :], [[-1, P]], 1, 0, 1.0, ALU.not_equal, [z2])
        z3 = pool(lambda e: e.memset(mask_qk[:, :, :], 0.0))
        select(mask_qk[:, :, :], [[0, 4], [-1, P]], 1, 0, MASKED, ALU.is_ge, [z3])
        z4 = pool(lambda e: e.memset(mask_kq[:, :, :], 0.0))
        masks = select(mask_kq[:, :, :], [[0, 4], [1, P]], -1, 0, MASKED, ALU.is_ge, [z4])
        z5 = pool(lambda e: e.memset(before[:, :], 1.0))
        select(before[:, :], [[1, P]], -1, -1, 0.0, ALU.is_ge, [z5])
        counters = pool(lambda e: e.memset(ones_b[:, :], 1.0))

        col_free = psum_ring.take()[1]
        turned = pe(lambda e: e.transpose(psum[:, 0, 0:n_cols], col_rows[:, :],
                                          ident[0:n_cols, 0:n_cols]), [cols_loaded, identity] + col_free)
        cols_in = dve(lambda e: e.tensor_copy(cols[:, :], psum[:, 0, 0:n_cols]), [turned])
        psum_ring.leave(0, [cols_in])
        cT = cols[:, 0:2 * B].rearrange("p (l b) -> p l b", l=2)

        zero512 = pool(lambda e: e.memset(const, 0.0))
        s_fill = stream("fill")
        for n in range(NCH):
            q_fill = load(s_fill, q_parts[:, 3, n * CHUNK:(n + 1) * CHUNK], const, [zero512])
        answers_v = answers.rearrange("(n p) c -> p n c", p=P)
        for n in range(TOPK * TOK // P // CT):
            answers_zero = load(s_fill, answers_v[:, n * CT:(n + 1) * CT, :],
                                const.rearrange("p (n c) -> p n c", c=C), [zero512])
        neg_rows = big2[:, CHUNK:2 * CHUNK]
        n1 = pool(lambda e: e.memset(neg_rows, 0.0))
        for i in range(P // HD):
            n1 = select(neg_rows, [[0, CHUNK]], 1, -HD * i, -1.0, ALU.not_equal, [n1])
        for n in range(NCH):
            k_fill = load(s_fill, k_parts[:, 3, n * CHUNK:(n + 1) * CHUNK], neg_rows, [n1])
        empty_row = sb("empty_row", [P, ROW])
        e1 = pool(lambda e: e.memset(empty_row[:, :], 0.0))
        e2 = pool(lambda e: e.memset(empty_row[:, C:C + 1], float(TOPK * TOK)), [e1])
        for n in range(SLOTS // P):
            routed_empty = load(s_fill, routed[n * P:(n + 1) * P, :], empty_row[:, :], [e2])

        sil = sb("sil", [P, 2, B])
        silu = act(lambda e: e.activation(sil[:, :, :], cT, ACT.Silu), [cols_in])
        modT = sb("modT", [P, 2, MOD, B])
        mod_ready = []
        for l in range(2):
            i, free = psum_ring.take()
            for g in range(MOD):
                last = mm(psum[:, i, g * B:(g + 1) * B], wmod[:, l, g * C:(g + 1) * C], sil[:, l, :],
                          after=[silu, mod_in] + free)
            src = psum[:, i, 0:MOD * B].rearrange("p (g b) -> p g b", b=B)
            cp = dve(lambda e, l=l, s=src: e.tensor_copy(modT[:, l, :, :], s), [last])
            psum_ring.leave(i, [cp])
            for g in (1, 4):
                m = modT[:, l, g, :]
                last = dve(lambda e, m=m: e.tensor_scalar(m, m, 1.0, None, ALU.add), [cp])
            mod_ready.append(last)
            for g in (2, 5):
                m = modT[:, l, g, :]
                sgn = sb(f"sgn{l}{g}", [P, B])
                mag = sb(f"mag{l}{g}", [P, B])
                s1 = dve(lambda e, m=m, t=sgn: e.tensor_scalar(t[:, :], m, 0.0, 2.0, ALU.is_ge, ALU.mult), [cp])
                s2 = dve(lambda e, m=m, t=mag: e.scalar_tensor_tensor(t[:, :], m, -1.0, m, ALU.mult, ALU.max), [cp])
                s2 = dve(lambda e, t=mag: e.tensor_scalar(t[:, :], t[:, :], 0.25, None, ALU.max), [s2])
                last = dve(lambda e, m=m, s=sgn, t=mag: e.scalar_tensor_tensor(
                    m, s[:, :], -1.0, t[:, :], ALU.add, ALU.mult), [s1, s2])
            mod_ready.append(last)
        def spread_gates(l, gb_free):
            for n in range(B // 4):
                i, free = psum_ring.take()
                for k in range(4):
                    b = 4 * n + k
                    t, tfree = tmp_ring.take()
                    rep = dve(lambda e, t=t, b=b: e.tensor_copy(
                        tmp[:, t, 0:P], modT[:, l, 5, b:b + 1].to_broadcast([P, P])), mod_ready + tfree)
                    last = mm(psum[:, i, k * C:(k + 1) * C], tmp[:, t, 0:P], ident[:, :],
                              after=[rep, identity] + free)
                    tmp_ring.leave(t, [last])
                cp = act(lambda e, i=i, n=n: e.copy(
                    gb_tok[:, 4 * n:4 * n + 4, :].rearrange("p b c -> p (b c)"), bank(i)), [last] + gb_free)
                psum_ring.leave(i, [cp])
            return cp

        stats = sb("stats", [P, NT, 6])
        mv = sb("mv", [P, NT, 2])
        rstd = sb("rstd", [P, NT])

        LG = 8
        ln_tmp = sb("ln_tmp", [P, NT])

        def rsqrt(y, v, t, ready, engine=dve):
            s1 = dve(lambda e: e.tensor_scalar(t.bitcast(I32), v.bitcast(I32), 1, None, ALU.arith_shift_right),
                     ready)
            s2 = dve(lambda e: e.tensor_scalar(y.bitcast(I32), t.bitcast(I32), -1.0, float(0x5F3759DF),
                                               ALU.mult, ALU.add), [s1])
            for _ in range(3):
                s1 = engine(lambda e: e.tensor_tensor(t, y, y, ALU.mult), [s2])
                s1 = engine(lambda e: e.tensor_tensor(t, t, v, ALU.mult), [s1])
                s1 = engine(lambda e: e.tensor_scalar(t, t, -0.5, 1.5, ALU.mult, ALU.add), [s1])
                s2 = engine(lambda e: e.tensor_tensor(y, y, t, ALU.mult), [s1])
            return s2

        rstd_ready = {}

        def normalise(b, l, second, x_ready):
            t0 = TPB * b
            if t0 % LG == 0:
                for t in range(t0, t0 + LG):
                    st = dve(lambda e, t=t: e.bn_stats(stats[:, t, :], x[:, t, :]), x_ready(t // TPB))
                    ag = dve(lambda e, t=t: e.bn_aggr(mv[:, t, :], stats[:, t, :]), [st])
                v = mv[:, t0:t0 + LG, 1]
                ev = dve(lambda e: e.tensor_scalar(v, v, EPS, None, ALU.add), [ag])
                rstd_ready[t0 // LG] = rsqrt(rstd[:, t0:t0 + LG], v, ln_tmp[:, t0:t0 + LG], [ev])
            rs = rstd_ready[t0 // LG]
            i, free = psum_ring.take()
            k, tfree = tmp_ring.take()
            for n in range(TPB):
                t = t0 + n
                z = tmp[:, k, n * C:(n + 1) * C]
                zs = dve(lambda e, z=z, t=t: e.tensor_scalar(z, x[:, t, :], mv[:, t, 0:1], rstd[:, t:t + 1],
                                                             ALU.subtract, ALU.mult), [rs] + tfree)
                tr = pe(lambda e, z=z, n=n, i=i: e.transpose(psum[:, i, n * P:(n + 1) * P], z, ident[:, :]),
                        [zs, identity] + free)
            tmp_ring.leave(k, [tr])
            g = 3 if second else 0
            w = act(lambda e: e.activation(hT[:, b * S:(b + 1) * S], psum[:, i, 0:S], ACT.Identity,
                                           bias=modT[:, l, g, b:b + 1], scale=modT[:, l, g + 1, b:b + 1]),
                    [tr] + mod_ready)
            psum_ring.leave(i, [w])
            return w

        hready = {}
        for b in range(B):
            hready[b] = normalise(b, 0, False, lambda b: [x_in[b // 4]])

        VW = C + HID
        vd = big1[:, :].rearrange("p (t n) -> p t n", n=VW)
        vd_in = {}
        bias_vd = rows[:, ROWS["L0_attn_bv"][0]:ROWS["L0_attn_bv"][0] + VW]
        for b in range(B):
            i, free = psum_ring.take()
            for n in range(TPB):
                t = TPB * b + n
                last = mm(psum[:, i, n * VW:(n + 1) * VW], hT[:, t * P:(t + 1) * P], wvd[:, :],
                          after=[hready[b], w_in] + free)
            src = psum[:, i, 0:TPB * VW].rearrange("p (t n) -> p t n", n=VW)
            vd_in[b] = dve(lambda e, s=src, b=b: e.tensor_tensor(
                vd[:, TPB * b:TPB * (b + 1), :], s, bias_vd.unsqueeze(1).to_broadcast([P, TPB, VW]), ALU.add),
                [last, rows_in])
            psum_ring.leave(i, [vd_in[b]])

        s_part = [stream(f"part{i}") for i in range(4)]
        part_sent = [[] for _ in range(4)]
        qk_stored = {}
        for n in range(NCH):
            cs = slice(n * CHUNK, (n + 1) * CHUNK)
            for w, name, dst in ((0, "L0_attn_bq", q_parts), (1, "L0_attn_bk", k_parts)):
                i, free = psum_ring.take()
                last = mm(bank(i), wqk[:, w, :], hT[:, cs], after=[hready[2 * n + 1], w_in] + free)
                k, tfree = tmp_ring.take()
                full = act(lambda e, k=k, i=i, name=name: e.activation(
                    tmp[:, k, :], bank(i), ACT.Identity, bias=col(name)), [last, cols_in] + tfree)
                psum_ring.leave(i, [full])
                hi, lo = parts[2 * w], parts[2 * w + 1]
                h = pool(lambda e, hi=hi, k=k: e.tensor_copy(hi[:, :], tmp[:, k, :]), [full] + part_sent[2 * w])
                l = dve(lambda e, lo=lo, hi=hi, k=k: e.tensor_tensor(
                    lo[:, :], tmp[:, k, :], hi[:, :].bitcast(F32), ALU.subtract), [full, h] + part_sent[2 * w + 1])
                tmp_ring.leave(k, [l])
                hi_at, lo_at = ((0, 2), 1) if w == 0 else ((0, 1), 2)
                for p in hi_at:
                    d = load(s_part[2 * w], dst[:, p, cs], hi[:, :].bitcast(F32), [h])
                part_sent[2 * w] = [d, l]
                d2 = load(s_part[2 * w + 1], dst[:, lo_at, cs], lo[:, :].bitcast(F32), [l])
                part_sent[2 * w + 1] = [d2]
                qk_stored[(n, w)] = [d, d2]

        va = big2[:, :].rearrange("p (t h d) -> p t h d", h=HEADS, d=HD + 1)
        gate = sb("gate", [P, NT])
        drift = sb("drift", [P, NT])
        dst_ = sb("dstats", [P, NT, 6])
        dmv = sb("dmv", [P, NT, 2])
        drs = sb("drs", [P, NT])
        for t in range(NT):
            st = dve(lambda e, t=t: e.bn_stats(dst_[:, t, :], vd[:, t, C:VW]), [vd_in[t // TPB]])
            ag = dve(lambda e, t=t: e.bn_aggr(dmv[:, t, :], dst_[:, t, :]), [st])
        ev = dve(lambda e: e.tensor_scalar(dmv[:, :, 1], dmv[:, :, 1], EPS, None, ALU.add), [ag])
        rs = rsqrt(drs[:, :], dmv[:, :, 1], ln_tmp[:, :], [ev])
        GT = CHUNK // HID
        gated = {}
        for n in range(NT // GT):
            ts = slice(n * GT, (n + 1) * GT)
            k, tfree = tmp_ring.take()
            t3 = tmp[:, k, :].rearrange("p (t n) -> p t n", n=HID)
            for m in range(GT):
                t = n * GT + m
                last = dve(lambda e, t=t, m=m, t3=t3: e.tensor_scalar(
                    t3[:, m, :], vd[:, t, C:VW], dmv[:, t, 0:1], drs[:, t:t + 1], ALU.subtract, ALU.mult),
                    [rs] + tfree)

            def rep(name, w=HID):
                return row(name).unsqueeze(1).to_broadcast([P, GT, w])

            s1 = pool(lambda e, t3=t3, r=rep("L0_attn_ln_g"): e.tensor_tensor(t3, t3, r, ALU.mult), [last])
            s2 = pool(lambda e, t3=t3, r=rep("L0_attn_ln_b"): e.tensor_tensor(t3, t3, r, ALU.add), [s1])
            s3 = act(lambda e, t3=t3: e.activation(t3, t3, ACT.Gelu), [s2])
            s4 = pool(lambda e, t3=t3, r=rep("L0_attn_dp_w2"): e.tensor_tensor(t3, t3, r, ALU.mult), [s3])
            s5 = dve(lambda e, t3=t3, ts=ts: e.tensor_reduce(drift[:, ts], t3, X_AXIS, ALU.add), [s4])
            s6 = dve(lambda e, ts=ts: e.tensor_scalar(drift[:, ts], drift[:, ts], row("L0_attn_dp_b2"), None,
                                                      ALU.add), [s5])
            g3 = tmp[:, k, 0:GT * GW].rearrange("p (t n) -> p t n", n=GW)
            s7 = dve(lambda e, g3=g3, ts=ts, r=rep("L0_attn_g_w1", GW): e.tensor_tensor(
                g3, drift[:, ts].unsqueeze(2).to_broadcast([P, GT, GW]), r, ALU.mult), [s6])
            s8 = dve(lambda e, g3=g3, r=rep("L0_attn_g_b1", GW): e.tensor_tensor(g3, g3, r, ALU.add), [s7])
            s9 = act(lambda e, g3=g3: e.activation(g3, g3, ACT.Gelu), [s8])
            s10 = dve(lambda e, g3=g3, r=rep("L0_attn_g_w2", GW): e.tensor_tensor(g3, g3, r, ALU.mult), [s9])
            s11 = dve(lambda e, g3=g3, ts=ts: e.tensor_reduce(gate[:, ts], g3, X_AXIS, ALU.add), [s10])
            tmp_ring.leave(k, [s11])
            s12 = act(lambda e, ts=ts: e.activation(gate[:, ts], gate[:, ts], ACT.Tanh,
                                                    bias=row("L0_attn_g_b2")), [s11])
            for m in range(GT):
                t = n * GT + m
                o = pool(lambda e, t=t: e.memset(va[:, t, :, HD:HD + 1], 1.0), [q_fill, k_fill, answers_zero])
                v = pool(lambda e, t=t: e.tensor_scalar(
                    va[:, t, :, 0:HD], vd[:, t, 0:C].rearrange("p (h d) -> p h d", d=HD), gate[:, t:t + 1], None,
                    ALU.mult), [s12, o])
                gated[t] = v

        s_qs = [stream(f"qs{i}") for i in range(QR)]
        s_ks = [stream(f"ks{i}") for i in range(QR)]
        s_m = [stream(f"maxrow{i}") for i in range(QR)]
        stacked, stack_free = {}, [[] for _ in range(QR)]
        mrow_ready = {}
        q_src = q_parts.rearrange("(i r) a t -> (r a) i t", i=4)
        k_src = k_parts.rearrange("(i r) a t -> (r a) i t", i=4)

        def stack(b):
            r = b % QR
            ts = slice(b * S, (b + 1) * S)
            n = b * S // CHUNK
            dq = load(s_qs[r], q_stack[r][:, :, :].bitcast(F32), q_src[:, :, ts],
                      qk_stored[(n, 0)] + [q_fill, k_fill] + stack_free[r])
            dk = load(s_ks[r], k_stack[r][:, :, :].bitcast(F32), k_src[:, :, ts], qk_stored[(n, 1)] + [k_fill])
            stacked[b] = [dq, dk]

        pair = Ring(3)
        for i in range(3):
            pair.leave(i, psum_ring.left[2 * i] + psum_ring.left[2 * i + 1])
        o_free = psum_ring.left[6]
        m_free = psum_ring.left[7]
        p_ring = Ring(4)
        for i in range(4):
            p_ring.leave(i, tmp_ring.left[2 * i] + tmp_ring.left[2 * i + 1])
        maxes = sb("maxes", [P, 2, TPB, 4, 4])
        m_hi = sb("m_hi", [HEADS, 2, S], F32R)
        max_in = {}

        def max_unit(b, u):
            r = b % QR
            s, free = pair.take()
            qb, jp = (0, u) if u < 2 else (1, (u - 2) % 2)
            width = P * (qb + 1)
            ii = range(4) if qb == 0 else range(2 * ((u - 2) // 2), 2 * ((u - 2) // 2) + 2)
            last = None
            for jl in range(2):
                out_m = bank(2 * s + jl).rearrange("p (g k) -> p g k", k=width)[:, :, width - P:width]
                mm(out_m, ident_b[:, :], mask_qk[:, 0:len(ii), :], start=True, stop=False,
                   after=[masks, identity_b] + free + stacked[b], skip=True)
            for n, i in enumerate(ii):
                for jl in range(2):
                    j = 2 * jp + jl
                    rows_ = slice(32 * j, 32 * j + 32)
                    last = mm(psum[:, 2 * s + jl, n * width:(n + 1) * width],
                              q_stack[r][rows_, i, qb * P:(qb + 1) * P], k_stack[r][rows_, i, 0:width],
                              start=False, stop=True, skip=True)
            src = psum[:, 2 * s:2 * s + 2, :].rearrange("p j (g k) -> p j g k", k=width)
            dst = maxes[:, b % 2, qb, ii[0]:ii[-1] + 1, 2 * jp:2 * jp + 2].rearrange("p i j -> p j i")
            red = dve(lambda e: e.tensor_reduce(dst, src, X_AXIS, ALU.max), [last])
            pair.leave(s, [red])
            max_in.setdefault(b, []).append(red)

        def max_rows(b):
            nonlocal m_free
            r = b % QR
            for qb in range(TPB):
                src = maxes[:, b % 2, qb, :, :].rearrange("p i j -> p (i j)")
                tr = pe(lambda e, src=src, qb=qb: e.transpose(
                    psum[0:HEADS, 7, qb * P:(qb + 1) * P], src, ident[:, :]), [max_in[b][-1]] + m_free)
            wait = mrow_ready.get(b - 2, [])
            cp = dve(lambda e: e.tensor_copy(m_hi[:, b % 2, :], psum[0:HEADS, 7, 0:S]), [tr] + wait)
            m_free = [cp]
            for i in range(4):
                d = load(s_m[r], q_stack[r][3:P:32, i, :].bitcast(F32), m_hi[4 * i:4 * i + 4, b % 2, :].bitcast(F32),
                         [cp])
            mrow_ready[b] = [d]

        def exp_unit(b, u):
            r = b % QR
            s, free = pair.take()
            kb, jp = (0, u % 2) if u < 4 else (1, u - 4)
            width = P * (2 - kb)
            ii = range(2 * (u // 2), 2 * (u // 2) + 2) if kb == 0 else range(4)
            for jl in range(2):
                out_m = bank(2 * s + jl).rearrange("p (g k) -> p g k", k=width)[:, :, 0:P]
                mm(out_m, ident_b[:, :], mask_kq[:, 0:len(ii), :], start=True, stop=False,
                   after=free + mrow_ready[b], skip=True)
            for n, i in enumerate(ii):
                for jl in range(2):
                    j = 2 * jp + jl
                    rows_ = slice(32 * j, 32 * j + 32)
                    last = mm(psum[:, 2 * s + jl, n * width:(n + 1) * width],
                              k_stack[r][rows_, i, kb * P:(kb + 1) * P], q_stack[r][rows_, i, kb * P:S],
                              start=False, stop=True, skip=True)
            pi, pfree = p_ring.take()
            dst = tmp[:, 2 * pi:2 * pi + 2, :]
            ex = act(lambda e: e.activation(dst, psum[:, 2 * s:2 * s + 2, :], ACT.Exp, scale=float(HD) ** -0.5),
                     [last] + pfree)
            pair.leave(s, [ex])
            return (b, u, kb, jp, list(ii), width, pi, ex, last)

        HW_ = HD + 1

        def value_unit(unit):
            nonlocal o_free
            b, u, kb, jp, ii, width, pi, ex, _ = unit
            first = u == 0
            for n, i in enumerate(ii):
                for jl in range(2):
                    h = 4 * i + 2 * jp + jl
                    for qb in range(kb, TPB):
                        pT = tmp[:, 2 * pi + jl, n * width + (qb - kb) * P:n * width + (qb - kb + 1) * P]
                        last = mm(psum[:, 6, (qb * HEADS + h) * HW_:(qb * HEADS + h + 1) * HW_], pT,
                                  va[:, TPB * b + kb, h, :], start=first, stop=True,
                                  after=[ex, gated[TPB * b + kb]] + (o_free if first else []), skip=True)
                        first = False
            p_ring.leave(pi, [last])
            if u == 5:
                o = psum[:, 6, 0:TPB * HEADS * HW_].rearrange("p (t h d) -> p t h d", h=HEADS, d=HW_)
                k = b % 2
                rc = dve(lambda e: e.reciprocal(recip[:, k, :, :], o[:, :, :, HD]), [last])
                dst = hT3[:, TPB * b:TPB * (b + 1), :].rearrange("p t (h d) -> p t h d", d=HD)
                for qb in range(TPB):
                    nm = dve(lambda e, qb=qb: e.tensor_tensor(
                        dst[:, qb, :, :], o[:, qb, :, 0:HD],
                        recip[:, k, qb, :].unsqueeze(2).to_broadcast([P, HEADS, HD]), ALU.mult), [rc])
                o_free = [nm]
                attn_out[b] = nm
            return last

        recip = sb("recip", [P, 2, TPB, HEADS])
        attn_out = {}
        LEAD = 9
        for b in range(min(QR, B)):
            stack(b)
        m_next = 0

        def advance_max():
            nonlocal m_next
            if m_next < 6 * B:
                max_unit(m_next // 6, m_next % 6)
                m_next += 1

        for _ in range(LEAD):
            advance_max()
        max_rows(0)
        rows_done = 1
        pending = None
        for e in range(6 * B):
            b, u = divmod(e, 6)
            advance_max()
            if pending is not None:
                lv = value_unit(pending)
                if pending[1] == 5 and pending[0] + QR < B:
                    stack_free[pending[0] % QR] = [lv]
                    stack(pending[0] + QR)
            pending = exp_unit(b, u)
            if rows_done < B and m_next >= 6 * (rows_done + 1) + 1:
                max_rows(rows_done)
                rows_done += 1
            elif rows_done < B and m_next == 6 * B and rows_done == B - 1:
                max_rows(rows_done)
                rows_done += 1
        value_unit(pending)
        for i in range(3):
            for k in (2 * i, 2 * i + 1):
                psum_ring.left[k] = pair.left[i]
        psum_ring.left[6] = o_free
        psum_ring.left[7] = m_free
        for i in range(4):
            for k in (2 * i, 2 * i + 1):
                tmp_ring.left[k] = p_ring.left[i]

        small = sb("small", [P, 2, MOD, B])

        def gated_bias(l, g, name, slot):
            return dve(lambda e: e.tensor_scalar(small[:, l, slot, :], modT[:, l, g, :], col(name), None, ALU.mult),
                       mod_ready + [cols_in])

        bo_ready = gated_bias(0, 2, "L0_attn_bo", 0)

        def add_back(n, src_tmp, ready):
            i, free = psum_ring.take()
            for k in range(CT):
                tr = pe(lambda e, k=k, i=i: e.transpose(psum[:, i, k * P:(k + 1) * P],
                                                       src_tmp[:, k * P:(k + 1) * P], ident[:, :]), ready + free)
            xs = x[:, CT * n:CT * (n + 1), :]
            ad = dve(lambda e, i=i: e.tensor_tensor(xs, xs, bank(i).rearrange("p (t c) -> p t c", c=C), ALU.add),
                     [tr])
            psum_ring.leave(i, [ad])
            return tr, ad

        x1 = {}
        for n in range(NCH):
            i, free = psum_ring.take()
            for k in range(CT):
                t = CT * n + k
                tr = pe(lambda e, k=k, t=t, i=i: e.transpose(psum[:, i, k * P:(k + 1) * P], hT3[:, t, :],
                                                            ident[:, :]), [attn_out[t // TPB]] + free)
            k, tfree = tmp_ring.take()
            cp = act(lambda e, k=k, i=i: e.copy(tmp[:, k, :], bank(i)), [tr] + tfree)
            psum_ring.leave(i, [cp])
            j, free = psum_ring.take()
            pr = mm(bank(j), wo[:, :], tmp[:, k, :], after=[cp] + free)
            k2, tfree2 = tmp_ring.take()
            for h in range(2):
                b = 2 * n + h
                sc = act(lambda e, k2=k2, j=j, b=b, h=h: e.activation(
                    tmp[:, k2, h * S:(h + 1) * S], psum[:, j, h * S:(h + 1) * S], ACT.Identity,
                    bias=small[:, 0, 0, b:b + 1], scale=modT[:, 0, 2, b:b + 1]), [pr, bo_ready] + tfree2)
            tmp_ring.leave(k, [pr])
            psum_ring.leave(j, [sc])
            tr, ad = add_back(n, tmp[:, k2, :], [sc])
            tmp_ring.leave(k2, [tr])
            x1[2 * n] = x1[2 * n + 1] = ad

        xpT = big1[:, 0:TOK]
        fvec = sb("fvec", [P, 2, 4, TPB])
        xp_ready = {}
        FS = 1.0 / float(np.sqrt(C))
        att_done = {}
        for b in range(B):
            bs = slice(b * S, (b + 1) * S)
            hr = normalise(b, 0, True, lambda b: [x1[b]])
            i, free = psum_ring.take()
            for w in range(2):
                last = mm(psum[:, i, w * S:(w + 1) * S], fw[:, w, :], hT[:, bs], after=[hr] + free)
            kq, f1 = tmp_ring.take()
            act(lambda e, kq=kq, i=i: e.activation(tmp[:, kq, 0:S], psum[:, i, 0:S], ACT.Identity,
                                                   bias=col("L0_ffn_bq")), [last] + f1)
            qk = act(lambda e, kq=kq, i=i: e.activation(tmp[:, kq, S:2 * S], psum[:, i, S:2 * S], ACT.Identity,
                                                        bias=col("L0_ffn_bk")))
            psum_ring.leave(i, [qk])
            i, free = psum_ring.take()
            for n in range(TPB):
                last = mm(psum[:, i, n * C:(n + 1) * C], hT[:, b * S + n * P:b * S + (n + 1) * P], fw[:, 2, :],
                          after=[hr] + free)
            kv, f2 = tmp_ring.take()
            vt = tmp[:, kv, 0:TPB * C].rearrange("p (t c) -> p t c", c=C)
            vr = dve(lambda e, vt=vt, i=i: e.tensor_tensor(
                vt, psum[:, i, 0:TPB * C].rearrange("p (t c) -> p t c", c=C),
                row("L0_ffn_bv").unsqueeze(1).to_broadcast([P, TPB, C]), ALU.add), [last] + f2)
            psum_ring.leave(i, [vr])
            i, free = psum_ring.take()
            for n in range(TPB):
                last = mm(psum[:, i, n * S:(n + 1) * S], tmp[:, kq, n * P:(n + 1) * P], tmp[:, kq, S:2 * S],
                          after=[qk] + free)
            tmp_ring.leave(kq, [last])
            fv = fvec[:, b % 2, :, :]
            mx = dve(lambda e, fv=fv, i=i: e.tensor_reduce(
                fv[:, 0, :], bank(i).rearrange("p (t k) -> p t k", k=S), X_AXIS, ALU.max), [last])
            ng = dve(lambda e, fv=fv: e.tensor_scalar(fv[:, 1, :], fv[:, 0, :], -FS, None, ALU.mult), [mx])
            kp, f3 = tmp_ring.take()
            for n in range(TPB):
                ex = act(lambda e, n=n, fv=fv, kp=kp, i=i: e.activation(
                    tmp[:, kp, n * S:(n + 1) * S], psum[:, i, n * S:(n + 1) * S], ACT.Exp,
                    bias=fv[:, 1, n:n + 1], scale=FS, accum_out=fv[:, 2, n:n + 1]), [ng] + f3)
            psum_ring.leave(i, [ex])
            rc = dve(lambda e, fv=fv: e.reciprocal(fv[:, 3, :], fv[:, 2, :]), [ex])
            for n in range(TPB):
                sc = dve(lambda e, n=n, fv=fv, kp=kp: e.tensor_scalar(
                    tmp[:, kp, n * S:(n + 1) * S], tmp[:, kp, n * S:(n + 1) * S], fv[:, 3, n:n + 1], None,
                    ALU.mult), [rc])
            i, free = psum_ring.take()
            for kb in range(TPB):
                for qb in range(TPB):
                    tr = pe(lambda e, kb=kb, qb=qb, kp=kp, i=i: e.transpose(
                        psum[:, i, kb * S + qb * P:kb * S + (qb + 1) * P],
                        tmp[:, kp, qb * S + kb * P:qb * S + (kb + 1) * P], ident[:, :]), [sc] + free)
            tmp_ring.leave(kp, [tr])
            kt, f4 = tmp_ring.take()
            cp = act(lambda e, kt=kt, i=i: e.copy(tmp[:, kt, :], bank(i)), [tr] + f4)
            psum_ring.leave(i, [cp])
            i, free = psum_ring.take()
            for kb in range(TPB):
                last = mm(psum[:, i, 0:S], vt[:, kb, :], tmp[:, kt, kb * S:(kb + 1) * S], start=kb == 0,
                          stop=kb == TPB - 1, after=[cp, vr] + free)
            tmp_ring.leave(kt, [last])
            tmp_ring.leave(kv, [last])
            ka, f5 = tmp_ring.take()
            cp = act(lambda e, ka=ka, i=i: e.copy(tmp[:, ka, 0:S], psum[:, i, 0:S]), [last] + f5)
            psum_ring.leave(i, [cp])
            i, free = psum_ring.take()
            last = mm(psum[:, i, 0:S], fw[:, 3, :], tmp[:, ka, 0:S], after=[cp] + free)
            tmp_ring.leave(ka, [last])
            xp_ready[b] = dve(lambda e, bs=bs, i=i: e.scalar_tensor_tensor(
                xpT[:, bs], psum[:, i, 0:S], col("L0_ffn_bo"), hT[:, bs], ALU.add, ALU.add), [last])
            psum_ring.leave(i, [xp_ready[b]])

        gates = sb("gates", [P, NT, NE])
        gmax = sb("gmax", [P, NT])
        i, free = psum_ring.take()
        for t in range(NT):
            last = mm(psum[:, i, t * NE:(t + 1) * NE], xpT[:, t * P:(t + 1) * P], wg[:, :],
                      after=[xp_ready[t // TPB]] + free)

        def softmax8(logits, src_i, last, bias):
            src = psum[:, src_i, 0:NT * NE].rearrange("p (t e) -> p t e", e=NE)
            if bias is not None:
                s1 = dve(lambda e: e.tensor_tensor(logits[:, :, :], src,
                                                   bias.unsqueeze(1).to_broadcast([P, NT, NE]), ALU.add), [last])
            else:
                s1 = dve(lambda e: e.tensor_copy(logits[:, :, :], src), [last])
            psum_ring.leave(src_i, [s1])
            wide = gmax[:, :].unsqueeze(2).to_broadcast([P, NT, NE])
            s2 = dve(lambda e: e.tensor_reduce(gmax[:, :], logits[:, :, :], X_AXIS, ALU.max), [s1])
            s3 = dve(lambda e: e.tensor_tensor(logits[:, :, :], logits[:, :, :], wide, ALU.subtract), [s2])
            s4 = act(lambda e: e.activation(logits[:, :, :], logits[:, :, :], ACT.Exp), [s3])
            s5 = dve(lambda e: e.tensor_reduce(gmax[:, :], logits[:, :, :], X_AXIS, ALU.add), [s4])
            s6 = dve(lambda e: e.reciprocal(gmax[:, :], gmax[:, :]), [s5])
            return dve(lambda e: e.tensor_tensor(logits[:, :, :], logits[:, :, :], wide, ALU.mult), [s6])

        gates_ready = softmax8(gates, i, last, row("L0_ffn_bg"))

        for n in range(NCH):
            k, tfree = tmp_ring.take()
            for h in range(2):
                b = 2 * n + h
                sc = pool(lambda e, k=k, b=b, h=h: e.tensor_scalar(
                    tmp[:, k, h * S:(h + 1) * S], xpT[:, b * S:(b + 1) * S], modT[:, 0, 5, b:b + 1], None, ALU.mult),
                    [xp_ready[b]] + tfree)
            tr, ad = add_back(n, tmp[:, k, :], [sc])
            tmp_ring.leave(k, [tr])
            x1[2 * n] = x1[2 * n + 1] = ad

        y = hT3
        gT = sb("gT", [NE, CHUNK])
        y_ready = {}
        for n in range(NCH):
            i, free = psum_ring.take()
            for k in range(CT):
                t = CT * n + k
                tr = pe(lambda e, k=k, t=t, i=i: e.transpose(psum[0:NE, i, k * P:(k + 1) * P], gates[:, t, :],
                                                            ident[:, :]), [gates_ready] + free)
            prev = [y_ready[CT * (n - 1)]] if n else []
            cp = act(lambda e, i=i: e.copy(gT[:, :], psum[0:NE, i, :]), [tr] + prev)
            psum_ring.leave(i, [cp])
            i, free = psum_ring.take()
            for k in range(CT):
                last = mm(psum[:, i, k * C:(k + 1) * C], gT[:, k * P:(k + 1) * P], b2[:, :], after=[cp, ew_in] + free)
            cp = act(lambda e, i=i, n=n: e.copy(hT[:, n * CHUNK:(n + 1) * CHUNK], bank(i)), [last])
            psum_ring.leave(i, [cp])
            for k in range(CT):
                y_ready[CT * n + k] = cp
        hid = big2[:, 0:2 * FC * CHUNK].rearrange("p (r f t) -> p r f t", r=2, f=FC)
        hid_ring = Ring(2)

        def up(e_, n, src, src_ready, func):
            r, hfree = hid_ring.take()
            done = []
            for f in range(FC):
                i, free = psum_ring.take()
                last = mm(bank(i), ew1[:, e_, f * P:(f + 1) * P], src, after=[src_ready] + free + ew_ready)
                done.append(func(i, r, f, e_, last, hfree))
            return r, done

        def down(e_, r, done):
            i, free = psum_ring.take()
            for k in range(CT):
                for f in range(FC):
                    last = mm(psum[:, i, k * C:(k + 1) * C], hid[:, r, f, k * P:(k + 1) * P], ew2[:, e_, f, :],
                              start=f == 0, stop=f == FC - 1, after=done + free)
            hid_ring.leave(r, [last])
            return i, last

        def relu(i, r, f, e_, last, hfree):
            s = act(lambda e: e.activation(hid[:, r, f, :], bank(i), ACT.Relu,
                                           bias=col("L0_ffn_b1", e_ * FC + f)), [last] + hfree)
            psum_ring.leave(i, [s])
            return s

        ew_ready = [ew_in]

        def mix(n, e_, i, last):
            for k in range(CT):
                t = CT * n + k
                s = dve(lambda e, k=k, t=t: e.scalar_tensor_tensor(
                    y[:, t, :], psum[:, i, k * C:(k + 1) * C], gates[:, t, e_:e_ + 1], y[:, t, :], ALU.mult, ALU.add),
                    [last, y_ready[t]])
                y_ready[t] = s
            psum_ring.leave(i, [s])

        pending = None
        for n in range(NCH):
            for e_ in range(NE):
                r, done = up(e_, n, xpT[:, n * CHUNK:(n + 1) * CHUNK], xp_ready[2 * n + 1], relu)
                if pending:
                    pn, pe_, pr, pdone = pending
                    i, last = down(pe_, pr, pdone)
                    mix(pn, pe_, i, last)
                pending = (n, e_, r, done)
        pn, pe_, pr, pdone = pending
        i, last_l0 = down(pe_, pr, pdone)
        mix(pn, pe_, i, last_l0)

        s_ew2 = stream("experts1")
        load(s_ew2, ew1[:, :, :], a["L1_ffn_w1"].rearrange("e p f -> p e f"), [last_l0])
        ew1_in = load(s_ew2, ew2[:, :, :, :], a["L1_ffn_w2"].rearrange("e (k p) c -> p e k c", p=P))

        gates_tok = spread_gates(0, [])

        def add_gated(n, src, ready):
            for h in range(2):
                b = 2 * n + h
                ts = slice(TPB * b, TPB * (b + 1))
                k, tfree = tmp_ring.take()
                t3 = tmp[:, k, 0:TPB * C].rearrange("p (t c) -> p t c", c=C)
                m = pool(lambda e, ts=ts, t3=t3, b=b: e.tensor_tensor(
                    t3, src[:, ts, :], gb_tok[:, b, :].unsqueeze(1).to_broadcast([P, TPB, C]), ALU.mult),
                    ready + tfree + [gates_tok])
                ad = dve(lambda e, ts=ts, t3=t3: e.tensor_tensor(x[:, ts, :], x[:, ts, :], t3, ALU.add),
                         [m, x1[b]])
                tmp_ring.leave(k, [ad])
                x1[b] = ad

        for n in range(NCH):
            add_gated(n, y, [y_ready[CT * n + CT - 1]])

        gates_tok = spread_gates(1, [x1[b] for b in range(B)])

        for g in range(5):
            i, free = psum_ring.take()
            tr = pe(lambda e, g=g, i=i: e.transpose(psum[:, i, 0:C], w_raw[:, g, :], ident[:, :]), free)
            wt = dve(lambda e, g=g, i=i: e.tensor_copy(w_t[:, g, :], psum[:, i, 0:C]), [tr, w_in])
            psum_ring.leave(i, [wt])
        G2 = 2 * HEADS
        cen = sb("cen", [P, G2])

        def centre(t, ready):
            t3 = t.rearrange("p (g d) -> p g d", d=HD)
            s1 = dve(lambda e: e.tensor_reduce(cen[:, :], t3, X_AXIS, ALU.add), ready)
            s2 = dve(lambda e: e.tensor_scalar(cen[:, :], cen[:, :], 1.0 / HD, None, ALU.mult), [s1])
            return dve(lambda e: e.tensor_tensor(t3, t3, cen[:, :].unsqueeze(2).to_broadcast([P, G2, HD]),
                                                 ALU.subtract), [s2])

        wkv = w_t[:, 1:3, :].rearrange("p g c -> p (g c)")
        wkv_ready = centre(wkv, [wt])
        bkv = rows[:, ROWS["L1_attn_qkv_b"][0] + C:ROWS["L1_attn_qkv_b"][0] + 3 * C]
        bkv_ready = centre(bkv, [wkv_ready])
        temp_blk = sb("temp_blk", [P, C])
        bias_blk = sb("bias_blk", [P, C])
        tcol = sb("tcol", [P, 1])
        s_blk = stream("blocks")
        z6 = pool(lambda e: e.memset(temp_blk[:, :], 1.0 / S))
        z7 = pool(lambda e: e.memset(bias_blk[:, :], 0.0))
        for h in range(HEADS):
            hs = slice(h * HD, (h + 1) * HD)
            load(s_blk, tcol[hs, :], a["L1_attn_temperature"][h, :, :].to_broadcast([HD, 1]))
            blk_in = load(s_blk, bias_blk[hs, hs], a["L1_attn_attn_bias"][h, :, :], [z7])
        t3 = temp_blk[:, :].rearrange("p (h d) -> p h d", d=HD)
        z8 = select(t3, [[-HD, HEADS], [0, HD]], 1, 0, 0.0, ALU.is_ge, [z6])
        z9 = select(t3, [[HD, HEADS], [0, HD]], -1, HD - 1, 0.0, ALU.is_ge, [z8])
        blk_ready = dve(lambda e: e.tensor_scalar(temp_blk[:, :], temp_blk[:, :], tcol[:, 0:1], None, ALU.mult),
                        [z9, blk_in])
        gam = sb("gam", [P, G2, HD])
        bet = sb("bet", [P, G2, HD])
        for half, nm in ((0, "kn"), (1, "vn")):
            for dst, wh in ((gam, "g"), (bet, "b")):
                affine = pool(lambda e, half=half, dst=dst, nm=nm, wh=wh: e.tensor_copy(
                    dst[:, half * HEADS:(half + 1) * HEADS, :],
                    row(f"L1_attn_{nm}_{wh}").unsqueeze(1).to_broadcast([P, HEADS, HD])), [rows_in])
        p2_ready = gated_bias(1, 2, "L1_attn_p2_b", 0)

        var = sb("var", [P, 2, TPB * G2])
        vrs = sb("vrs", [P, 2, TPB * G2])
        vt_ = sb("vt", [P, 2, TPB * G2])
        for b in range(B):
            bs = slice(b * S, (b + 1) * S)
            hr = normalise(b, 1, False, lambda b: [x1[b]])
            i, free = psum_ring.take()
            last = mm(psum[:, i, 0:S], w_t[:, 0, :], hT[:, bs], after=[hr, wt] + free)
            kq, f1 = tmp_ring.take()
            qs = act(lambda e, kq=kq, i=i: e.activation(tmp[:, kq, 0:S], psum[:, i, 0:S], ACT.Identity,
                                                        bias=col("L1_attn_qkv_b")), [last] + f1)
            psum_ring.leave(i, [qs])
            i, free = psum_ring.take()
            for n in range(TPB):
                last = mm(psum[:, i, n * 2 * C:(n + 1) * 2 * C], hT[:, b * S + n * P:b * S + (n + 1) * P], wkv,
                          after=[hr, wkv_ready] + free)
            kk, f2 = tmp_ring.take()
            t2 = tmp[:, kk, :].rearrange("p (t n) -> p t n", n=2 * C)
            kvb = dve(lambda e, t2=t2, i=i: e.tensor_tensor(
                t2, bank(i).rearrange("p (t n) -> p t n", n=2 * C), bkv.unsqueeze(1).to_broadcast([P, TPB, 2 * C]),
                ALU.add), [last, bkv_ready] + f2)
            psum_ring.leave(i, [kvb])
            ks, f3 = tmp_ring.take()
            sq = act(lambda e, ks=ks, kk=kk: e.activation(tmp[:, ks, :], tmp[:, kk, :], ACT.Square), [kvb] + f3)
            vv = var[:, b % 2, :]
            s1 = dve(lambda e, ks=ks, vv=vv: e.tensor_reduce(
                vv, tmp[:, ks, :].rearrange("p (g d) -> p g d", d=HD), X_AXIS, ALU.add), [sq])
            tmp_ring.leave(ks, [s1])
            s2 = dve(lambda e, vv=vv: e.tensor_scalar(vv, vv, 1.0 / HD, EPS, ALU.mult, ALU.add), [s1])
            vr_ = vrs[:, b % 2, :]
            s3 = rsqrt(vr_, vv, vt_[:, b % 2, :], [s2], pool)
            kg = tmp[:, kk, :].rearrange("p (g d) -> p g d", d=HD)
            s4 = dve(lambda e, kg=kg, vr_=vr_: e.tensor_tensor(
                kg, kg, vr_.unsqueeze(2).to_broadcast([P, TPB * G2, HD]), ALU.mult), [s3])
            g2 = gam[:, :, :].rearrange("p g d -> p (g d)").unsqueeze(1).to_broadcast([P, TPB, 2 * C])
            be2 = bet[:, :, :].rearrange("p g d -> p (g d)").unsqueeze(1).to_broadcast([P, TPB, 2 * C])
            s5 = pool(lambda e, t2=t2, g2=g2: e.tensor_tensor(t2, t2, g2, ALU.mult), [s4, affine])
            s6 = pool(lambda e, t2=t2, be2=be2: e.tensor_tensor(t2, t2, be2, ALU.add), [s5])
            i, free = psum_ring.take()
            for n in range(TPB):
                last = mm(psum[:, i, 0:C], t2[:, n, 0:C], t2[:, n, C:2 * C], start=n == 0, stop=n == TPB - 1,
                          after=[s6] + free)
            tmp_ring.leave(kk, [last])
            kb_, f4 = tmp_ring.take()
            s7 = dve(lambda e, kb_=kb_, i=i: e.tensor_tensor(tmp[:, kb_, 0:C], psum[:, i, 0:C], temp_blk[:, :],
                                                             ALU.mult), [last, blk_ready] + f4)
            psum_ring.leave(i, [s7])
            s8 = dve(lambda e, kb_=kb_: e.tensor_tensor(tmp[:, kb_, 0:C], tmp[:, kb_, 0:C], bias_blk[:, :],
                                                        ALU.add), [s7])
            i, free = psum_ring.take()
            last = mm(psum[:, i, 0:S], tmp[:, kb_, 0:C], tmp[:, kq, 0:S], after=[s8, qs] + free)
            tmp_ring.leave(kb_, [last])
            tmp_ring.leave(kq, [last])
            ka, f5 = tmp_ring.take()
            at = dve(lambda e, ka=ka, i=i, bs=bs: e.tensor_tensor(tmp[:, ka, 0:S], psum[:, i, 0:S], hT[:, bs],
                                                                  ALU.add), [last] + f5)
            psum_ring.leave(i, [at])
            i, free = psum_ring.take()
            last = mm(psum[:, i, 0:S], w_t[:, 3, :], tmp[:, ka, 0:S], after=[at] + free)
            tmp_ring.leave(ka, [last])
            kh, f6 = tmp_ring.take()
            ge = act(lambda e, kh=kh, i=i: e.activation(tmp[:, kh, 0:S], psum[:, i, 0:S], ACT.Gelu,
                                                        bias=col("L1_attn_p1_b")), [last] + f6)
            psum_ring.leave(i, [ge])
            i, free = psum_ring.take()
            last = mm(psum[:, i, 0:S], w_t[:, 4, :], tmp[:, kh, 0:S], after=[ge] + free)
            tmp_ring.leave(kh, [last])
            ko, f7 = tmp_ring.take()
            o1 = dve(lambda e, ko=ko, i=i, bs=bs: e.tensor_tensor(tmp[:, ko, 0:S], psum[:, i, 0:S], hT[:, bs],
                                                                  ALU.add), [last] + f7)
            psum_ring.leave(i, [o1])
            o2 = act(lambda e, ko=ko, b=b: e.activation(
                tmp[:, ko, 0:S], tmp[:, ko, 0:S], ACT.Identity, bias=small[:, 1, 0, b:b + 1],
                scale=modT[:, 1, 2, b:b + 1]), [o1, p2_ready])
            i, free = psum_ring.take()
            for n in range(TPB):
                tr = pe(lambda e, n=n, ko=ko, i=i: e.transpose(psum[:, i, n * P:(n + 1) * P],
                                                              tmp[:, ko, n * P:(n + 1) * P], ident[:, :]),
                        [o2] + free)
            tmp_ring.leave(ko, [tr])
            ts = slice(TPB * b, TPB * (b + 1))
            x1[b] = dve(lambda e, ts=ts, i=i: e.tensor_tensor(
                x[:, ts, :], x[:, ts, :], psum[:, i, 0:S].rearrange("p (t c) -> p t c", c=C), ALU.add), [tr])
            psum_ring.leave(i, [x1[b]])

        h4 = {b: normalise(b, 1, True, lambda b: [x1[b]]) for b in range(B)}
        sc = sb("scores", [P, NT, NE])
        i, free = psum_ring.take()
        for t in range(NT):
            last = mm(psum[:, i, t * NE:(t + 1) * NE], hT[:, t * P:(t + 1) * P], wr[:, :],
                      after=[h4[t // TPB]] + free)
        scored = softmax8(sc, i, last, None)
        desc = sb("desc", [P, NE])
        capbase = sb("capbase", [P, NE])
        for e_ in range(NE):
            pool(lambda e, e_=e_: e.memset(desc[:, e_:e_ + 1], float(NE - e_)))
            tables = pool(lambda e, e_=e_: e.memset(capbase[:, e_:e_ + 1], float(CAP * e_)))

        def wide(t):
            return t[:, :].unsqueeze(1).to_broadcast([P, NT, NE])

        def over(t):
            return t.unsqueeze(2).to_broadcast([P, NT, NE])

        def carve(n, dims, **sizes):
            return big2[:, n * NT * NE:(n + 1) * NT * NE].rearrange(dims, **sizes)

        pick = [carve(k, "p (t e) -> p t e", e=NE) for k in range(TOPK)]
        wts = sb("wts", [P, TOPK, NT])
        best = sb("best", [P, NT])
        left = carve(2, "p (t e) -> p t e", e=NE)
        ready = dve(lambda e: e.tensor_copy(left[:, :, :], sc[:, :, :]), [scored])
        for k in range(TOPK):
            pk = pick[k]
            r1 = dve(lambda e, k=k: e.tensor_reduce(wts[:, k, :], left[:, :, :], X_AXIS, ALU.max), [ready])
            r2 = dve(lambda e, k=k, pk=pk: e.tensor_tensor(pk[:, :, :], left[:, :, :], over(wts[:, k, :]),
                                                           ALU.is_equal), [r1])
            r3 = dve(lambda e, pk=pk: e.tensor_tensor(pk[:, :, :], pk[:, :, :], wide(desc), ALU.mult), [r2, tables])
            r4 = dve(lambda e, pk=pk: e.tensor_reduce(best[:, :], pk[:, :, :], X_AXIS, ALU.max), [r3])
            r5 = dve(lambda e, pk=pk: e.tensor_tensor(pk[:, :, :], pk[:, :, :], over(best[:, :]), ALU.is_equal),
                     [r4])
            ready = dve(lambda e, pk=pk: e.scalar_tensor_tensor(
                left[:, :, :], pk[:, :, :], -2.0, left[:, :, :], ALU.mult, ALU.add), [r5])
        sel = sb("sel", [P, NE, NT], BF16)
        sl = dve(lambda e: e.tensor_tensor(sel[:, :, :].rearrange("p e t -> p t e"), pick[0][:, :, :],
                                           pick[1][:, :, :], ALU.add), [ready])
        iw, free1 = psum_ring.take()
        it, free2 = psum_ring.take()
        flat = sel[:, :, :].rearrange("p e t -> p (e t)")
        mw = mm(psum[:, iw, 0:NE * NT], before[:, :], flat, after=[sl, counters] + free1)
        mt = mm(psum[:, it, 0:NE * NT], ones_b[:, :], flat, after=free2)
        tot = carve(3, "p (e t) -> p e t", t=NT)
        run = carve(4, "p (e t) -> p e t", t=NT)
        keep = carve(5, "p (e t) -> p e t", t=NT)
        k1 = pool(lambda e: e.memset(keep[:, :, :], 1.0))
        k2 = pool(lambda e: e.memset(keep[:, :, 0:1], 0.0), [k1])
        c1 = dve(lambda e: e.tensor_copy(tot[:, :, :], psum[:, it, 0:NE * NT].rearrange("p (e t) -> p e t", t=NT)),
                 [mt])
        psum_ring.leave(it, [c1])
        c2 = dve(lambda e: e.tensor_tensor_scan(
            run[:, :, :].rearrange("p e t -> p (e t)"), keep[:, :, :].rearrange("p e t -> p (e t)"),
            tot[:, :, :].rearrange("p e t -> p (e t)"), 0.0, ALU.mult, ALU.add), [c1, k2])
        c3 = dve(lambda e: e.tensor_tensor(run[:, :, :], run[:, :, :], tot[:, :, :], ALU.subtract), [c2])
        c4 = dve(lambda e: e.tensor_tensor(
            run[:, :, :], psum[:, iw, 0:NE * NT].rearrange("p (e t) -> p e t", t=NT), run[:, :, :], ALU.add),
            [c3, mw])
        psum_ring.leave(iw, [c4])
        rank = run[:, :, :].rearrange("p e t -> p t e")
        slot_f = sb("slot_f", [P, TOPK, NT])
        rank_f = sb("rank_f", [P, TOPK, NT])
        slot_i = sb("slot_i", [P, TOPK, NT], I32)
        for k in range(TOPK):
            d1 = dve(lambda e, k=k: e.tensor_tensor(left[:, :, :], pick[k][:, :, :], rank, ALU.mult), [c4])
            d2 = dve(lambda e, k=k: e.tensor_reduce(rank_f[:, k, :], left[:, :, :], X_AXIS, ALU.add), [d1])
            d3 = dve(lambda e, k=k: e.tensor_tensor(left[:, :, :], pick[k][:, :, :], wide(capbase), ALU.mult), [d2])
            d4 = dve(lambda e, k=k: e.tensor_reduce(slot_f[:, k, :], left[:, :, :], X_AXIS, ALU.add), [d3])
            d5 = dve(lambda e, k=k: e.tensor_tensor(slot_f[:, k, :], slot_f[:, k, :], rank_f[:, k, :], ALU.add),
                     [d4])
            d6 = dve(lambda e, k=k: e.tensor_scalar(rank_f[:, k, :], rank_f[:, k, :], float(CAP), float(SLOTS),
                                                    ALU.is_ge, ALU.mult), [d5])
            d7 = dve(lambda e, k=k: e.tensor_tensor(slot_f[:, k, :], slot_f[:, k, :], rank_f[:, k, :], ALU.add),
                     [d6])
            slots_ready = dve(lambda e, k=k: e.tensor_copy(slot_i[:, k, :], slot_f[:, k, :]), [d7])

        RT = 16
        rows_buf = big1[:, 0:RT * TOPK * ROW].rearrange("p (t k n) -> p t k n", k=TOPK, n=ROW)
        dest = sb("dest", [P, TOPK, NT], I32)
        io = pool(lambda e: e.iota(dest[:, :, :], pattern=[[TOK, TOPK], [P, NT]], base=0, channel_multiplier=1))
        s_sc = [stream(f"scatter{i}") for i in range(2)]
        sent = []
        for half in range(NT // RT):
            h0 = half * RT
            for k in range(TOPK):
                m1 = dve(lambda e, k=k, h0=h0: e.tensor_copy(rows_buf[:, :, k, C], dest[:, k, h0:h0 + RT]),
                         [io] + sent)
                m2 = dve(lambda e, k=k, h0=h0: e.tensor_copy(rows_buf[:, :, k, C + 1], wts[:, k, h0:h0 + RT]), sent)
            new = []
            for n in range(RT // CT):
                i, free = psum_ring.take()
                for m in range(CT):
                    t = h0 + n * CT + m
                    tr = pe(lambda e, m=m, t=t, i=i: e.transpose(psum[:, i, m * P:(m + 1) * P],
                                                                hT[:, t * P:(t + 1) * P], ident[:, :]),
                            [h4[t // TPB]] + free)
                src = bank(i).rearrange("p (t c) -> p t c", c=C)
                ca = act(lambda e, n=n, src=src: e.copy(rows_buf[:, n * CT:(n + 1) * CT, 0, 0:C], src),
                         [tr] + sent)
                cb = dve(lambda e, n=n, src=src: e.tensor_copy(rows_buf[:, n * CT:(n + 1) * CT, 1, 0:C], src),
                         [ca] + sent)
                psum_ring.leave(i, [cb])
                for m in range(CT):
                    t = h0 + n * CT + m
                    for k in range(TOPK):
                        d = q.dma("gpsimd", s_sc[half], lambda e, k=k, t=t, m=m, n=n: e.indirect_dma_start(
                            out=routed, out_offset=bass.IndirectOffsetOnAxis(ap=slot_i[:, k, t:t + 1], axis=0),
                            in_=rows_buf[:, n * CT + m, k, :], in_offset=None, bounds_check=SLOTS - 1,
                            oob_is_err=False), [ca, cb, m1, m2, slots_ready, routed_empty])
            new = [d]
            sent = new
            all_sent = (all_sent if half else []) + [d]

        xb = big1[:, RT * TOPK * ROW:RT * TOPK * ROW + 2 * CT * ROW].rearrange("p (r n c) -> p r n c", r=2, c=ROW)
        to = sb("to", [P, 2, CT], I32)
        s_xb = [stream(f"xb{i}") for i in range(2)]
        s_out = [stream(f"ans{i}") for i in range(2)]
        xb_left = [[], []]
        routed_v = routed.rearrange("(u n p) c -> u p n c", p=P, n=CT)
        UNITS = SLOTS // CHUNK
        yw = [None, None]
        ans_sent = [[], []]
        ew_ready = [ew1_in]
        ans_buf = hT[:, 0:2 * CHUNK].rearrange("p (r n c) -> p r n c", r=2, c=C)

        def gelu(i, r, f, e_, last, hfree):
            s = act(lambda e: e.activation(hid[:, r, f, :], bank(i), ACT.Gelu_apprx_tanh), [last] + hfree)
            psum_ring.leave(i, [s])
            return s

        def finish(unit, r, done):
            k = unit % 2
            e_ = unit * CHUNK // CAP
            i, last = down(e_, r, done)
            for m in range(CT):
                s = dve(lambda e, m=m: e.tensor_scalar(ans_buf[:, k, m, :], psum[:, i, m * C:(m + 1) * C],
                                                       xb[:, k, m, C + 1:C + 2], None, ALU.mult),
                        [last] + ans_sent[k] + [xb_in[unit], h4_read])
            psum_ring.leave(i, [s])
            for m in range(CT):
                d = q.dma("gpsimd", s_out[k], lambda e, m=m: e.indirect_dma_start(
                    out=answers, out_offset=bass.IndirectOffsetOnAxis(ap=to[:, k, m:m + 1], axis=0),
                    in_=ans_buf[:, k, m, :], in_offset=None, bounds_check=TOPK * TOK - 1, oob_is_err=False),
                    [s, to_in[unit], answers_zero])
            ans_sent[k] = [d]
            xb_left[k] = [s]

        h4_read = tr
        xb_in, to_in = {}, {}
        pending = None
        for unit in range(UNITS):
            k = unit % 2
            xb_in[unit] = load(s_xb[k], xb[:, k, :, :], routed_v[unit], all_sent + xb_left[k] + ans_sent[k])
            to_in[unit] = dve(lambda e, k=k: e.tensor_copy(to[:, k, :], xb[:, k, :, C]),
                              [xb_in[unit]] + ans_sent[k])
            i, free = psum_ring.take()
            for m in range(CT):
                tr = pe(lambda e, m=m, k=k, i=i: e.transpose(psum[:, i, m * P:(m + 1) * P], xb[:, k, m, 0:C],
                                                            ident[:, :]), [xb_in[unit]] + free)
            kx, tfree = tmp_ring.take()
            cp = dve(lambda e, kx=kx, i=i: e.tensor_copy(tmp[:, kx, :], bank(i)), [tr] + tfree)
            psum_ring.leave(i, [cp])
            r, done = up(unit * CHUNK // CAP, unit, tmp[:, kx, :], cp, gelu)
            tmp_ring.leave(kx, done)
            if pending:
                finish(*pending)
            pending = (unit, r, done)
        finish(*pending)

        out_v = out.rearrange("b (t p) c -> p (b t) c", p=P)
        s_y = [stream(f"yin{i}") for i in range(2)]
        s_res = stream("result")
        ans_v = answers.rearrange("(k n p) c -> k p n c", k=TOPK, p=P)
        yb = big1[:, 0:4 * CHUNK].rearrange("p (r k t c) -> p r k t c", r=2, k=TOPK, c=C)
        yfree = [[], []]
        s_last = ans_sent[0] + ans_sent[1]
        for n in range(NCH):
            r = n % 2
            ts = slice(CT * n, CT * (n + 1))
            for k in range(TOPK):
                d = load(s_y[r], yb[:, r, k, :, :], ans_v[k, :, ts, :], s_last + yfree[r])
            s1 = dve(lambda e, r=r: e.tensor_tensor(yb[:, r, 0, :, :], yb[:, r, 0, :, :], yb[:, r, 1, :, :],
                                                    ALU.add), [d])
            s2 = dve(lambda e, r=r: e.tensor_tensor(
                yb[:, r, 0, :, :], yb[:, r, 0, :, :], row("L1_ffn_bias").unsqueeze(1).to_broadcast([P, CT, C]),
                ALU.add), [s1])
            add_gated_src = yb[:, r, 0, :, :]
            for h in range(2):
                b = 2 * n + h
                m = dve(lambda e, h=h, b=b, src=add_gated_src: e.tensor_tensor(
                    src[:, TPB * h:TPB * (h + 1), :], src[:, TPB * h:TPB * (h + 1), :],
                    gb_tok[:, b, :].unsqueeze(1).to_broadcast([P, TPB, C]), ALU.mult), [s2, gates_tok])
            ad = dve(lambda e, ts=ts, src=add_gated_src: e.tensor_tensor(x[:, ts, :], x[:, ts, :], src, ALU.add),
                     [m, x1[2 * n + 1]])
            yfree[r] = [ad]
            res = load(s_res, out_v[:, ts, :], x[:, ts, :], [ad])

        q.number()
        block = ctx.enter_context(nc.Block())

        @block.sync
        def _(eng):
            q.play("sync", eng)
            for st in [s_res, s_fill] + s_part + s_sc + s_out:
                eng.wait_ge(st.sem, st.count)

        @block.tensor
        def _(eng):
            q.play("tensor", eng)

        @block.vector
        def _(eng):
            q.play("vector", eng)

        @block.scalar
        def _(eng):
            q.play("scalar", eng)

        @block.gpsimd
        def _(eng):
            q.play("gpsimd", eng)


def kernel(**inputs):
    import concourse.bacc as bacc
    from concourse.bass_utils import run_bass_kernel_spmd

    nc = bacc.Bacc("TRN2", target_bir_lowering=False, num_devices=1)
    arrays, aps = {}, {}
    for name, value in inputs.items():
        v = np.ascontiguousarray(value)
        arrays[f"in_{name}"] = v
        aps[name] = nc.dram_tensor(f"in_{name}", v.shape, mybir.dt.from_np(v.dtype), kind="ExternalInput").ap()
    out = nc.dram_tensor("out", (B, S, C), F32, kind="ExternalOutput").ap()
    build(nc, aps, out)
    r = run_bass_kernel_spmd(nc, [arrays], core_ids=[0])
    return r.results[0]["out"]
```

```python
from contextlib import ExitStack

import numpy as np
import concourse.bass as bass
from concourse import mybir

F32 = mybir.dt.float32
F32R = mybir.dt.float32r
BF16 = mybir.dt.bfloat16
I32 = mybir.dt.int32
ALU = mybir.AluOpType
ACT = mybir.ActivationFunctionType
X_AXIS = mybir.AxisListType.X

B, S, C = 16, 256, 128
P = 128
TOK = B * S
NT = TOK // P
TPB = S // P
HEADS, HD = 16, 8
HID = 64
GW = 16
NE, FF = 8, 512
FC = FF // P
CHUNK = 512
NCH = TOK // CHUNK
CT = CHUNK // P
TOPK = 2
CAP = TOPK * TOK // NE
SLOTS = NE * CAP
EPS = 1e-5
MASKED = -1e30
ROW = C + 2
MOD = 6


class Step:

    def __init__(self, engine, emit, after):
        self.engine, self.emit, self.after, self.signals, self.value = engine, emit, after, False, None


class Landed:

    def __init__(self, stream, value):
        self.stream, self.value = stream, value


class Stream:

    def __init__(self, sem):
        self.sem, self.count = sem, 0


class Queues:

    def __init__(self, nc, new_sem):
        self.nc = nc
        self.lists = {n: [] for n in ("tensor", "vector", "scalar", "gpsimd", "sync")}
        self.sems = {n: new_sem(f"done_{n}") for n in ("tensor", "vector", "scalar", "gpsimd")}

    def step(self, engine, emit, after=()):
        s = Step(engine, emit, list(after))
        for a in s.after:
            if isinstance(a, Step):
                a.signals = True
        self.lists[engine].append(s)
        return s

    def dma(self, engine, stream, emit, after=()):
        s = self.step(engine, emit, after)
        s.stream = stream
        stream.count += 16
        return Landed(stream, stream.count)

    def number(self):
        for name, steps in self.lists.items():
            n = 0
            for s in steps:
                if s.signals:
                    n += 1
                    s.value = n

    def play(self, name, eng):
        seen = {}
        for s in self.lists[name]:
            need = {}
            for a in s.after:
                if isinstance(a, Step):
                    sem, value = self.sems[a.engine], a.value
                else:
                    sem, value = a.stream.sem, a.value
                key = id(sem)
                if value > seen.get(key, 0) and value > need.get(key, (None, 0))[1]:
                    need[key] = (sem, value)
            for key, (sem, value) in need.items():
                eng.wait_ge(sem, value)
                seen[key] = value
            inst = s.emit(eng)
            if hasattr(s, "stream"):
                inst.then_inc(s.stream.sem, 16)
            elif s.signals:
                inst.then_inc(self.sems[name], 1)


class Ring:

    def __init__(self, ids):
        self.free = [(i, []) for i in ids]

    def take(self):
        return self.free.pop(0)

    def leave(self, i, steps):
        self.free.append((i, list(steps)))

    def lend(self, i):
        at = next(n for n, f in enumerate(self.free) if f[0] == i)
        return self.free.pop(at)[1]


def interleave(tasks, width):
    tasks, active = list(tasks), []
    while tasks or active:
        while tasks and len(active) < width:
            active.append(tasks.pop(0))
        for t in list(active):
            try:
                next(t)
            except StopIteration:
                active.remove(t)


def finish_task(task):
    while True:
        try:
            next(task)
        except StopIteration as end:
            return end.value


def build(nc, a, out):
    ctx = ExitStack()
    with ctx:
        def sb(name, shape, dt=F32):
            return ctx.enter_context(nc.sbuf_tensor(name, shape, dt))

        def new_sem(name):
            return ctx.enter_context(nc.semaphore(name))

        q = Queues(nc, new_sem)

        def pe(emit, after=()):
            return q.step("tensor", emit, after)

        def dve(emit, after=()):
            return q.step("vector", emit, after)

        def act(emit, after=()):
            return q.step("scalar", emit, after)

        def pool(emit, after=()):
            return q.step("gpsimd", emit, after)

        def mm(o, l, r, start=True, stop=True, after=(), skip=False):
            return pe(lambda e: e.matmul(o, l, r, start=start, stop=stop, skip_group_check=skip), after)

        def stream(name):
            return Stream(new_sem(name))

        def load(st, dst, src, after=(), engine="sync"):
            return q.dma(engine, st, lambda e: e.dma_start(dst, src), after)

        x = sb("x", [P, NT, C])
        hT = sb("hT", [P, TOK])
        hT3 = hT[:, :].rearrange("p (t c) -> p t c", c=C)
        big1 = sb("big1", [P, NT * (C + HID)])
        VAW = HEADS * (HD + 1) + P // 4 - (HD + 1)
        big2 = sb("big2", [P, NT * VAW])
        tmp = sb("tmp", [P, 8, CHUNK])
        gb_tok = sb("gb_tok", [P, B, C])
        ew1 = sb("ew1", [P, NE, FF])
        ew2 = sb("ew2", [P, NE, FC, C])
        QR = 4
        q_stack = [sb(f"q_stack{i}", [P, 4, S], F32R) for i in range(QR)]
        k_stack = [sb(f"k_stack{i}", [P, 4, S], F32R) for i in range(QR)]
        parts = [sb(f"parts{i}", [P, CHUNK], F32R) for i in range(4)]
        ident = sb("ident", [P, P])
        ident_b = sb("ident_b", [P, P], BF16)
        mask_qk = sb("mask_qk", [P, 4, P], BF16)
        mask_kq = sb("mask_kq", [P, 4, P], BF16)
        before = sb("before", [P, P], BF16)
        ones_b = sb("ones_b", [P, P], BF16)
        const = big2[:, 0:CHUNK]
        psum = ctx.enter_context(nc.psum_tensor("psum", [P, 8, CHUNK], F32))

        def bank(i, n=CHUNK):
            return psum[:, i, 0:n]

        psum_ring = Ring(range(8))
        tmp_ring = Ring(range(8))

        def T(k):
            return tmp[:, k, :] if k < 8 else big2[:, (k - 8) * CHUNK:(k - 7) * CHUNK]


        q_parts = nc.dram_tensor("q_parts", [P, 4, TOK], F32, kind="Internal").ap()
        k_parts = nc.dram_tensor("k_parts", [P, 4, TOK], F32, kind="Internal").ap()
        routed = nc.dram_tensor("routed", [SLOTS, ROW], F32, kind="Internal").ap()
        answers = nc.dram_tensor("answers", [TOPK * TOK, C], F32, kind="Internal").ap()

        s_mod, s_w, s_col, s_rowp, s_ew = (stream(n) for n in ("mod", "weights", "cols", "rows", "experts"))
        s_x = [stream(f"x{i}") for i in range(4)]
        wmod = big1[:, 0:2 * MOD * C].rearrange("p (l n) -> p l n", l=2)
        for l in range(2):
            mod_in = load(s_mod, wmod[:, l, :], a[f"L{l}_wmod"])
        xd = a["L0_attn_x"].rearrange("b (t p) c -> p (b t) c", p=P)
        x_in = [load(s_x[i], x[:, 8 * i:8 * i + 8, :], xd[:, 8 * i:8 * i + 8, :]) for i in range(4)]

        wqk = sb("wqk", [P, 2, C])
        wvd = sb("wvd", [P, C + HID])
        wo = sb("wo", [P, C])
        fw = sb("fw", [P, 4, C])
        wg = sb("wg", [P, NE])
        w_t = sb("w_t", [P, 5, C])
        wr = sb("wr", [P, NE])
        load(s_w, wqk[:, 0, :], a["L0_attn_Wq"])
        load(s_w, wqk[:, 1, :], a["L0_attn_Wk"])
        load(s_w, wvd[:, 0:C], a["L0_attn_Wv"])
        load(s_w, wvd[:, C:C + HID], a["L0_attn_dp_w1"])
        load(s_w, wo[:, :], a["L0_attn_Wo"])
        for i, n in enumerate("qkvo"):
            load(s_w, fw[:, i, :], a[f"L0_ffn_W{n}"])
        load(s_w, wg[:, :], a["L0_ffn_Wg"])
        w_in = load(s_w, wr[:, :], a["L1_ffn_w_router"])

        COLS = {}
        n_cols = 0
        for name, n in (("L0_c", B), ("L1_c", B),
                        ("L0_attn_bq", 1), ("L0_attn_bk", 1), ("L0_attn_bo", 1), ("L0_ffn_bq", 1),
                        ("L0_ffn_bk", 1), ("L0_ffn_bo", 1), ("L1_attn_p1_b", 1), ("L1_attn_p2_b", 1),
                        ("L1_attn_qkv_b", 3), ("L0_ffn_b1", NE * FC)):
            COLS[name] = n_cols
            n_cols += n
        cols = sb("cols", [P, n_cols])
        col_rows = sb("col_rows", [n_cols, P])
        for name, at in COLS.items():
            v = a[name]
            if len(v.shape) == 2:
                v = v.rearrange("e f -> (e f)")
            n = v.shape[0] // P
            cols_loaded = load(s_col, col_rows[at:at + n, :], v.rearrange("(n p) -> n p", p=P))

        def col(name, i=0):
            return cols[:, COLS[name] + i:COLS[name] + i + 1]

        ROWS = {}
        n_rows = 0
        for name, n in (("L0_attn_bv", C), ("L0_attn_dp_b1", HID), ("L0_attn_ln_g", HID), ("L0_attn_ln_b", HID),
                        ("L0_attn_dp_w2", HID), ("L0_attn_dp_b2", 1), ("L0_attn_g_w1", GW), ("L0_attn_g_b1", GW),
                        ("L0_attn_g_w2", GW), ("L0_attn_g_b2", 1), ("L0_ffn_bv", C), ("L0_ffn_bg", NE),
                        ("L1_attn_qkv_b", 3 * C), ("L1_attn_kn_g", HD), ("L1_attn_vn_g", HD),
                        ("L1_attn_kn_b", HD), ("L1_attn_vn_b", HD), ("L1_ffn_bias", C)):
            ROWS[name] = (n_rows, n)
            n_rows += n
        rows = sb("rows", [P, n_rows])
        for name, (at, n) in ROWS.items():
            v = a[name]
            if len(v.shape) == 2:
                v = v.rearrange("a b -> (a b)")
            if len(v.shape) == 3:
                v = v.rearrange("a b c -> (a b c)")
            rows_in = load(s_rowp, rows[:, at:at + n], v.unsqueeze(0).to_broadcast([P, n]))

        def row(name):
            at, n = ROWS[name]
            return rows[:, at:at + n]

        b2 = sb("b2", [NE, C])
        load(s_ew, b2[:, :], a["L0_ffn_b2"])
        load(s_ew, ew1[:, :, :], a["L0_ffn_W1"].rearrange("e p f -> p e f"))
        ew_in = load(s_ew, ew2[:, :, :, :], a["L0_ffn_W2"].rearrange("e (k p) c -> p e k c", p=P))

        def select(t, pattern, mult, base, fill, cmp, after):
            return pool(lambda e: e.affine_select(out=t, in_=t, pattern=pattern, compare_op=cmp, fill=fill,
                                                  base=base, channel_multiplier=mult), after)

        z1 = pool(lambda e: e.memset(ident[:, :], 0.0))
        identity = select(ident[:, :], [[-1, P]], 1, 0, 1.0, ALU.not_equal, [z1])
        z2 = pool(lambda e: e.memset(ident_b[:, :], 0.0))
        identity_b = select(ident_b[:, :], [[-1, P]], 1, 0, 1.0, ALU.not_equal, [z2])
        z3 = pool(lambda e: e.memset(mask_qk[:, :, :], 0.0))
        select(mask_qk[:, :, :], [[0, 4], [-1, P]], 1, 0, MASKED, ALU.is_ge, [z3])
        z4 = pool(lambda e: e.memset(mask_kq[:, :, :], 0.0))
        masks = select(mask_kq[:, :, :], [[0, 4], [1, P]], -1, 0, MASKED, ALU.is_ge, [z4])
        z5 = pool(lambda e: e.memset(before[:, :], 1.0))
        select(before[:, :], [[1, P]], -1, -1, 0.0, ALU.is_ge, [z5])
        counters = pool(lambda e: e.memset(ones_b[:, :], 1.0))

        col_free = psum_ring.take()[1]
        turned = pe(lambda e: e.transpose(psum[:, 0, 0:n_cols], col_rows[:, :],
                                          ident[0:n_cols, 0:n_cols]), [cols_loaded, identity] + col_free)
        cols_in = dve(lambda e: e.tensor_copy(cols[:, :], psum[:, 0, 0:n_cols]), [turned])
        psum_ring.leave(0, [cols_in])
        cT = cols[:, 0:2 * B].rearrange("p (l b) -> p l b", l=2)

        zero512 = pool(lambda e: e.memset(const, 0.0))
        s_fill = stream("fill")
        for n in range(NCH):
            q_fill = load(s_fill, q_parts[:, 3, n * CHUNK:(n + 1) * CHUNK], const, [zero512])
        answers_v = answers.rearrange("(n p) c -> p n c", p=P)
        for n in range(TOPK * TOK // P // CT):
            answers_zero = load(s_fill, answers_v[:, n * CT:(n + 1) * CT, :],
                                const.rearrange("p (n c) -> p n c", c=C), [zero512])
        neg_rows = big2[:, CHUNK:2 * CHUNK]
        n1 = pool(lambda e: e.memset(neg_rows, 0.0))
        for i in range(P // HD):
            n1 = select(neg_rows, [[0, CHUNK]], 1, -HD * i, -1.0, ALU.not_equal, [n1])
        for n in range(NCH):
            k_fill = load(s_fill, k_parts[:, 3, n * CHUNK:(n + 1) * CHUNK], neg_rows, [n1])
        empty_row = sb("empty_row", [P, ROW])
        e1 = pool(lambda e: e.memset(empty_row[:, :], 0.0))
        e2 = pool(lambda e: e.memset(empty_row[:, C:C + 1], float(TOPK * TOK)), [e1])
        for n in range(SLOTS // P):
            routed_empty = load(s_fill, routed[n * P:(n + 1) * P, :], empty_row[:, :], [e2])

        sil = sb("sil", [P, 2, B])
        silu = act(lambda e: e.activation(sil[:, :, :], cT, ACT.Silu), [cols_in])
        modT = sb("modT", [P, 2, MOD, B])
        mod_ready = []
        for l in range(2):
            i, free = psum_ring.take()
            for g in range(MOD):
                last = mm(psum[:, i, g * B:(g + 1) * B], wmod[:, l, g * C:(g + 1) * C], sil[:, l, :],
                          after=[silu, mod_in] + free)
            src = psum[:, i, 0:MOD * B].rearrange("p (g b) -> p g b", b=B)
            cp = dve(lambda e, l=l, s=src: e.tensor_copy(modT[:, l, :, :], s), [last])
            psum_ring.leave(i, [cp])
            for g in (1, 4):
                m = modT[:, l, g, :]
                last = dve(lambda e, m=m: e.tensor_scalar(m, m, 1.0, None, ALU.add), [cp])
            mod_ready.append(last)
            for g in (2, 5):
                m = modT[:, l, g, :]
                sgn = sb(f"sgn{l}{g}", [P, B])
                mag = sb(f"mag{l}{g}", [P, B])
                s1 = dve(lambda e, m=m, t=sgn: e.tensor_scalar(t[:, :], m, 0.0, 2.0, ALU.is_ge, ALU.mult), [cp])
                s2 = dve(lambda e, m=m, t=mag: e.scalar_tensor_tensor(t[:, :], m, -1.0, m, ALU.mult, ALU.max), [cp])
                s2 = dve(lambda e, t=mag: e.tensor_scalar(t[:, :], t[:, :], 0.25, None, ALU.max), [s2])
                last = dve(lambda e, m=m, s=sgn, t=mag: e.scalar_tensor_tensor(
                    m, s[:, :], -1.0, t[:, :], ALU.add, ALU.mult), [s1, s2])
            mod_ready.append(last)
        def spread_gates(l, gb_free):
            for n in range(B // 4):
                i, free = psum_ring.take()
                for k in range(4):
                    b = 4 * n + k
                    t, tfree = tmp_ring.take()
                    rep = dve(lambda e, t=t, b=b: e.tensor_copy(
                        T(t)[:, 0:P], modT[:, l, 5, b:b + 1].to_broadcast([P, P])), mod_ready + tfree)
                    last = mm(psum[:, i, k * C:(k + 1) * C], T(t)[:, 0:P], ident[:, :],
                              after=[rep, identity] + free)
                    tmp_ring.leave(t, [last])
                cp = act(lambda e, i=i, n=n: e.copy(
                    gb_tok[:, 4 * n:4 * n + 4, :].rearrange("p b c -> p (b c)"), bank(i)), [last] + gb_free)
                psum_ring.leave(i, [cp])
            return cp

        stats = sb("stats", [P, NT, 6])
        mv = sb("mv", [P, NT, 2])
        rstd = sb("rstd", [P, NT])

        LG = 8
        ln_tmp = sb("ln_tmp", [P, NT])

        def rsqrt(y, v, t, ready):
            s1 = dve(lambda e: e.tensor_scalar(t.bitcast(I32), v.bitcast(I32), 1, None, ALU.arith_shift_right),
                     ready)
            yield
            s2 = dve(lambda e: e.tensor_scalar(y.bitcast(I32), t.bitcast(I32), -1.0, float(0x5F3759DF),
                                               ALU.mult, ALU.add), [s1])
            for _ in range(3):
                yield
                s1 = dve(lambda e: e.scalar_tensor_tensor(t, y, -0.5, y, ALU.mult, ALU.mult), [s2])
                yield
                s1 = dve(lambda e: e.tensor_tensor(t, t, v, ALU.mult), [s1])
                yield
                s2 = dve(lambda e: e.scalar_tensor_tensor(y, t, 1.5, y, ALU.add, ALU.mult), [s1])
            return s2

        rstd_ready = {}

        def statistics(kind, g, x_ready):
            t0 = LG * g
            for t in range(t0, t0 + LG):
                st = dve(lambda e, t=t: e.bn_stats(stats[:, t, :], x[:, t, :]), x_ready(t // TPB))
                if t % 2:
                    yield
            for t in range(t0, t0 + LG):
                ag = dve(lambda e, t=t: e.bn_aggr(mv[:, t, :], stats[:, t, :]), [st])
            yield
            v = mv[:, t0:t0 + LG, 1]
            ev = dve(lambda e: e.tensor_scalar(v, v, EPS, None, ALU.add), [ag])
            rstd_ready[kind, g] = yield from rsqrt(rstd[:, t0:t0 + LG], v, ln_tmp[:, t0:t0 + LG], [ev])

        def with_statistics(kind, tasks, x_ready):
            per = LG // TPB
            out = [statistics(kind, 0, x_ready)]
            for b in range(B):
                if b % per == 0 and b // per + 1 < B // per:
                    out.append(statistics(kind, b // per + 1, x_ready))
                out.append(tasks(b))
            return out

        def normalise(b, kind):
            l, second = kind
            t0 = TPB * b
            while (kind, t0 // LG) not in rstd_ready:
                yield
            rs = rstd_ready[kind, t0 // LG]
            i, free = psum_ring.take()
            k, tfree = tmp_ring.take()
            for n in range(TPB):
                t = t0 + n
                z = T(k)[:, n * C:(n + 1) * C]
                zs = dve(lambda e, z=z, t=t: e.tensor_scalar(z, x[:, t, :], mv[:, t, 0:1], rstd[:, t:t + 1],
                                                             ALU.subtract, ALU.mult), [rs] + tfree)
                tr = pe(lambda e, z=z, n=n, i=i: e.transpose(psum[:, i, n * P:(n + 1) * P], z, ident[:, :]),
                        [zs, identity] + free)
            tmp_ring.leave(k, [tr])
            g = 3 * second
            w = act(lambda e: e.activation(hT[:, b * S:(b + 1) * S], psum[:, i, 0:S], ACT.Identity,
                                           bias=modT[:, l, g, b:b + 1], scale=modT[:, l, g + 1, b:b + 1]),
                    [tr] + mod_ready)
            psum_ring.leave(i, [w])
            return w

        hready = {}
        VW = C + HID
        vd = big1[:, :].rearrange("p (t n) -> p t n", n=VW)
        vd_in = {}
        bias_vd = rows[:, ROWS["L0_attn_bv"][0]:ROWS["L0_attn_bv"][0] + VW]

        def values(b):
            hready[b] = yield from normalise(b, (0, 0))
            yield
            i, free = psum_ring.take()
            for n in range(TPB):
                t = TPB * b + n
                last = mm(psum[:, i, n * VW:(n + 1) * VW], hT[:, t * P:(t + 1) * P], wvd[:, :],
                          after=[hready[b], w_in] + free)
            src = psum[:, i, 0:TPB * VW].rearrange("p (t n) -> p t n", n=VW)
            vd_in[b] = dve(lambda e: e.tensor_tensor(
                vd[:, TPB * b:TPB * (b + 1), :], src, bias_vd.unsqueeze(1).to_broadcast([P, TPB, VW]), ALU.add),
                [last, rows_in])
            psum_ring.leave(i, [vd_in[b]])

        interleave(with_statistics((0, 0), values, lambda b: [x_in[b // 4]]), 4)

        s_part = [stream(f"part{i}") for i in range(4)]
        part_sent = [[] for _ in range(4)]
        qk_stored = {}
        for n in range(NCH):
            cs = slice(n * CHUNK, (n + 1) * CHUNK)
            for w, name, dst in ((0, "L0_attn_bq", q_parts), (1, "L0_attn_bk", k_parts)):
                i, free = psum_ring.take()
                last = mm(bank(i), wqk[:, w, :], hT[:, cs], after=[hready[2 * n + 1], w_in] + free)
                k, tfree = tmp_ring.take()
                full = act(lambda e, k=k, i=i, name=name: e.activation(
                    T(k)[:, :], bank(i), ACT.Identity, bias=col(name)), [last, cols_in] + tfree)
                psum_ring.leave(i, [full])
                hi, lo = parts[2 * w], parts[2 * w + 1]
                h = pool(lambda e, hi=hi, k=k: e.tensor_copy(hi[:, :], T(k)[:, :]), [full] + part_sent[2 * w])
                l = dve(lambda e, lo=lo, hi=hi, k=k: e.tensor_tensor(
                    lo[:, :], T(k)[:, :], hi[:, :].bitcast(F32), ALU.subtract), [full, h] + part_sent[2 * w + 1])
                tmp_ring.leave(k, [l])
                hi_at, lo_at = ((0, 2), 1) if w == 0 else ((0, 1), 2)
                for p in hi_at:
                    d = load(s_part[2 * w], dst[:, p, cs], hi[:, :].bitcast(F32), [h])
                part_sent[2 * w] = [d, l]
                d2 = load(s_part[2 * w + 1], dst[:, lo_at, cs], lo[:, :].bitcast(F32), [l])
                part_sent[2 * w + 1] = [d2]
                qk_stored[(n, w)] = [d, d2]

        va_flat = big2[:, :].rearrange("p (t n) -> p t n", n=VAW)
        va = va_flat[:, :, 0:HEADS * (HD + 1)].rearrange("p t (h d) -> p t h d", d=HD + 1)
        va_pad = pool(lambda e: e.memset(va_flat[:, :, HEADS * (HD + 1):VAW], 0.0), [q_fill, k_fill, answers_zero])
        gate = sb("gate", [P, NT])
        drift = sb("drift", [P, NT])
        dst_ = sb("dstats", [P, NT, 6])
        dmv = sb("dmv", [P, NT, 2])
        drs = sb("drs", [P, NT])
        for t in range(NT):
            st = dve(lambda e, t=t: e.bn_stats(dst_[:, t, :], vd[:, t, C:VW]), [vd_in[t // TPB]])
            ag = dve(lambda e, t=t: e.bn_aggr(dmv[:, t, :], dst_[:, t, :]), [st])
        ev = dve(lambda e: e.tensor_scalar(dmv[:, :, 1], dmv[:, :, 1], EPS, None, ALU.add), [ag])
        rs = finish_task(rsqrt(drs[:, :], dmv[:, :, 1], ln_tmp[:, :], [ev]))
        GT = CHUNK // HID
        gated = {}
        for n in range(NT // GT):
            ts = slice(n * GT, (n + 1) * GT)
            k, tfree = tmp_ring.take()
            t3 = T(k)[:, :].rearrange("p (t n) -> p t n", n=HID)
            for m in range(GT):
                t = n * GT + m
                last = dve(lambda e, t=t, m=m, t3=t3: e.tensor_scalar(
                    t3[:, m, :], vd[:, t, C:VW], dmv[:, t, 0:1], drs[:, t:t + 1], ALU.subtract, ALU.mult),
                    [rs] + tfree)

            def rep(name, w=HID):
                return row(name).unsqueeze(1).to_broadcast([P, GT, w])

            s1 = pool(lambda e, t3=t3, r=rep("L0_attn_ln_g"): e.tensor_tensor(t3, t3, r, ALU.mult), [last])
            s2 = pool(lambda e, t3=t3, r=rep("L0_attn_ln_b"): e.tensor_tensor(t3, t3, r, ALU.add), [s1])
            s3 = act(lambda e, t3=t3: e.activation(t3, t3, ACT.Gelu), [s2])
            s4 = pool(lambda e, t3=t3, r=rep("L0_attn_dp_w2"): e.tensor_tensor(t3, t3, r, ALU.mult), [s3])
            s5 = dve(lambda e, t3=t3, ts=ts: e.tensor_reduce(drift[:, ts], t3, X_AXIS, ALU.add), [s4])
            s6 = dve(lambda e, ts=ts: e.tensor_scalar(drift[:, ts], drift[:, ts], row("L0_attn_dp_b2"), None,
                                                      ALU.add), [s5])
            g3 = T(k)[:, 0:GT * GW].rearrange("p (t n) -> p t n", n=GW)
            s7 = dve(lambda e, g3=g3, ts=ts, r=rep("L0_attn_g_w1", GW): e.tensor_tensor(
                g3, drift[:, ts].unsqueeze(2).to_broadcast([P, GT, GW]), r, ALU.mult), [s6])
            s8 = dve(lambda e, g3=g3, r=rep("L0_attn_g_b1", GW): e.tensor_tensor(g3, g3, r, ALU.add), [s7])
            s9 = act(lambda e, g3=g3: e.activation(g3, g3, ACT.Gelu), [s8])
            s10 = dve(lambda e, g3=g3, r=rep("L0_attn_g_w2", GW): e.tensor_tensor(g3, g3, r, ALU.mult), [s9])
            s11 = dve(lambda e, g3=g3, ts=ts: e.tensor_reduce(gate[:, ts], g3, X_AXIS, ALU.add), [s10])
            tmp_ring.leave(k, [s11])
            s12 = act(lambda e, ts=ts: e.activation(gate[:, ts], gate[:, ts], ACT.Tanh,
                                                    bias=row("L0_attn_g_b2")), [s11])
            for m in range(GT):
                t = n * GT + m
                o = pool(lambda e, t=t: e.memset(va[:, t, :, HD:HD + 1], 1.0), [q_fill, k_fill, answers_zero])
                v = pool(lambda e, t=t: e.tensor_scalar(
                    va[:, t, :, 0:HD], vd[:, t, 0:C].rearrange("p (h d) -> p h d", d=HD), gate[:, t:t + 1], None,
                    ALU.mult), [s12, o])
                gated[t] = v

        s_qs = [stream(f"qs{i}") for i in range(QR)]
        s_ks = [stream(f"ks{i}") for i in range(QR)]
        s_m = [stream(f"maxrow{i}") for i in range(QR)]
        stacked, stack_free = {}, [[] for _ in range(QR)]
        mrow_ready = {}
        q_src = q_parts.rearrange("(i r) a t -> (r a) i t", i=4)
        k_src = k_parts.rearrange("(i r) a t -> (r a) i t", i=4)

        def stack(b):
            r = b % QR
            ts = slice(b * S, (b + 1) * S)
            n = b * S // CHUNK
            dq = load(s_qs[r], q_stack[r][:, :, :].bitcast(F32), q_src[:, :, ts],
                      qk_stored[(n, 0)] + [q_fill, k_fill] + stack_free[r])
            dk = load(s_ks[r], k_stack[r][:, :, :].bitcast(F32), k_src[:, :, ts], qk_stored[(n, 1)] + [k_fill])
            stacked[b] = [dq, dk]

        pair = Ring([])
        for i in range(3):
            pair.leave(i, psum_ring.lend(2 * i) + psum_ring.lend(2 * i + 1))
        o_free = psum_ring.lend(6) + psum_ring.lend(7)
        p_ring = Ring([])
        for i in range(4):
            p_ring.leave(i, tmp_ring.lend(2 * i) + tmp_ring.lend(2 * i + 1))
        for i in range(4, 8):
            p_ring.leave(i, [gated[NT - 1]])

        def pair_of_tiles(i):
            if i < 4:
                return tmp[:, 2 * i:2 * i + 2, :]
            at = 2 * CHUNK * (i - 4)
            return big1[:, at:at + 2 * CHUNK].rearrange("p (j n) -> p j n", j=2)
        maxes = sb("maxes", [P, 2, TPB, 4, 4])
        m_hi = sb("m_hi", [HEADS, 2, S], F32R)
        max_in = {}

        def max_unit(b, u):
            r = b % QR
            s, free = pair.take()
            qb, jp = (0, u) if u < 2 else (1, (u - 2) % 2)
            width = P * (qb + 1)
            ii = range(4) if qb == 0 else range(2 * ((u - 2) // 2), 2 * ((u - 2) // 2) + 2)
            last = None
            for jl in range(2):
                out_m = bank(2 * s + jl).rearrange("p (g k) -> p g k", k=width)[:, :, width - P:width]
                mm(out_m, ident_b[:, :], mask_qk[:, 0:len(ii), :], start=True, stop=False,
                   after=[masks, identity_b] + free + stacked[b], skip=True)
            for n, i in enumerate(ii):
                for jl in range(2):
                    j = 2 * jp + jl
                    rows_ = slice(32 * j, 32 * j + 32)
                    last = mm(psum[:, 2 * s + jl, n * width:(n + 1) * width],
                              q_stack[r][rows_, i, qb * P:(qb + 1) * P], k_stack[r][rows_, i, 0:width],
                              start=False, stop=True, skip=True)
            src = psum[:, 2 * s:2 * s + 2, :].rearrange("p j (g k) -> p j g k", k=width)
            dst = maxes[:, b % 2, qb, ii[0]:ii[-1] + 1, 2 * jp:2 * jp + 2].rearrange("p i j -> p j i")
            red = dve(lambda e: e.tensor_reduce(dst, src, X_AXIS, ALU.max), [last])
            pair.leave(s, [red])
            max_in.setdefault(b, []).append(red)

        def max_rows(b):
            r = b % QR
            s, free = pair.take()
            for qb in range(TPB):
                src = maxes[:, b % 2, qb, :, :].rearrange("p i j -> p (i j)")
                tr = pe(lambda e, src=src, qb=qb: e.transpose(
                    psum[0:HEADS, 2 * s, qb * P:(qb + 1) * P], src, ident[:, :]), [max_in[b][-1]] + free)
            wait = mrow_ready.get(b - 2, [])
            cp = dve(lambda e: e.tensor_copy(m_hi[:, b % 2, :], psum[0:HEADS, 2 * s, 0:S]), [tr] + wait)
            pair.leave(s, [cp])
            for i in range(4):
                d = load(s_m[r], q_stack[r][3:P:32, i, :].bitcast(F32), m_hi[4 * i:4 * i + 4, b % 2, :].bitcast(F32),
                         [cp])
            mrow_ready[b] = [d]

        def exp_unit(b, u):
            r = b % QR
            s, free = pair.take()
            kb, jp = (0, u % 2) if u < 4 else (1, u - 4)
            width = P * (2 - kb)
            ii = range(2 * (u // 2), 2 * (u // 2) + 2) if kb == 0 else range(4)
            for jl in range(2):
                out_m = bank(2 * s + jl).rearrange("p (g k) -> p g k", k=width)[:, :, 0:P]
                mm(out_m, ident_b[:, :], mask_kq[:, 0:len(ii), :], start=True, stop=False,
                   after=free + mrow_ready[b], skip=True)
            for n, i in enumerate(ii):
                for jl in range(2):
                    j = 2 * jp + jl
                    rows_ = slice(32 * j, 32 * j + 32)
                    last = mm(psum[:, 2 * s + jl, n * width:(n + 1) * width],
                              k_stack[r][rows_, i, kb * P:(kb + 1) * P], q_stack[r][rows_, i, kb * P:S],
                              start=False, stop=True, skip=True)
            pi, pfree = p_ring.take()
            dst = pair_of_tiles(pi)
            ex = act(lambda e: e.activation(dst, psum[:, 2 * s:2 * s + 2, :], ACT.Exp, scale=float(HD) ** -0.5),
                     [last] + pfree)
            pair.leave(s, [ex])
            return (b, u, kb, jp, list(ii), width, pi, ex, last)

        QUAD = P // 4

        def value_unit(unit):
            nonlocal o_free
            b, u, kb, jp, ii, width, pi, ex, _ = unit
            weights = pair_of_tiles(pi)
            for n, i in enumerate(ii):
                for jl in range(2):
                    c = 2 * jp + jl
                    at = (4 * i + c) * (HD + 1)
                    last = mm(psum[QUAD * c:QUAD * (c + 1), 6 + i // 2, (i % 2) * S + kb * P:(i % 2 + 1) * S],
                              va_flat[:, TPB * b + kb, at:at + QUAD], weights[:, jl, n * width:(n + 1) * width],
                              start=kb == 0 and i % 2 == 0, stop=True,
                              after=[ex, gated[TPB * b + kb], va_pad] + (o_free if u == 0 else []), skip=True)
            p_ring.leave(pi, [last])
            if u == 5:
                k, free = p_ring.take()
                cp = act(lambda e: e.copy(pair_of_tiles(k), psum[:, 6:8, :]), [last] + free)
                o_free = [cp]
                turn[b] = (k, cp)
            return last

        turn = {}

        def turn_batch(b):
            k, cp = turn.pop(b)
            s, free = pair.take()
            for i in range(4):
                for qb in range(TPB):
                    at = (i % 2) * S + qb * P
                    tr = pe(lambda e, i=i, qb=qb, at=at: e.transpose(
                        psum[:, 2 * s + qb, i * P:(i + 1) * P], pair_of_tiles(k)[:, i // 2, at:at + P], ident[:, :]),
                        [cp] + free)
            p_ring.leave(k, [tr])
            o = psum[:, 2 * s:2 * s + 2, :].rearrange("p t (h d) -> p t h d", d=QUAD)
            rc = dve(lambda e: e.reciprocal(recip[:, b % 2, :, :], o[:, :, :, HD]), [tr])
            dst = hT3[:, TPB * b:TPB * (b + 1), :].rearrange("p t (h d) -> p t h d", d=HD)
            for qb in range(TPB):
                nm = dve(lambda e, qb=qb: e.tensor_tensor(
                    dst[:, qb, :, :], o[:, qb, :, 0:HD],
                    recip[:, b % 2, qb, :].unsqueeze(2).to_broadcast([P, HEADS, HD]), ALU.mult), [rc])
            pair.leave(s, [nm])
            attn_out[b] = nm

        recip = sb("recip", [P, 2, TPB, HEADS])
        attn_out = {}
        LEAD = 9
        for b in range(min(QR, B)):
            stack(b)
        m_next = 0

        def advance_max():
            nonlocal m_next
            if m_next < 6 * B:
                max_unit(m_next // 6, m_next % 6)
                m_next += 1

        for _ in range(LEAD):
            advance_max()
        max_rows(0)
        rows_done = 1
        DELAY = 2
        waiting = []
        for e in range(6 * B):
            b, u = divmod(e, 6)
            advance_max()
            if rows_done < B and (m_next >= 6 * (rows_done + 1) + 1 or m_next == 6 * B):
                max_rows(rows_done)
                rows_done += 1
            for done in list(turn):
                turn_batch(done)
            if len(waiting) == DELAY:
                unit = waiting.pop(0)
                lv = value_unit(unit)
            waiting.append(exp_unit(b, u))
            if u == 5 and b + QR < B:
                stack_free[b % QR] = [waiting[-1][-1]]
                stack(b + QR)
        for unit in waiting:
            va_read = value_unit(unit)
        turn_batch(B - 1)
        for i in range(3):
            free = pair.lend(i)
            for k in (2 * i, 2 * i + 1):
                psum_ring.leave(k, free)
        for k in (6, 7):
            psum_ring.leave(k, o_free)
        for i in range(4):
            free = p_ring.lend(i)
            for k in (2 * i, 2 * i + 1):
                tmp_ring.leave(k, free)
        w_raw = big1[:, TOK:TOK + 5 * C].rearrange("p (g c) -> p g c", c=C)
        s_raw = stream("weights1")
        load(s_raw, w_raw[:, 0:3, :], a["L1_attn_qkv_w"].rearrange("(g p) c -> p g c", p=P), [va_read])
        load(s_raw, w_raw[:, 3, :], a["L1_attn_p1_w"])
        w_raw_in = load(s_raw, w_raw[:, 4, :], a["L1_attn_p2_w"])

        EXTRA = range(8, 16)
        for k in EXTRA:
            tmp_ring.leave(k, [va_read])
        LANES = 5

        small = sb("small", [P, 2, MOD, B])

        def gated_bias(l, g, name, slot):
            return dve(lambda e: e.tensor_scalar(small[:, l, slot, :], modT[:, l, g, :], col(name), None, ALU.mult),
                       mod_ready + [cols_in])

        bo_ready = gated_bias(0, 2, "L0_attn_bo", 0)

        def add_back(n, src_tmp, ready):
            i, free = psum_ring.take()
            for k in range(CT):
                tr = pe(lambda e, k=k, i=i: e.transpose(psum[:, i, k * P:(k + 1) * P],
                                                       src_tmp[:, k * P:(k + 1) * P], ident[:, :]), ready + free)
            xs = x[:, CT * n:CT * (n + 1), :]
            ad = dve(lambda e, i=i: e.tensor_tensor(xs, xs, bank(i).rearrange("p (t c) -> p t c", c=C), ALU.add),
                     [tr])
            psum_ring.leave(i, [ad])
            return tr, ad

        x1 = {}
        for n in range(NCH):
            i, free = psum_ring.take()
            for k in range(CT):
                t = CT * n + k
                tr = pe(lambda e, k=k, t=t, i=i: e.transpose(psum[:, i, k * P:(k + 1) * P], hT3[:, t, :],
                                                            ident[:, :]), [attn_out[t // TPB]] + free)
            k, tfree = tmp_ring.take()
            cp = act(lambda e, k=k, i=i: e.copy(T(k)[:, :], bank(i)), [tr] + tfree)
            psum_ring.leave(i, [cp])
            j, free = psum_ring.take()
            pr = mm(bank(j), wo[:, :], T(k)[:, :], after=[cp] + free)
            k2, tfree2 = tmp_ring.take()
            for h in range(2):
                b = 2 * n + h
                sc = act(lambda e, k2=k2, j=j, b=b, h=h: e.activation(
                    T(k2)[:, h * S:(h + 1) * S], psum[:, j, h * S:(h + 1) * S], ACT.Identity,
                    bias=small[:, 0, 0, b:b + 1], scale=modT[:, 0, 2, b:b + 1]), [pr, bo_ready] + tfree2)
            tmp_ring.leave(k, [pr])
            psum_ring.leave(j, [sc])
            tr, ad = add_back(n, T(k2)[:, :], [sc])
            tmp_ring.leave(k2, [tr])
            x1[2 * n] = x1[2 * n + 1] = ad

        xpT = big1[:, 0:TOK]
        fvec = sb("fvec", [P, LANES, 4, TPB])
        xp_ready = {}
        FS = 1.0 / float(np.sqrt(C))
        att_done = {}
        def mixture_attention(b):
            bs = slice(b * S, (b + 1) * S)
            hr = yield from normalise(b, (0, 1))
            yield
            i, free = psum_ring.take()
            for w in range(2):
                last = mm(psum[:, i, w * S:(w + 1) * S], fw[:, w, :], hT[:, bs], after=[hr] + free)
            kq, f1 = tmp_ring.take()
            act(lambda e, kq=kq, i=i: e.activation(T(kq)[:, 0:S], psum[:, i, 0:S], ACT.Identity,
                                                   bias=col("L0_ffn_bq")), [last] + f1)
            qk = act(lambda e, kq=kq, i=i: e.activation(T(kq)[:, S:2 * S], psum[:, i, S:2 * S], ACT.Identity,
                                                        bias=col("L0_ffn_bk")))
            psum_ring.leave(i, [qk])
            yield
            i, free = psum_ring.take()
            for n in range(TPB):
                last = mm(psum[:, i, n * C:(n + 1) * C], hT[:, b * S + n * P:b * S + (n + 1) * P], fw[:, 2, :],
                          after=[hr] + free)
            kv, f2 = tmp_ring.take()
            vt = T(kv)[:, 0:TPB * C].rearrange("p (t c) -> p t c", c=C)
            yield
            vr = dve(lambda e, vt=vt, i=i: e.tensor_tensor(
                vt, psum[:, i, 0:TPB * C].rearrange("p (t c) -> p t c", c=C),
                row("L0_ffn_bv").unsqueeze(1).to_broadcast([P, TPB, C]), ALU.add), [last] + f2)
            psum_ring.leave(i, [vr])
            yield
            i, free = psum_ring.take()
            for n in range(TPB):
                last = mm(psum[:, i, n * S:(n + 1) * S], T(kq)[:, n * P:(n + 1) * P], T(kq)[:, S:2 * S],
                          after=[qk] + free)
            tmp_ring.leave(kq, [last])
            fv = fvec[:, b % LANES, :, :]
            yield
            mx = dve(lambda e, fv=fv, i=i: e.tensor_reduce(
                fv[:, 0, :], bank(i).rearrange("p (t k) -> p t k", k=S), X_AXIS, ALU.max), [last])
            yield
            ng = dve(lambda e, fv=fv: e.tensor_scalar(fv[:, 1, :], fv[:, 0, :], -FS, None, ALU.mult), [mx])
            kp, f3 = tmp_ring.take()
            for n in range(TPB):
                ex = act(lambda e, n=n, fv=fv, kp=kp, i=i: e.activation(
                    T(kp)[:, n * S:(n + 1) * S], psum[:, i, n * S:(n + 1) * S], ACT.Exp,
                    bias=fv[:, 1, n:n + 1], scale=FS, accum_out=fv[:, 2, n:n + 1]), [ng] + f3)
            psum_ring.leave(i, [ex])
            yield
            rc = dve(lambda e, fv=fv: e.reciprocal(fv[:, 3, :], fv[:, 2, :]), [ex])
            for n in range(TPB):
                sc = dve(lambda e, n=n, fv=fv, kp=kp: e.tensor_scalar(
                    T(kp)[:, n * S:(n + 1) * S], T(kp)[:, n * S:(n + 1) * S], fv[:, 3, n:n + 1], None,
                    ALU.mult), [rc])
            yield
            i, free = psum_ring.take()
            for kb in range(TPB):
                for qb in range(TPB):
                    tr = pe(lambda e, kb=kb, qb=qb, kp=kp, i=i: e.transpose(
                        psum[:, i, kb * S + qb * P:kb * S + (qb + 1) * P],
                        T(kp)[:, qb * S + kb * P:qb * S + (kb + 1) * P], ident[:, :]), [sc] + free)
            tmp_ring.leave(kp, [tr])
            kt, f4 = tmp_ring.take()
            yield
            cp = act(lambda e, kt=kt, i=i: e.copy(T(kt)[:, :], bank(i)), [tr] + f4)
            psum_ring.leave(i, [cp])
            yield
            i, free = psum_ring.take()
            for kb in range(TPB):
                last = mm(psum[:, i, 0:S], vt[:, kb, :], T(kt)[:, kb * S:(kb + 1) * S], start=kb == 0,
                          stop=kb == TPB - 1, after=[cp, vr] + free)
            tmp_ring.leave(kt, [last])
            tmp_ring.leave(kv, [last])
            ka, f5 = tmp_ring.take()
            yield
            cp = act(lambda e, ka=ka, i=i: e.copy(T(ka)[:, 0:S], psum[:, i, 0:S]), [last] + f5)
            psum_ring.leave(i, [cp])
            yield
            i, free = psum_ring.take()
            last = mm(psum[:, i, 0:S], fw[:, 3, :], T(ka)[:, 0:S], after=[cp] + free)
            tmp_ring.leave(ka, [last])
            yield
            xp_ready[b] = dve(lambda e, bs=bs, i=i: e.scalar_tensor_tensor(
                xpT[:, bs], psum[:, i, 0:S], col("L0_ffn_bo"), hT[:, bs], ALU.add, ALU.add), [last])
            psum_ring.leave(i, [xp_ready[b]])

        interleave(with_statistics((0, 1), mixture_attention, lambda b: [x1[b]]), LANES)

        gates = sb("gates", [P, NT, NE])
        gmax = sb("gmax", [P, NT])
        i, free = psum_ring.take()
        for t in range(NT):
            last = mm(psum[:, i, t * NE:(t + 1) * NE], xpT[:, t * P:(t + 1) * P], wg[:, :],
                      after=[xp_ready[t // TPB]] + free)

        def softmax8(logits, src_i, last, bias):
            src = psum[:, src_i, 0:NT * NE].rearrange("p (t e) -> p t e", e=NE)
            if bias is not None:
                s1 = dve(lambda e: e.tensor_tensor(logits[:, :, :], src,
                                                   bias.unsqueeze(1).to_broadcast([P, NT, NE]), ALU.add), [last])
            else:
                s1 = dve(lambda e: e.tensor_copy(logits[:, :, :], src), [last])
            psum_ring.leave(src_i, [s1])
            wide = gmax[:, :].unsqueeze(2).to_broadcast([P, NT, NE])
            s2 = dve(lambda e: e.tensor_reduce(gmax[:, :], logits[:, :, :], X_AXIS, ALU.max), [s1])
            s3 = dve(lambda e: e.tensor_tensor(logits[:, :, :], logits[:, :, :], wide, ALU.subtract), [s2])
            s4 = act(lambda e: e.activation(logits[:, :, :], logits[:, :, :], ACT.Exp), [s3])
            s5 = dve(lambda e: e.tensor_reduce(gmax[:, :], logits[:, :, :], X_AXIS, ALU.add), [s4])
            s6 = dve(lambda e: e.reciprocal(gmax[:, :], gmax[:, :]), [s5])
            return dve(lambda e: e.tensor_tensor(logits[:, :, :], logits[:, :, :], wide, ALU.mult), [s6])

        gates_ready = softmax8(gates, i, last, row("L0_ffn_bg"))

        for n in range(NCH):
            k, tfree = tmp_ring.take()
            for h in range(2):
                b = 2 * n + h
                sc = pool(lambda e, k=k, b=b, h=h: e.tensor_scalar(
                    T(k)[:, h * S:(h + 1) * S], xpT[:, b * S:(b + 1) * S], modT[:, 0, 5, b:b + 1], None, ALU.mult),
                    [xp_ready[b]] + tfree)
            tr, ad = add_back(n, T(k)[:, :], [sc])
            tmp_ring.leave(k, [tr])
            x1[2 * n] = x1[2 * n + 1] = ad

        y = hT3
        gT = sb("gT", [NE, CHUNK])
        y_ready = {}
        for n in range(NCH):
            i, free = psum_ring.take()
            for k in range(CT):
                t = CT * n + k
                tr = pe(lambda e, k=k, t=t, i=i: e.transpose(psum[0:NE, i, k * P:(k + 1) * P], gates[:, t, :],
                                                            ident[:, :]), [gates_ready] + free)
            prev = [y_ready[CT * (n - 1)]] if n else []
            cp = act(lambda e, i=i: e.copy(gT[:, :], psum[0:NE, i, :]), [tr] + prev)
            psum_ring.leave(i, [cp])
            i, free = psum_ring.take()
            for k in range(CT):
                last = mm(psum[:, i, k * C:(k + 1) * C], gT[:, k * P:(k + 1) * P], b2[:, :], after=[cp, ew_in] + free)
            cp = act(lambda e, i=i, n=n: e.copy(hT[:, n * CHUNK:(n + 1) * CHUNK], bank(i)), [last])
            psum_ring.leave(i, [cp])
            for k in range(CT):
                y_ready[CT * n + k] = cp
        hid = big2[:, 0:2 * FC * CHUNK].rearrange("p (r f t) -> p r f t", r=2, f=FC)
        hid_ring = Ring([])
        for r in range(2):
            hid_ring.leave(r, [w for k in EXTRA[r * FC:(r + 1) * FC] for w in tmp_ring.lend(k)])

        def up(e_, n, src, src_ready, func):
            r, hfree = hid_ring.take()
            done = []
            for f in range(FC):
                i, free = psum_ring.take()
                last = mm(bank(i), ew1[:, e_, f * P:(f + 1) * P], src, after=[src_ready] + free + ew_ready)
                done.append(func(i, r, f, e_, last, hfree))
            return r, done

        def down(e_, r, done):
            i, free = psum_ring.take()
            for k in range(CT):
                for f in range(FC):
                    last = mm(psum[:, i, k * C:(k + 1) * C], hid[:, r, f, k * P:(k + 1) * P], ew2[:, e_, f, :],
                              start=f == 0, stop=f == FC - 1, after=done + free)
            hid_ring.leave(r, [last])
            return i, last

        def relu(i, r, f, e_, last, hfree):
            s = act(lambda e: e.activation(hid[:, r, f, :], bank(i), ACT.Relu,
                                           bias=col("L0_ffn_b1", e_ * FC + f)), [last] + hfree)
            psum_ring.leave(i, [s])
            return s

        ew_ready = [ew_in]

        def mix(n, e_, i, last):
            for k in range(CT):
                t = CT * n + k
                s = dve(lambda e, k=k, t=t: e.scalar_tensor_tensor(
                    y[:, t, :], psum[:, i, k * C:(k + 1) * C], gates[:, t, e_:e_ + 1], y[:, t, :], ALU.mult, ALU.add),
                    [last, y_ready[t]])
                y_ready[t] = s
            psum_ring.leave(i, [s])

        pending = None
        for n in range(NCH):
            for e_ in range(NE):
                r, done = up(e_, n, xpT[:, n * CHUNK:(n + 1) * CHUNK], xp_ready[2 * n + 1], relu)
                if pending:
                    pn, pe_, pr, pdone = pending
                    i, last = down(pe_, pr, pdone)
                    mix(pn, pe_, i, last)
                pending = (n, e_, r, done)
        pn, pe_, pr, pdone = pending
        i, last_l0 = down(pe_, pr, pdone)
        mix(pn, pe_, i, last_l0)

        s_ew2 = stream("experts1")
        load(s_ew2, ew1[:, :, :], a["L1_ffn_w1"].rearrange("e p f -> p e f"), [last_l0])
        ew1_in = load(s_ew2, ew2[:, :, :, :], a["L1_ffn_w2"].rearrange("e (k p) c -> p e k c", p=P))

        gates_tok = spread_gates(0, [])

        def add_gated(n, src, ready):
            for h in range(2):
                b = 2 * n + h
                ts = slice(TPB * b, TPB * (b + 1))
                k, tfree = tmp_ring.take()
                t3 = T(k)[:, 0:TPB * C].rearrange("p (t c) -> p t c", c=C)
                m = pool(lambda e, ts=ts, t3=t3, b=b: e.tensor_tensor(
                    t3, src[:, ts, :], gb_tok[:, b, :].unsqueeze(1).to_broadcast([P, TPB, C]), ALU.mult),
                    ready + tfree + [gates_tok])
                ad = dve(lambda e, ts=ts, t3=t3: e.tensor_tensor(x[:, ts, :], x[:, ts, :], t3, ALU.add),
                         [m, x1[b]])
                tmp_ring.leave(k, [ad])
                x1[b] = ad

        for n in range(NCH):
            add_gated(n, y, [y_ready[CT * n + CT - 1]])

        gates_tok = spread_gates(1, [x1[b] for b in range(B)])

        for r in range(2):
            free = hid_ring.lend(r)
            for k in EXTRA[r * FC:(r + 1) * FC]:
                tmp_ring.leave(k, free)

        for g in range(5):
            i, free = psum_ring.take()
            tr = pe(lambda e, g=g, i=i: e.transpose(psum[:, i, 0:C], w_raw[:, g, :], ident[:, :]), [w_raw_in] + free)
            wt = dve(lambda e, g=g, i=i: e.tensor_copy(w_t[:, g, :], psum[:, i, 0:C]), [tr])
            psum_ring.leave(i, [wt])
        G2 = 2 * HEADS
        cen = sb("cen", [P, G2])

        def centre(t, ready):
            t3 = t.rearrange("p (g d) -> p g d", d=HD)
            s1 = dve(lambda e: e.tensor_reduce(cen[:, :], t3, X_AXIS, ALU.add), ready)
            s2 = dve(lambda e: e.tensor_scalar(cen[:, :], cen[:, :], 1.0 / HD, None, ALU.mult), [s1])
            return dve(lambda e: e.tensor_tensor(t3, t3, cen[:, :].unsqueeze(2).to_broadcast([P, G2, HD]),
                                                 ALU.subtract), [s2])

        wkv = w_t[:, 1:3, :].rearrange("p g c -> p (g c)")
        wkv_ready = centre(wkv, [wt])
        bkv = rows[:, ROWS["L1_attn_qkv_b"][0] + C:ROWS["L1_attn_qkv_b"][0] + 3 * C]
        bkv_ready = centre(bkv, [wkv_ready])
        temp_blk = parts[3][:, 0:C].bitcast(F32)
        bias_blk = parts[3][:, C:2 * C].bitcast(F32)
        tcol = sb("tcol", [P, 1])
        s_blk = stream("blocks")
        z6 = pool(lambda e: e.memset(temp_blk[:, :], 1.0 / S))
        z7 = pool(lambda e: e.memset(bias_blk[:, :], 0.0))
        for h in range(HEADS):
            hs = slice(h * HD, (h + 1) * HD)
            load(s_blk, tcol[hs, :], a["L1_attn_temperature"][h, :, :].to_broadcast([HD, 1]))
            blk_in = load(s_blk, bias_blk[hs, hs], a["L1_attn_attn_bias"][h, :, :], [z7])
        t3 = temp_blk[:, :].rearrange("p (h d) -> p h d", d=HD)
        z8 = select(t3, [[-HD, HEADS], [0, HD]], 1, 0, 0.0, ALU.is_ge, [z6])
        z9 = select(t3, [[HD, HEADS], [0, HD]], -1, HD - 1, 0.0, ALU.is_ge, [z8])
        blk_ready = dve(lambda e: e.tensor_scalar(temp_blk[:, :], temp_blk[:, :], tcol[:, 0:1], None, ALU.mult),
                        [z9, blk_in])
        gam = sb("gam", [P, G2, HD])
        bet = sb("bet", [P, G2, HD])
        for half, nm in ((0, "kn"), (1, "vn")):
            for dst, wh in ((gam, "g"), (bet, "b")):
                affine = pool(lambda e, half=half, dst=dst, nm=nm, wh=wh: e.tensor_copy(
                    dst[:, half * HEADS:(half + 1) * HEADS, :],
                    row(f"L1_attn_{nm}_{wh}").unsqueeze(1).to_broadcast([P, HEADS, HD])), [rows_in])
        p2_ready = gated_bias(1, 2, "L1_attn_p2_b", 0)

        var, vrs, vt_ = (parts[k][:, 0:LANES * TPB * G2].bitcast(F32).rearrange("p (l g) -> p l g", l=LANES)
                         for k in range(3))
        def linear_attention(b):
            bs = slice(b * S, (b + 1) * S)
            hr = yield from normalise(b, (1, 0))
            yield
            i, free = psum_ring.take()
            last = mm(psum[:, i, 0:S], w_t[:, 0, :], hT[:, bs], after=[hr, wt] + free)
            kq, f1 = tmp_ring.take()
            yield
            qs = act(lambda e, kq=kq, i=i: e.activation(T(kq)[:, 0:S], psum[:, i, 0:S], ACT.Identity,
                                                        bias=col("L1_attn_qkv_b")), [last] + f1)
            psum_ring.leave(i, [qs])
            yield
            i, free = psum_ring.take()
            for n in range(TPB):
                last = mm(psum[:, i, n * 2 * C:(n + 1) * 2 * C], hT[:, b * S + n * P:b * S + (n + 1) * P], wkv,
                          after=[hr, wkv_ready] + free)
            kk, f2 = tmp_ring.take()
            t2 = T(kk)[:, :].rearrange("p (t n) -> p t n", n=2 * C)
            yield
            kvb = dve(lambda e, t2=t2, i=i: e.tensor_tensor(
                t2, bank(i).rearrange("p (t n) -> p t n", n=2 * C), bkv.unsqueeze(1).to_broadcast([P, TPB, 2 * C]),
                ALU.add), [last, bkv_ready] + f2)
            psum_ring.leave(i, [kvb])
            ks, f3 = tmp_ring.take()
            yield
            sq = act(lambda e, ks=ks, kk=kk: e.activation(T(ks)[:, :], T(kk)[:, :], ACT.Square), [kvb] + f3)
            vv = var[:, b % LANES, :]
            yield
            s1 = dve(lambda e, ks=ks, vv=vv: e.tensor_reduce(
                vv, T(ks)[:, :].rearrange("p (g d) -> p g d", d=HD), X_AXIS, ALU.add), [sq])
            tmp_ring.leave(ks, [s1])
            yield
            s2 = dve(lambda e, vv=vv: e.tensor_scalar(vv, vv, 1.0 / HD, EPS, ALU.mult, ALU.add), [s1])
            vr_ = vrs[:, b % LANES, :]
            s3 = yield from rsqrt(vr_, vv, vt_[:, b % LANES, :], [s2])
            kg = T(kk)[:, :].rearrange("p (g d) -> p g d", d=HD)
            yield
            s4 = dve(lambda e, kg=kg, vr_=vr_: e.tensor_tensor(
                kg, kg, vr_.unsqueeze(2).to_broadcast([P, TPB * G2, HD]), ALU.mult), [s3])
            g2 = gam[:, :, :].rearrange("p g d -> p (g d)").unsqueeze(1).to_broadcast([P, TPB, 2 * C])
            be2 = bet[:, :, :].rearrange("p g d -> p (g d)").unsqueeze(1).to_broadcast([P, TPB, 2 * C])
            yield
            s5 = pool(lambda e, t2=t2, g2=g2: e.tensor_tensor(t2, t2, g2, ALU.mult), [s4, affine])
            yield
            s6 = pool(lambda e, t2=t2, be2=be2: e.tensor_tensor(t2, t2, be2, ALU.add), [s5])
            yield
            i, free = psum_ring.take()
            for n in range(TPB):
                last = mm(psum[:, i, 0:C], t2[:, n, 0:C], t2[:, n, C:2 * C], start=n == 0, stop=n == TPB - 1,
                          after=[s6] + free)
            tmp_ring.leave(kk, [last])
            kb_, f4 = tmp_ring.take()
            yield
            s7 = dve(lambda e, kb_=kb_, i=i: e.tensor_tensor(T(kb_)[:, 0:C], psum[:, i, 0:C], temp_blk[:, :],
                                                             ALU.mult), [last, blk_ready] + f4)
            psum_ring.leave(i, [s7])
            yield
            s8 = dve(lambda e, kb_=kb_: e.tensor_tensor(T(kb_)[:, 0:C], T(kb_)[:, 0:C], bias_blk[:, :],
                                                        ALU.add), [s7])
            yield
            i, free = psum_ring.take()
            last = mm(psum[:, i, 0:S], T(kb_)[:, 0:C], T(kq)[:, 0:S], after=[s8, qs] + free)
            tmp_ring.leave(kb_, [last])
            tmp_ring.leave(kq, [last])
            ka, f5 = tmp_ring.take()
            yield
            at = dve(lambda e, ka=ka, i=i, bs=bs: e.tensor_tensor(T(ka)[:, 0:S], psum[:, i, 0:S], hT[:, bs],
                                                                  ALU.add), [last] + f5)
            psum_ring.leave(i, [at])
            yield
            i, free = psum_ring.take()
            last = mm(psum[:, i, 0:S], w_t[:, 3, :], T(ka)[:, 0:S], after=[at] + free)
            tmp_ring.leave(ka, [last])
            kh, f6 = tmp_ring.take()
            yield
            ge = act(lambda e, kh=kh, i=i: e.activation(T(kh)[:, 0:S], psum[:, i, 0:S], ACT.Gelu,
                                                        bias=col("L1_attn_p1_b")), [last] + f6)
            psum_ring.leave(i, [ge])
            yield
            i, free = psum_ring.take()
            last = mm(psum[:, i, 0:S], w_t[:, 4, :], T(kh)[:, 0:S], after=[ge] + free)
            tmp_ring.leave(kh, [last])
            ko, f7 = tmp_ring.take()
            yield
            o1 = dve(lambda e, ko=ko, i=i, bs=bs: e.tensor_tensor(T(ko)[:, 0:S], psum[:, i, 0:S], hT[:, bs],
                                                                  ALU.add), [last] + f7)
            psum_ring.leave(i, [o1])
            yield
            o2 = act(lambda e, ko=ko, b=b: e.activation(
                T(ko)[:, 0:S], T(ko)[:, 0:S], ACT.Identity, bias=small[:, 1, 0, b:b + 1],
                scale=modT[:, 1, 2, b:b + 1]), [o1, p2_ready])
            yield
            i, free = psum_ring.take()
            for n in range(TPB):
                tr = pe(lambda e, n=n, ko=ko, i=i: e.transpose(psum[:, i, n * P:(n + 1) * P],
                                                              T(ko)[:, n * P:(n + 1) * P], ident[:, :]),
                        [o2] + free)
            tmp_ring.leave(ko, [tr])
            ts = slice(TPB * b, TPB * (b + 1))
            yield
            x1[b] = dve(lambda e, ts=ts, i=i: e.tensor_tensor(
                x[:, ts, :], x[:, ts, :], psum[:, i, 0:S].rearrange("p (t c) -> p t c", c=C), ALU.add), [tr])
            psum_ring.leave(i, [x1[b]])

        interleave(with_statistics((1, 0), linear_attention, lambda b: [x1[b]]), LANES)

        tables_free = []
        for r in range(2):
            free = [w for k in EXTRA[r * FC:(r + 1) * FC] for w in tmp_ring.lend(k)]
            hid_ring.leave(r, free)
            tables_free += free

        h4 = {}

        def routed_input(b):
            h4[b] = yield from normalise(b, (1, 1))

        interleave(with_statistics((1, 1), routed_input, lambda b: [x1[b]]), LANES)
        sc = sb("scores", [P, NT, NE])
        i, free = psum_ring.take()
        for t in range(NT):
            last = mm(psum[:, i, t * NE:(t + 1) * NE], hT[:, t * P:(t + 1) * P], wr[:, :],
                      after=[h4[t // TPB]] + free)
        scored = softmax8(sc, i, last, None)
        desc = sb("desc", [P, NE])
        capbase = sb("capbase", [P, NE])
        for e_ in range(NE):
            pool(lambda e, e_=e_: e.memset(desc[:, e_:e_ + 1], float(NE - e_)))
            tables = pool(lambda e, e_=e_: e.memset(capbase[:, e_:e_ + 1], float(CAP * e_)))

        def wide(t):
            return t[:, :].unsqueeze(1).to_broadcast([P, NT, NE])

        def over(t):
            return t.unsqueeze(2).to_broadcast([P, NT, NE])

        def carve(n, dims, **sizes):
            return big2[:, n * NT * NE:(n + 1) * NT * NE].rearrange(dims, **sizes)

        pick = [carve(k, "p (t e) -> p t e", e=NE) for k in range(TOPK)]
        wts = dst_[:, :, 2 * TOPK:3 * TOPK].rearrange("p t k -> p k t")
        best = sb("best", [P, NT])
        left = carve(2, "p (t e) -> p t e", e=NE)
        ready = dve(lambda e: e.tensor_copy(left[:, :, :], sc[:, :, :]), [scored] + tables_free)
        for k in range(TOPK):
            pk = pick[k]
            r1 = dve(lambda e, k=k: e.tensor_reduce(wts[:, k, :], left[:, :, :], X_AXIS, ALU.max), [ready])
            r2 = dve(lambda e, k=k, pk=pk: e.tensor_tensor(pk[:, :, :], left[:, :, :], over(wts[:, k, :]),
                                                           ALU.is_equal), [r1])
            r3 = dve(lambda e, pk=pk: e.tensor_tensor(pk[:, :, :], pk[:, :, :], wide(desc), ALU.mult), [r2, tables])
            r4 = dve(lambda e, pk=pk: e.tensor_reduce(best[:, :], pk[:, :, :], X_AXIS, ALU.max), [r3])
            r5 = dve(lambda e, pk=pk: e.tensor_tensor(pk[:, :, :], pk[:, :, :], over(best[:, :]), ALU.is_equal),
                     [r4])
            ready = dve(lambda e, pk=pk: e.scalar_tensor_tensor(
                left[:, :, :], pk[:, :, :], -2.0, left[:, :, :], ALU.mult, ALU.add), [r5])
        sel = sb("sel", [P, NE, NT], BF16)
        sl = dve(lambda e: e.tensor_tensor(sel[:, :, :].rearrange("p e t -> p t e"), pick[0][:, :, :],
                                           pick[1][:, :, :], ALU.add), [ready])
        iw, free1 = psum_ring.take()
        it, free2 = psum_ring.take()
        flat = sel[:, :, :].rearrange("p e t -> p (e t)")
        mw = mm(psum[:, iw, 0:NE * NT], before[:, :], flat, after=[sl, counters] + free1)
        mt = mm(psum[:, it, 0:NE * NT], ones_b[:, :], flat, after=free2)
        tot = carve(3, "p (e t) -> p e t", t=NT)
        run = carve(4, "p (e t) -> p e t", t=NT)
        keep = carve(5, "p (e t) -> p e t", t=NT)
        k1 = pool(lambda e: e.memset(keep[:, :, :], 1.0), tables_free)
        k2 = pool(lambda e: e.memset(keep[:, :, 0:1], 0.0), [k1])
        c1 = dve(lambda e: e.tensor_copy(tot[:, :, :], psum[:, it, 0:NE * NT].rearrange("p (e t) -> p e t", t=NT)),
                 [mt])
        psum_ring.leave(it, [c1])
        c2 = dve(lambda e: e.tensor_tensor_scan(
            run[:, :, :].rearrange("p e t -> p (e t)"), keep[:, :, :].rearrange("p e t -> p (e t)"),
            tot[:, :, :].rearrange("p e t -> p (e t)"), 0.0, ALU.mult, ALU.add), [c1, k2])
        c3 = dve(lambda e: e.tensor_tensor(run[:, :, :], run[:, :, :], tot[:, :, :], ALU.subtract), [c2])
        c4 = dve(lambda e: e.tensor_tensor(
            run[:, :, :], psum[:, iw, 0:NE * NT].rearrange("p (e t) -> p e t", t=NT), run[:, :, :], ALU.add),
            [c3, mw])
        psum_ring.leave(iw, [c4])
        rank = run[:, :, :].rearrange("p e t -> p t e")
        slot_f, rank_f = (dst_[:, :, k * TOPK:(k + 1) * TOPK].rearrange("p t k -> p k t")
                               for k in range(2))
        slot_i = sb("slot_i", [P, TOPK, NT], I32)
        for k in range(TOPK):
            d1 = dve(lambda e, k=k: e.tensor_tensor(left[:, :, :], pick[k][:, :, :], rank, ALU.mult), [c4])
            d2 = dve(lambda e, k=k: e.tensor_reduce(rank_f[:, k, :], left[:, :, :], X_AXIS, ALU.add), [d1])
            d3 = dve(lambda e, k=k: e.tensor_tensor(left[:, :, :], pick[k][:, :, :], wide(capbase), ALU.mult), [d2])
            d4 = dve(lambda e, k=k: e.tensor_reduce(slot_f[:, k, :], left[:, :, :], X_AXIS, ALU.add), [d3])
            d5 = dve(lambda e, k=k: e.tensor_tensor(slot_f[:, k, :], slot_f[:, k, :], rank_f[:, k, :], ALU.add),
                     [d4])
            d6 = dve(lambda e, k=k: e.tensor_scalar(rank_f[:, k, :], rank_f[:, k, :], float(CAP), float(SLOTS),
                                                    ALU.is_ge, ALU.mult), [d5])
            d7 = dve(lambda e, k=k: e.tensor_tensor(slot_f[:, k, :], slot_f[:, k, :], rank_f[:, k, :], ALU.add),
                     [d6])
            slots_ready = dve(lambda e, k=k: e.tensor_copy(slot_i[:, k, :], slot_f[:, k, :]), [d7])

        RT = 16
        rows_buf = big1[:, 0:RT * TOPK * ROW].rearrange("p (t k n) -> p t k n", k=TOPK, n=ROW)
        dest = sb("dest", [P, TOPK, NT], I32)
        io = pool(lambda e: e.iota(dest[:, :, :], pattern=[[TOK, TOPK], [P, NT]], base=0, channel_multiplier=1))
        s_sc = [stream(f"scatter{i}") for i in range(2)]
        sent = []
        for half in range(NT // RT):
            h0 = half * RT
            for k in range(TOPK):
                m1 = dve(lambda e, k=k, h0=h0: e.tensor_copy(rows_buf[:, :, k, C], dest[:, k, h0:h0 + RT]),
                         [io] + sent)
                m2 = dve(lambda e, k=k, h0=h0: e.tensor_copy(rows_buf[:, :, k, C + 1], wts[:, k, h0:h0 + RT]), sent)
            new = []
            for n in range(RT // CT):
                i, free = psum_ring.take()
                for m in range(CT):
                    t = h0 + n * CT + m
                    tr = pe(lambda e, m=m, t=t, i=i: e.transpose(psum[:, i, m * P:(m + 1) * P],
                                                                hT[:, t * P:(t + 1) * P], ident[:, :]),
                            [h4[t // TPB]] + free)
                src = bank(i).rearrange("p (t c) -> p t c", c=C)
                ca = act(lambda e, n=n, src=src: e.copy(rows_buf[:, n * CT:(n + 1) * CT, 0, 0:C], src),
                         [tr] + sent)
                cb = dve(lambda e, n=n, src=src: e.tensor_copy(rows_buf[:, n * CT:(n + 1) * CT, 1, 0:C], src),
                         [ca] + sent)
                psum_ring.leave(i, [cb])
                for m in range(CT):
                    t = h0 + n * CT + m
                    for k in range(TOPK):
                        d = q.dma("gpsimd", s_sc[half], lambda e, k=k, t=t, m=m, n=n: e.indirect_dma_start(
                            out=routed, out_offset=bass.IndirectOffsetOnAxis(ap=slot_i[:, k, t:t + 1], axis=0),
                            in_=rows_buf[:, n * CT + m, k, :], in_offset=None, bounds_check=SLOTS - 1,
                            oob_is_err=False), [ca, cb, m1, m2, slots_ready, routed_empty])
            new = [d]
            sent = new
            all_sent = (all_sent if half else []) + [d]

        xb = big1[:, RT * TOPK * ROW:RT * TOPK * ROW + 2 * CT * ROW].rearrange("p (r n c) -> p r n c", r=2, c=ROW)
        to = sb("to", [P, 2, CT], I32)
        s_xb = [stream(f"xb{i}") for i in range(2)]
        s_out = [stream(f"ans{i}") for i in range(2)]
        xb_left = [[], []]
        routed_v = routed.rearrange("(u n p) c -> u p n c", p=P, n=CT)
        UNITS = SLOTS // CHUNK
        yw = [None, None]
        ans_sent = [[], []]
        ew_ready = [ew1_in]
        ans_buf = hT[:, 0:2 * CHUNK].rearrange("p (r n c) -> p r n c", r=2, c=C)

        def gelu(i, r, f, e_, last, hfree):
            s = act(lambda e: e.activation(hid[:, r, f, :], bank(i), ACT.Gelu_apprx_tanh), [last] + hfree)
            psum_ring.leave(i, [s])
            return s

        def finish(unit, r, done):
            k = unit % 2
            e_ = unit * CHUNK // CAP
            i, last = down(e_, r, done)
            for m in range(CT):
                s = dve(lambda e, m=m: e.tensor_scalar(ans_buf[:, k, m, :], psum[:, i, m * C:(m + 1) * C],
                                                       xb[:, k, m, C + 1:C + 2], None, ALU.mult),
                        [last] + ans_sent[k] + [xb_in[unit], h4_read])
            psum_ring.leave(i, [s])
            for m in range(CT):
                d = q.dma("gpsimd", s_out[k], lambda e, m=m: e.indirect_dma_start(
                    out=answers, out_offset=bass.IndirectOffsetOnAxis(ap=to[:, k, m:m + 1], axis=0),
                    in_=ans_buf[:, k, m, :], in_offset=None, bounds_check=TOPK * TOK - 1, oob_is_err=False),
                    [s, to_in[unit], answers_zero])
            ans_sent[k] = [d]
            xb_left[k] = [s]

        h4_read = tr
        xb_in, to_in = {}, {}
        pending = None
        for unit in range(UNITS):
            k = unit % 2
            xb_in[unit] = load(s_xb[k], xb[:, k, :, :], routed_v[unit], all_sent + xb_left[k] + ans_sent[k])
            to_in[unit] = dve(lambda e, k=k: e.tensor_copy(to[:, k, :], xb[:, k, :, C]),
                              [xb_in[unit]] + ans_sent[k])
            i, free = psum_ring.take()
            for m in range(CT):
                tr = pe(lambda e, m=m, k=k, i=i: e.transpose(psum[:, i, m * P:(m + 1) * P], xb[:, k, m, 0:C],
                                                            ident[:, :]), [xb_in[unit]] + free)
            kx, tfree = tmp_ring.take()
            cp = dve(lambda e, kx=kx, i=i: e.tensor_copy(T(kx)[:, :], bank(i)), [tr] + tfree)
            psum_ring.leave(i, [cp])
            r, done = up(unit * CHUNK // CAP, unit, T(kx)[:, :], cp, gelu)
            tmp_ring.leave(kx, done)
            if pending:
                finish(*pending)
            pending = (unit, r, done)
        finish(*pending)

        out_v = out.rearrange("b (t p) c -> p (b t) c", p=P)
        s_y = [stream(f"yin{i}") for i in range(2)]
        s_res = stream("result")
        ans_v = answers.rearrange("(k n p) c -> k p n c", k=TOPK, p=P)
        yb = big1[:, 0:4 * CHUNK].rearrange("p (r k t c) -> p r k t c", r=2, k=TOPK, c=C)
        yfree = [[], []]
        s_last = ans_sent[0] + ans_sent[1]
        for n in range(NCH):
            r = n % 2
            ts = slice(CT * n, CT * (n + 1))
            for k in range(TOPK):
                d = load(s_y[r], yb[:, r, k, :, :], ans_v[k, :, ts, :], s_last + yfree[r])
            s1 = dve(lambda e, r=r: e.tensor_tensor(yb[:, r, 0, :, :], yb[:, r, 0, :, :], yb[:, r, 1, :, :],
                                                    ALU.add), [d])
            s2 = dve(lambda e, r=r: e.tensor_tensor(
                yb[:, r, 0, :, :], yb[:, r, 0, :, :], row("L1_ffn_bias").unsqueeze(1).to_broadcast([P, CT, C]),
                ALU.add), [s1])
            add_gated_src = yb[:, r, 0, :, :]
            for h in range(2):
                b = 2 * n + h
                m = dve(lambda e, h=h, b=b, src=add_gated_src: e.tensor_tensor(
                    src[:, TPB * h:TPB * (h + 1), :], src[:, TPB * h:TPB * (h + 1), :],
                    gb_tok[:, b, :].unsqueeze(1).to_broadcast([P, TPB, C]), ALU.mult), [s2, gates_tok])
            ad = dve(lambda e, ts=ts, src=add_gated_src: e.tensor_tensor(x[:, ts, :], x[:, ts, :], src, ALU.add),
                     [m, x1[2 * n + 1]])
            yfree[r] = [ad]
            res = load(s_res, out_v[:, ts, :], x[:, ts, :], [ad])

        q.number()
        block = ctx.enter_context(nc.Block())

        @block.sync
        def _(eng):
            q.play("sync", eng)
            for st in [s_res, s_fill] + s_part + s_sc + s_out:
                eng.wait_ge(st.sem, st.count)

        @block.tensor
        def _(eng):
            q.play("tensor", eng)

        @block.vector
        def _(eng):
            q.play("vector", eng)

        @block.scalar
        def _(eng):
            q.play("scalar", eng)

        @block.gpsimd
        def _(eng):
            q.play("gpsimd", eng)


def kernel(**inputs):
    import concourse.bacc as bacc
    from concourse.bass_utils import run_bass_kernel_spmd

    nc = bacc.Bacc("TRN2", target_bir_lowering=False, num_devices=1)
    arrays, aps = {}, {}
    for name, value in inputs.items():
        v = np.ascontiguousarray(value)
        arrays[f"in_{name}"] = v
        aps[name] = nc.dram_tensor(f"in_{name}", v.shape, mybir.dt.from_np(v.dtype), kind="ExternalInput").ap()
    out = nc.dram_tensor("out", (B, S, C), F32, kind="ExternalOutput").ap()
    build(nc, aps, out)
    r = run_bass_kernel_spmd(nc, [arrays], core_ids=[0])
    return r.results[0]["out"]
```

```python
from contextlib import ExitStack

import numpy as np
import concourse.bass as bass
from concourse import mybir

F32 = mybir.dt.float32
F32R = mybir.dt.float32r
BF16 = mybir.dt.bfloat16
I32 = mybir.dt.int32
ALU = mybir.AluOpType
ACT = mybir.ActivationFunctionType
X_AXIS = mybir.AxisListType.X

B, S, C = 16, 256, 128
P = 128
QUAD = P // 4
TOK = B * S
NT = TOK // P
TPB = S // P
HEADS, HD = 16, 8
HID = 64
GW = 16
NE, FF = 8, 512
FC = FF // P
CHUNK = 512
NCH = TOK // CHUNK
CT = CHUNK // P
TOPK = 2
CAP = TOPK * TOK // NE
SLOTS = NE * CAP
EPS = 1e-5
MASKED = -1e30
ROW = C + 2
MOD = 6


class Step:

    def __init__(self, engine, emit, after):
        self.engine, self.emit, self.after, self.signals, self.value = engine, emit, after, False, None


class Landed:

    def __init__(self, stream, value):
        self.stream, self.value = stream, value


class Stream:

    def __init__(self, sem):
        self.sem, self.count = sem, 0


class Queues:

    def __init__(self, nc, new_sem):
        self.nc = nc
        self.lists = {n: [] for n in ("tensor", "vector", "scalar", "gpsimd", "sync")}
        self.sems = {n: new_sem(f"done_{n}") for n in ("tensor", "vector", "scalar", "gpsimd")}

    def step(self, engine, emit, after=()):
        s = Step(engine, emit, list(after))
        for a in s.after:
            if isinstance(a, Step):
                a.signals = True
        self.lists[engine].append(s)
        return s

    def dma(self, engine, stream, emit, after=()):
        s = self.step(engine, emit, after)
        s.stream = stream
        stream.count += 16
        return Landed(stream, stream.count)

    def number(self):
        for name, steps in self.lists.items():
            n = 0
            for s in steps:
                if s.signals:
                    n += 1
                    s.value = n

    def play(self, name, eng):
        seen = {}
        for s in self.lists[name]:
            need = {}
            for a in s.after:
                if isinstance(a, Step):
                    sem, value = self.sems[a.engine], a.value
                else:
                    sem, value = a.stream.sem, a.value
                key = id(sem)
                if value > seen.get(key, 0) and value > need.get(key, (None, 0))[1]:
                    need[key] = (sem, value)
            for key, (sem, value) in need.items():
                eng.wait_ge(sem, value)
                seen[key] = value
            inst = s.emit(eng)
            if hasattr(s, "stream"):
                inst.then_inc(s.stream.sem, 16)
            elif s.signals:
                inst.then_inc(self.sems[name], 1)


class Ring:

    def __init__(self, ids):
        self.free = [(i, []) for i in ids]

    def take(self):
        return self.free.pop(0)

    def leave(self, i, steps):
        self.free.append((i, list(steps)))

    def lend(self, i):
        at = next(n for n, f in enumerate(self.free) if f[0] == i)
        return self.free.pop(at)[1]


def room(ring, n):
    yield
    while len(ring.free) < n:
        yield


class Lanes:

    def __init__(self, tasks, width):
        self.tasks, self.width, self.active = list(tasks), width, []

    def advance(self):
        while self.tasks and len(self.active) < self.width:
            self.active.append(self.tasks.pop(0))
        for t in list(self.active):
            try:
                next(t)
            except StopIteration:
                self.active.remove(t)
        return bool(self.tasks or self.active)


def interleave(tasks, width):
    lanes = Lanes(tasks, width)
    while lanes.advance():
        pass


def build(nc, a, out):
    ctx = ExitStack()
    with ctx:
        def sb(name, shape, dt=F32):
            return ctx.enter_context(nc.sbuf_tensor(name, shape, dt))

        def new_sem(name):
            return ctx.enter_context(nc.semaphore(name))

        q = Queues(nc, new_sem)

        def pe(emit, after=()):
            return q.step("tensor", emit, after)

        def dve(emit, after=()):
            return q.step("vector", emit, after)

        def act(emit, after=()):
            return q.step("scalar", emit, after)

        def pool(emit, after=()):
            return q.step("gpsimd", emit, after)

        def mm(o, l, r, start=True, stop=True, after=(), skip=False):
            return pe(lambda e: e.matmul(o, l, r, start=start, stop=stop, skip_group_check=skip), after)

        def stream(name):
            return Stream(new_sem(name))

        def load(st, dst, src, after=(), engine="sync"):
            return q.dma(engine, st, lambda e: e.dma_start(dst, src), after)

        x = sb("x", [P, NT, C])
        hT = sb("hT", [P, TOK])
        hT3 = hT[:, :].rearrange("p (t c) -> p t c", c=C)
        big1 = sb("big1", [P, NT * (C + HID)])
        VAW = HEADS * (HD + 1) + P // 4 - (HD + 1)
        big2 = sb("big2", [P, NT * VAW])
        tmp = sb("tmp", [P, 8, CHUNK])
        gb_tok = sb("gb_tok", [P, B, C])
        ew1 = sb("ew1", [P, NE, FF])
        ew2 = sb("ew2", [P, NE, FC, C])
        QR = 4
        q_stack = [sb(f"q_stack{i}", [P, 4, S], F32R) for i in range(QR)]
        k_stack = [sb(f"k_stack{i}", [P, 4, S], F32R) for i in range(QR)]
        parts = [sb(f"parts{i}", [P, CHUNK], F32R) for i in range(4)]
        ident = sb("ident", [P, P])
        ident_b = sb("ident_b", [P, P], BF16)
        mask_qk = sb("mask_qk", [P, 4, P], BF16)
        mask_kq = sb("mask_kq", [P, 4, P], BF16)
        before = sb("before", [P, P], BF16)
        ones_b = sb("ones_b", [P, P], BF16)
        psum = ctx.enter_context(nc.psum_tensor("psum", [P, 8, CHUNK], F32))

        def bank(i, n=CHUNK):
            return psum[:, i, 0:n]

        psum_ring = Ring(range(8))
        tmp_ring = Ring(range(8))

        def T(k):
            if k < 8:
                return tmp[:, k, :]
            at = TOK + 5 * C + (k - 8) * CHUNK
            return big1[:, at:at + CHUNK]


        q_parts = nc.dram_tensor("q_parts", [P, 3, TOK], F32, kind="Internal").ap()
        k_parts = nc.dram_tensor("k_parts", [P, 3, TOK], F32, kind="Internal").ap()
        routed = nc.dram_tensor("routed", [SLOTS, ROW], F32, kind="Internal").ap()
        answers = nc.dram_tensor("answers", [TOPK * TOK, C], F32, kind="Internal").ap()

        s_col, s_w, s_late, s_rowp, s_ew = (stream(n) for n in ("cols", "weights", "late", "rows", "experts"))
        s_mod = [stream(f"mod{i}") for i in range(2)]
        s_x = [stream(f"x{i}") for i in range(4)]
        wqk = sb("wqk", [P, 2, C])
        wvd = sb("wvd", [P, C + HID])
        wo = sb("wo", [P, C])
        fw = sb("fw", [P, 4, C])
        wg = sb("wg", [P, NE])
        w_t = sb("w_t", [P, 5, C])
        wr = sb("wr", [P, NE])
        spare = gb_tok[:, :, :].rearrange("p b c -> p (b c)")
        wmod = spare[:, 0:MOD * C]
        zeros = spare[:, MOD * C:MOD * C + S]
        minus = spare[:, MOD * C + S:MOD * C + 2 * S]
        xd = a["L0_attn_x"].rearrange("b (t p) c -> p (b t) c", p=P)
        XT = NT // len(s_x)
        x_in = []

        def load_x(i):
            x_in.append(load(s_x[i], x[:, XT * i:XT * (i + 1), :], xd[:, XT * i:XT * (i + 1), :]))

        load_x(0)

        COLS = {}
        n_cols = 0
        for name, n in (("L0_c", B), ("L1_c", B),
                        ("L0_attn_bq", 1), ("L0_attn_bk", 1), ("L0_attn_bo", 1), ("L0_ffn_bq", 1),
                        ("L0_ffn_bk", 1), ("L0_ffn_bo", 1), ("L1_attn_p1_b", 1), ("L1_attn_p2_b", 1),
                        ("L1_attn_qkv_b", 3), ("L0_ffn_b1", NE * FC)):
            COLS[name] = n_cols
            n_cols += n
        cols = sb("cols", [P, n_cols])
        col_rows = sb("col_rows", [n_cols, P])
        for name, at in COLS.items():
            v = a[name]
            if len(v.shape) == 2:
                v = v.rearrange("e f -> (e f)")
            n = v.shape[0] // P
            cols_loaded = load(s_col, col_rows[at:at + n, :], v.rearrange("(n p) -> n p", p=P))

        mod_in = {0: load(s_mod[0], wmod, a["L0_wmod"])}
        load(s_w, wvd[:, 0:C], a["L0_attn_Wv"])
        load(s_w, wvd[:, C:C + HID], a["L0_attn_dp_w1"])
        load(s_w, wqk[:, 0, :], a["L0_attn_Wq"])
        w_in = load(s_w, wqk[:, 1, :], a["L0_attn_Wk"])
        load_x(1)

        def col(name, i=0):
            return cols[:, COLS[name] + i:COLS[name] + i + 1]

        ROWS = {}
        n_rows = 0
        for name, n in (("L0_attn_bv", C), ("L0_attn_dp_b1", HID), ("L0_attn_ln_g", HID), ("L0_attn_ln_b", HID),
                        ("L0_attn_dp_w2", HID), ("L0_attn_dp_b2", 1), ("L0_attn_g_w1", GW), ("L0_attn_g_b1", GW),
                        ("L0_attn_g_w2", GW), ("L0_attn_g_b2", 1), ("L0_ffn_bv", C), ("L0_ffn_bg", NE),
                        ("L1_attn_qkv_b", 3 * C), ("L1_attn_kn_g", HD), ("L1_attn_vn_g", HD),
                        ("L1_attn_kn_b", HD), ("L1_attn_vn_b", HD), ("L1_ffn_bias", C)):
            ROWS[name] = (n_rows, n)
            n_rows += n
        rows = sb("rows", [P, n_rows])
        for name, (at, n) in ROWS.items():
            v = a[name]
            if len(v.shape) == 2:
                v = v.rearrange("a b -> (a b)")
            if len(v.shape) == 3:
                v = v.rearrange("a b c -> (a b c)")
            rows_in = load(s_rowp, rows[:, at:at + n], v.unsqueeze(0).to_broadcast([P, n]))

        def row(name):
            at, n = ROWS[name]
            return rows[:, at:at + n]

        load_x(2)
        load_x(3)
        load(s_late, wo[:, :], a["L0_attn_Wo"])
        for i, n in enumerate("qkvo"):
            load(s_late, fw[:, i, :], a[f"L0_ffn_W{n}"])
        load(s_late, wg[:, :], a["L0_ffn_Wg"])
        def select(t, pattern, mult, base, fill, cmp, after):
            return pool(lambda e: e.affine_select(out=t, in_=t, pattern=pattern, compare_op=cmp, fill=fill,
                                                  base=base, channel_multiplier=mult), after)

        z1 = pool(lambda e: e.memset(ident[:, :], 0.0))
        identity = select(ident[:, :], [[-1, P]], 1, 0, 1.0, ALU.not_equal, [z1])
        z2 = pool(lambda e: e.memset(ident_b[:, :], 0.0))
        identity_b = select(ident_b[:, :], [[-1, P]], 1, 0, 1.0, ALU.not_equal, [z2])
        z3 = pool(lambda e: e.memset(mask_qk[:, :, :], 0.0))
        select(mask_qk[:, :, :], [[0, 4], [-1, P]], 1, 0, MASKED, ALU.is_ge, [z3])
        z4 = pool(lambda e: e.memset(mask_kq[:, :, :], 0.0))
        masks = select(mask_kq[:, :, :], [[0, 4], [1, P]], -1, 0, MASKED, ALU.is_ge, [z4])
        z5 = pool(lambda e: e.memset(before[:, :], 1.0))
        select(before[:, :], [[1, P]], -1, -1, 0.0, ALU.is_ge, [z5])
        counters = pool(lambda e: e.memset(ones_b[:, :], 1.0))

        col_free = psum_ring.take()[1]
        turned = pe(lambda e: e.transpose(psum[:, 0, 0:n_cols], col_rows[:, :],
                                          ident[0:n_cols, 0:n_cols]), [cols_loaded, identity] + col_free)
        cols_in = dve(lambda e: e.tensor_copy(cols[:, :], psum[:, 0, 0:n_cols]), [turned])
        psum_ring.leave(0, [cols_in])
        cT = cols[:, 0:2 * B].rearrange("p (l b) -> p l b", l=2)

        z6 = pool(lambda e: e.memset(zeros, 0.0))
        z7 = pool(lambda e: e.memset(minus, 0.0))
        for i in range(P // HD):
            z7 = select(minus, [[0, S]], 1, -HD * i, -1.0, ALU.not_equal, [z7])
        s_fill = stream("fill")
        PARTS = 4
        for r in range(QR):
            for dst, src in ((q_stack, zeros), (k_stack, minus)):
                part3_filled = load(s_fill, dst[r][PARTS - 1:P:PARTS, :, :].bitcast(F32),
                                    src[0:P // PARTS, :].unsqueeze(1).to_broadcast([P // PARTS, 4, S]), [z6, z7])

        sil = sb("sil", [P, 2, B])
        silu = act(lambda e: e.activation(sil[:, :, :], cT, ACT.Silu), [cols_in])
        modT = sb("modT", [P, 2, MOD, B])
        mod_ready = {}

        def modulation(l):
            i, free = psum_ring.take()
            for g in range(MOD):
                last = mm(psum[:, i, g * B:(g + 1) * B], wmod[:, g * C:(g + 1) * C], sil[:, l, :],
                          after=[silu, mod_in[l]] + free)
            cp = dve(lambda e: e.tensor_copy(
                modT[:, l, :, :], psum[:, i, 0:MOD * B].rearrange("p (g b) -> p g b", b=B)), [last])
            psum_ring.leave(i, [cp])
            scales = modT[:, l, 1:MOD:3, :]
            mod_ready[l] = [dve(lambda e: e.tensor_scalar(scales, scales, 1.0, None, ALU.add), [cp])]
            gates_ = modT[:, l, 2:MOD:3, :]
            s1 = dve(lambda e: e.tensor_scalar(sgn[:, :, :], gates_, 0.0, 2.0, ALU.is_ge, ALU.mult), [cp])
            s2 = dve(lambda e: e.scalar_tensor_tensor(mag[:, :, :], gates_, -1.0, gates_, ALU.mult, ALU.max), [cp])
            s3 = dve(lambda e: e.tensor_scalar(mag[:, :, :], mag[:, :, :], 0.25, None, ALU.max), [s2])
            mod_ready[l].append(dve(lambda e: e.scalar_tensor_tensor(
                gates_, sgn[:, :, :], -1.0, mag[:, :, :], ALU.add, ALU.mult), [s1, s3]))
            return last

        sgn = sb("sgn", [P, 2, B])
        mag = sb("mag", [P, 2, B])
        wmod_read = modulation(0)
        mod_in[1] = load(s_mod[1], wmod, a["L1_wmod"], [wmod_read])

        def spread_gates(l, gb_free):
            for n in range(B // 4):
                i, free = psum_ring.take()
                for k in range(4):
                    b = 4 * n + k
                    t, tfree = tmp_ring.take()
                    rep = dve(lambda e, t=t, b=b: e.tensor_copy(
                        T(t)[:, 0:P], modT[:, l, 5, b:b + 1].to_broadcast([P, P])), mod_ready[l] + tfree)
                    last = mm(psum[:, i, k * C:(k + 1) * C], T(t)[:, 0:P], ident[:, :],
                              after=[rep, identity] + free)
                    tmp_ring.leave(t, [last])
                cp = act(lambda e, i=i, n=n: e.copy(
                    gb_tok[:, 4 * n:4 * n + 4, :].rearrange("p b c -> p (b c)"), bank(i)), [last] + gb_free)
                psum_ring.leave(i, [cp])
            return cp

        stats = sb("stats", [P, NT, 6])
        mv = sb("mv", [P, NT, 2])
        rstd = sb("rstd", [P, NT])

        LG = CT
        ln_tmp = sb("ln_tmp", [P, NT])

        def rsqrt(y, v, t, ready):
            s1 = dve(lambda e: e.tensor_scalar(t.bitcast(I32), v.bitcast(I32), 1, None, ALU.arith_shift_right),
                     ready)
            yield
            s2 = dve(lambda e: e.tensor_scalar(y.bitcast(I32), t.bitcast(I32), -1.0, float(0x5F3759DF),
                                               ALU.mult, ALU.add), [s1])
            for _ in range(3):
                yield
                s1 = dve(lambda e: e.scalar_tensor_tensor(t, y, -0.5, y, ALU.mult, ALU.mult), [s2])
                yield
                s1 = dve(lambda e: e.tensor_tensor(t, t, v, ALU.mult), [s1])
                yield
                s2 = dve(lambda e: e.scalar_tensor_tensor(y, t, 1.5, y, ALU.add, ALU.mult), [s1])
            return s2

        rstd_ready = {}

        def statistics(kind, g, x_ready):
            t0 = LG * g
            while any(t // TPB not in x_ready for t in range(t0, t0 + LG)):
                yield
            for t in range(t0, t0 + LG):
                st = dve(lambda e, t=t: e.bn_stats(stats[:, t, :], x[:, t, :]), [x_ready[t // TPB]])
                if t % 2:
                    yield
            for t in range(t0, t0 + LG):
                ag = dve(lambda e, t=t: e.bn_aggr(mv[:, t, :], stats[:, t, :]), [st])
            yield
            v = mv[:, t0:t0 + LG, 1]
            ev = dve(lambda e: e.tensor_scalar(v, v, EPS, None, ALU.add), [ag])
            rstd_ready[kind, g] = yield from rsqrt(rstd[:, t0:t0 + LG], v, ln_tmp[:, t0:t0 + LG], [ev])

        def with_statistics(kind, tasks, x_ready):
            per = LG // TPB
            out = [statistics(kind, 0, x_ready)]
            for b in range(B):
                if b % per == 0 and b // per + 1 < B // per:
                    out.append(statistics(kind, b // per + 1, x_ready))
                out.append(tasks(b))
            return out

        def normalise(b, kind):
            l, second = kind
            t0 = TPB * b
            while (kind, t0 // LG) not in rstd_ready:
                yield
            rs = rstd_ready[kind, t0 // LG]
            yield from room(tmp_ring, 1)
            i, free = psum_ring.take()
            k, tfree = tmp_ring.take()
            zs = []
            for n in range(TPB):
                z, t = T(k)[:, n * C:(n + 1) * C], t0 + n
                zs.append(dve(lambda e, z=z, t=t: e.tensor_scalar(z, x[:, t, :], mv[:, t, 0:1], rstd[:, t:t + 1],
                                                                  ALU.subtract, ALU.mult), [rs] + tfree))
            yield
            for n in range(TPB):
                z = T(k)[:, n * C:(n + 1) * C]
                tr = pe(lambda e, z=z, n=n, i=i: e.transpose(psum[:, i, n * P:(n + 1) * P], z, ident[:, :]),
                        [zs[n], identity] + free)
            tmp_ring.leave(k, [tr])
            g = 3 * second
            w = act(lambda e: e.activation(hT[:, b * S:(b + 1) * S], psum[:, i, 0:S], ACT.Identity,
                                           bias=modT[:, l, g, b:b + 1], scale=modT[:, l, g + 1, b:b + 1]),
                    [tr] + mod_ready[l])
            psum_ring.leave(i, [w])
            return w

        hready = {}
        VW = C + HID
        vd = big1[:, :].rearrange("p (t n) -> p t n", n=VW)
        vd_in = {}
        bias_vd = rows[:, ROWS["L0_attn_bv"][0]:ROWS["L0_attn_bv"][0] + VW]

        def values(b):
            hready[b] = yield from normalise(b, (0, 0))
            yield
            i, free = psum_ring.take()
            for n in range(TPB):
                t = TPB * b + n
                last = mm(psum[:, i, n * VW:(n + 1) * VW], hT[:, t * P:(t + 1) * P], wvd[:, :],
                          after=[hready[b], w_in] + free)
            src = psum[:, i, 0:TPB * VW].rearrange("p (t n) -> p t n", n=VW)
            yield
            vd_in[b] = dve(lambda e: e.tensor_tensor(
                vd[:, TPB * b:TPB * (b + 1), :], src, bias_vd.unsqueeze(1).to_broadcast([P, TPB, VW]), ALU.add),
                [last, rows_in])
            psum_ring.leave(i, [vd_in[b]])

        s_part = [stream(f"part{i}") for i in range(4)]
        part_sent = [[] for _ in range(4)]
        qk_stored = {}

        def project(n):
            cs = slice(n * CHUNK, (n + 1) * CHUNK)
            while 2 * n + 1 not in hready or (n and (n - 1, 1) not in qk_stored):
                yield
            for w, name, dst in ((0, "L0_attn_bq", q_parts), (1, "L0_attn_bk", k_parts)):
                i, free = psum_ring.take()
                last = mm(bank(i), wqk[:, w, :], hT[:, cs], after=[hready[2 * n + 1], w_in] + free)
                yield
                k, tfree = tmp_ring.take()
                hi, lo = parts[2 * w], parts[2 * w + 1]
                h = act(lambda e, hi=hi, i=i, name=name: e.activation(
                    hi[:, :], bank(i), ACT.Identity, bias=col(name)), [last, cols_in] + part_sent[2 * w])
                full = act(lambda e, k=k, i=i, name=name: e.activation(
                    T(k)[:, :], bank(i), ACT.Identity, bias=col(name)), [last, cols_in] + tfree)
                psum_ring.leave(i, [full])
                yield
                l = dve(lambda e, lo=lo, hi=hi, k=k: e.tensor_tensor(
                    lo[:, :], T(k)[:, :], hi[:, :].bitcast(F32), ALU.subtract), [full, h] + part_sent[2 * w + 1])
                tmp_ring.leave(k, [l])
                hi_at, lo_at = ((0, 2), 1) if w == 0 else ((0, 1), 2)
                for p in hi_at:
                    d = load(s_part[2 * w], dst[:, p, cs], hi[:, :].bitcast(F32), [h])
                part_sent[2 * w] = [d, l]
                d2 = load(s_part[2 * w + 1], dst[:, lo_at, cs], lo[:, :].bitcast(F32), [l])
                part_sent[2 * w + 1] = [d2]
                qk_stored[(n, w)] = [d, d2]
                yield

        va_flat = big2[:, :].rearrange("p (t n) -> p t n", n=VAW)
        va = va_flat[:, :, 0:HEADS * (HD + 1)].rearrange("p t (h d) -> p t h d", d=HD + 1)
        va_pad = pool(lambda e: e.memset(va_flat[:, :, HEADS * (HD + 1):VAW], 0.0))
        va_ones = [pool(lambda e, t=t: e.memset(va[:, 8 * t:8 * t + 8, :, HD], 1.0)) for t in range(NT // 8)][-1]
        gate = sb("gate", [P, NT])
        drift = sb("drift", [P, NT])
        dst_ = sb("dstats", [P, NT, 6])
        dmv = sb("dmv", [P, NT, 2])
        drs = sb("drs", [P, NT])
        GT = CHUNK // HID
        gated = {}

        def gate_values(n):
            while TPB * len(vd_in) < (n + 1) * GT:
                yield
            ts = slice(n * GT, (n + 1) * GT)
            for t in range(n * GT, (n + 1) * GT):
                st = dve(lambda e, t=t: e.bn_stats(dst_[:, t, :], vd[:, t, C:VW]), [vd_in[t // TPB]])
                if t % 4 == 3:
                    yield
            for t in range(n * GT, (n + 1) * GT):
                ag = dve(lambda e, t=t: e.bn_aggr(dmv[:, t, :], dst_[:, t, :]), [st])
            yield
            ev = dve(lambda e: e.tensor_scalar(dmv[:, ts, 1], dmv[:, ts, 1], EPS, None, ALU.add), [ag])
            rs = yield from rsqrt(drs[:, ts], dmv[:, ts, 1], dln_tmp[:, ts], [ev])
            yield
            k, tfree = tmp_ring.take()
            t3 = T(k)[:, :].rearrange("p (t n) -> p t n", n=HID)
            for m in range(GT):
                t = n * GT + m
                last = dve(lambda e, t=t, m=m: e.tensor_scalar(
                    t3[:, m, :], vd[:, t, C:VW], dmv[:, t, 0:1], drs[:, t:t + 1], ALU.subtract, ALU.mult),
                    [rs] + tfree)
                if m % 4 == 3:
                    yield

            def rep(name, w=HID):
                return row(name).unsqueeze(1).to_broadcast([P, GT, w])

            s1 = pool(lambda e: e.tensor_tensor(t3, t3, rep("L0_attn_ln_g"), ALU.mult), [last, rows_in])
            yield
            s2 = pool(lambda e: e.tensor_tensor(t3, t3, rep("L0_attn_ln_b"), ALU.add), [s1])
            yield
            s3 = act(lambda e: e.activation(t3, t3, ACT.Gelu), [s2])
            yield
            s4 = pool(lambda e: e.tensor_tensor(t3, t3, rep("L0_attn_dp_w2"), ALU.mult), [s3])
            yield
            s5 = dve(lambda e: e.tensor_reduce(drift[:, ts], t3, X_AXIS, ALU.add), [s4])
            yield
            s6 = dve(lambda e: e.tensor_scalar(drift[:, ts], drift[:, ts], row("L0_attn_dp_b2"), None, ALU.add),
                     [s5])
            g3 = T(k)[:, 0:GT * GW].rearrange("p (t n) -> p t n", n=GW)
            yield
            s7 = dve(lambda e: e.tensor_tensor(
                g3, drift[:, ts].unsqueeze(2).to_broadcast([P, GT, GW]), rep("L0_attn_g_w1", GW), ALU.mult), [s6])
            yield
            s8 = dve(lambda e: e.tensor_tensor(g3, g3, rep("L0_attn_g_b1", GW), ALU.add), [s7])
            yield
            s9 = act(lambda e: e.activation(g3, g3, ACT.Gelu), [s8])
            yield
            s10 = dve(lambda e: e.tensor_tensor(g3, g3, rep("L0_attn_g_w2", GW), ALU.mult), [s9])
            yield
            s11 = dve(lambda e: e.tensor_reduce(gate[:, ts], g3, X_AXIS, ALU.add), [s10])
            tmp_ring.leave(k, [s11])
            yield
            s12 = act(lambda e: e.activation(gate[:, ts], gate[:, ts], ACT.Tanh, bias=row("L0_attn_g_b2")), [s11])
            yield
            for m in range(0, GT, TPB):
                t = n * GT + m
                v = pool(lambda e, t=t: e.tensor_tensor(
                    va[:, t:t + TPB, :, 0:HD], vd[:, t:t + TPB, 0:C].rearrange("p t (h d) -> p t h d", d=HD),
                    gate[:, t:t + TPB].unsqueeze(2).unsqueeze(3).to_broadcast([P, TPB, HEADS, HD]), ALU.mult),
                    [s12, va_ones])
                gated[t] = gated[t + 1] = v

        dln_tmp = sb("dln_tmp", [P, NT])
        tasks = with_statistics((0, 0), values, {b: x_in[b * TPB // XT] for b in range(B)})
        order = tasks[:1]
        batch = 0
        for t in tasks[1:]:
            order.append(t)
            if t.__name__ == "values":
                batch += 1
                if batch % 2 == 0:
                    order.append(project(batch // 2 - 1))
                if batch * TPB % GT == 0:
                    order.append(gate_values(batch * TPB // GT - 1))
        interleave(order, 7)
        modulation(1)

        s_qs = [stream(f"qs{i}") for i in range(QR)]
        s_ks = [stream(f"ks{i}") for i in range(QR)]
        s_m = [stream(f"maxrow{i}") for i in range(QR)]
        stacked, stack_free = {}, [[] for _ in range(QR)]
        mrow_ready = {}
        q_src = q_parts.rearrange("(i r) a t -> a r i t", i=4)
        k_src = k_parts.rearrange("(i r) a t -> a r i t", i=4)

        def stack(b):
            r = b % QR
            ts = slice(b * S, (b + 1) * S)
            n = b * S // CHUNK
            free = [part3_filled] + stack_free[r]
            for p in range(PARTS - 1):
                dq = load(s_qs[r], q_stack[r][p:P:PARTS, :, :].bitcast(F32), q_src[p, :, :, ts],
                          qk_stored[(n, 0)] + free)
                dk = load(s_ks[r], k_stack[r][p:P:PARTS, :, :].bitcast(F32), k_src[p, :, :, ts],
                          qk_stored[(n, 1)] + free)
            if b >= QR:
                dq = load(s_qs[r], q_stack[r][PARTS - 1:P:QUAD, :, :].bitcast(F32),
                          zeros[0:4, :].unsqueeze(1).to_broadcast([4, 4, S]), free)
            stacked[b] = [dq, dk]

        pair = Ring([])
        for i in range(3):
            pair.leave(i, psum_ring.lend(2 * i) + psum_ring.lend(2 * i + 1))
        o_free = psum_ring.lend(6) + psum_ring.lend(7)
        p_ring = Ring([])
        for i in range(4):
            p_ring.leave(i, tmp_ring.lend(2 * i) + tmp_ring.lend(2 * i + 1))
        for i in range(4, 8):
            p_ring.leave(i, [gated[NT - 1]])

        def pair_of_tiles(i):
            if i < 4:
                return tmp[:, 2 * i:2 * i + 2, :]
            at = 2 * CHUNK * (i - 4)
            return big1[:, at:at + 2 * CHUNK].rearrange("p (j n) -> p j n", j=2)
        maxes = sb("maxes", [P, 2, TPB, 4, 4])
        m_hi = sb("m_hi", [HEADS, 2, S], F32R)
        max_in = {}

        def max_unit(b, u):
            r = b % QR
            s, free = pair.take()
            qb, jp = (0, u) if u < 2 else (1, (u - 2) % 2)
            width = P * (qb + 1)
            ii = range(4) if qb == 0 else range(2 * ((u - 2) // 2), 2 * ((u - 2) // 2) + 2)
            last = None
            for jl in range(2):
                out_m = bank(2 * s + jl).rearrange("p (g k) -> p g k", k=width)[:, :, width - P:width]
                mm(out_m, ident_b[:, :], mask_qk[:, 0:len(ii), :], start=True, stop=False,
                   after=[masks, identity_b] + free + stacked[b], skip=True)
            for n, i in enumerate(ii):
                for jl in range(2):
                    j = 2 * jp + jl
                    rows_ = slice(32 * j, 32 * j + 32)
                    last = mm(psum[:, 2 * s + jl, n * width:(n + 1) * width],
                              q_stack[r][rows_, i, qb * P:(qb + 1) * P], k_stack[r][rows_, i, 0:width],
                              start=False, stop=True, skip=True)
            src = psum[:, 2 * s:2 * s + 2, :].rearrange("p j (g k) -> p j g k", k=width)
            dst = maxes[:, b % 2, qb, ii[0]:ii[-1] + 1, 2 * jp:2 * jp + 2].rearrange("p i j -> p j i")
            red = dve(lambda e: e.tensor_reduce(dst, src, X_AXIS, ALU.max), [last])
            pair.leave(s, [red])
            max_in.setdefault(b, []).append(red)

        def max_rows(b):
            r = b % QR
            s, free = pair.take()
            for qb in range(TPB):
                src = maxes[:, b % 2, qb, :, :].rearrange("p i j -> p (i j)")
                tr = pe(lambda e, src=src, qb=qb: e.transpose(
                    psum[0:HEADS, 2 * s, qb * P:(qb + 1) * P], src, ident[:, :]), [max_in[b][-1]] + free)
            wait = mrow_ready.get(b - 2, [])
            cp = dve(lambda e: e.tensor_copy(m_hi[:, b % 2, :], psum[0:HEADS, 2 * s, 0:S]), [tr] + wait)
            pair.leave(s, [cp])
            for i in range(4):
                d = load(s_m[r], q_stack[r][3:P:32, i, :].bitcast(F32), m_hi[4 * i:4 * i + 4, b % 2, :].bitcast(F32),
                         [cp])
            mrow_ready[b] = [d]

        def exp_unit(b, u):
            r = b % QR
            s, free = pair.take()
            kb, jp = (0, u % 2) if u < 4 else (1, u - 4)
            width = P * (2 - kb)
            ii = range(2 * (u // 2), 2 * (u // 2) + 2) if kb == 0 else range(4)
            for jl in range(2):
                out_m = bank(2 * s + jl).rearrange("p (g k) -> p g k", k=width)[:, :, 0:P]
                mm(out_m, ident_b[:, :], mask_kq[:, 0:len(ii), :], start=True, stop=False,
                   after=free + mrow_ready[b], skip=True)
            for n, i in enumerate(ii):
                for jl in range(2):
                    j = 2 * jp + jl
                    rows_ = slice(32 * j, 32 * j + 32)
                    last = mm(psum[:, 2 * s + jl, n * width:(n + 1) * width],
                              k_stack[r][rows_, i, kb * P:(kb + 1) * P], q_stack[r][rows_, i, kb * P:S],
                              start=False, stop=True, skip=True)
            pi, pfree = p_ring.take()
            dst = pair_of_tiles(pi)
            ex = act(lambda e: e.activation(dst, psum[:, 2 * s:2 * s + 2, :], ACT.Exp, scale=float(HD) ** -0.5),
                     [last] + pfree)
            pair.leave(s, [ex])
            return (b, u, kb, jp, list(ii), width, pi, ex, last)

        def value_unit(unit):
            nonlocal o_free
            b, u, kb, jp, ii, width, pi, ex, _ = unit
            weights = pair_of_tiles(pi)
            for n, i in enumerate(ii):
                for jl in range(2):
                    c = 2 * jp + jl
                    at = (4 * i + c) * (HD + 1)
                    last = mm(psum[QUAD * c:QUAD * (c + 1), 6 + i // 2, (i % 2) * S + kb * P:(i % 2 + 1) * S],
                              va_flat[:, TPB * b + kb, at:at + QUAD], weights[:, jl, n * width:(n + 1) * width],
                              start=kb == 0 and i % 2 == 0, stop=True,
                              after=[ex, gated[TPB * b + kb], va_pad] + (o_free if u == 0 else []), skip=True)
            p_ring.leave(pi, [last])
            if u == 5:
                k, free = p_ring.take()
                cp = act(lambda e: e.copy(pair_of_tiles(k), psum[:, 6:8, :]), [last] + free)
                o_free = [cp]
                turn[b] = (k, cp)
            return last

        turn = {}

        def turn_batch(b):
            k, cp = turn.pop(b)
            s, free = pair.take()
            for i in range(4):
                for qb in range(TPB):
                    at = (i % 2) * S + qb * P
                    tr = pe(lambda e, i=i, qb=qb, at=at: e.transpose(
                        psum[:, 2 * s + qb, i * P:(i + 1) * P], pair_of_tiles(k)[:, i // 2, at:at + P], ident[:, :]),
                        [cp] + free)
            p_ring.leave(k, [tr])
            o = psum[:, 2 * s:2 * s + 2, :].rearrange("p t (h d) -> p t h d", d=QUAD)
            rc = dve(lambda e: e.reciprocal(recip[:, b % 2, :, :], o[:, :, :, HD]), [tr])
            dst = hT3[:, TPB * b:TPB * (b + 1), :].rearrange("p t (h d) -> p t h d", d=HD)
            for qb in range(TPB):
                nm = dve(lambda e, qb=qb: e.tensor_tensor(
                    dst[:, qb, :, :], o[:, qb, :, 0:HD],
                    recip[:, b % 2, qb, :].unsqueeze(2).to_broadcast([P, HEADS, HD]), ALU.mult), [rc])
            pair.leave(s, [nm])
            attn_out[b] = nm

        recip = sb("recip", [P, 2, TPB, HEADS])
        attn_out = {}
        LEAD = 9
        for b in range(min(QR, B)):
            stack(b)
        m_next = 0

        def advance_max():
            nonlocal m_next
            if m_next < 6 * B:
                max_unit(m_next // 6, m_next % 6)
                m_next += 1

        b2 = sb("b2", [NE, C])
        load(s_late, b2[:, :], a["L0_ffn_b2"])
        late_in = load(s_late, wr[:, :], a["L1_ffn_w_router"])
        empty_row = sb("empty_row", [P, ROW])
        e1 = pool(lambda e: e.memset(empty_row[:, :], 0.0))
        e2 = pool(lambda e: e.memset(empty_row[:, C:C + 1], float(TOPK * TOK)), [e1])
        answers_z = answers.rearrange("(n p) c -> p n c", p=P)
        routed_z = routed.rearrange("(n p) c -> p n c", p=P)
        PIECE = SLOTS // P // 4
        background = [(s_ew, ew1[:, 0:4, :], a["L0_ffn_W1"][0:4].rearrange("e p f -> p e f")),
                      (s_ew, ew1[:, 4:8, :], a["L0_ffn_W1"][4:8].rearrange("e p f -> p e f")),
                      (s_ew, ew2[:, 0:4, :, :], a["L0_ffn_W2"][0:4].rearrange("e (k p) c -> p e k c", p=P)),
                      (s_ew, ew2[:, 4:8, :, :], a["L0_ffn_W2"][4:8].rearrange("e (k p) c -> p e k c", p=P))]
        for n in range(4):
            ns = slice(n * PIECE, (n + 1) * PIECE)
            background.append((s_fill, answers_z[:, ns, :], zeros[:, 0:C].unsqueeze(1).to_broadcast([P, PIECE, C])))
            background.append((s_fill, routed_z[:, ns, :], empty_row[:, :].unsqueeze(1).to_broadcast([P, PIECE, ROW])))
        landed = {}
        LANES = 4

        small = sb("small", [P, 2, MOD, B])

        def gated_bias(l, g, name, slot):
            return dve(lambda e: e.tensor_scalar(small[:, l, slot, :], modT[:, l, g, :], col(name), None, ALU.mult),
                       mod_ready[l] + [cols_in])

        bo_ready = gated_bias(0, 2, "L0_attn_bo", 0)

        def add_back(n, src_tmp, ready):
            i, free = psum_ring.take()
            for k in range(CT):
                tr = pe(lambda e, k=k, i=i: e.transpose(psum[:, i, k * P:(k + 1) * P],
                                                       src_tmp[:, k * P:(k + 1) * P], ident[:, :]), ready + free)
            xs = x[:, CT * n:CT * (n + 1), :]
            ad = dve(lambda e, i=i: e.tensor_tensor(xs, xs, bank(i).rearrange("p (t c) -> p t c", c=C), ALU.add),
                     [tr])
            psum_ring.leave(i, [ad])
            return tr, ad

        x1 = {}

        def project_out(n):
            yield from room(tmp_ring, 2)
            yield from room(psum_ring, spare_banks)
            i, free = psum_ring.take()
            for k in range(CT):
                t = CT * n + k
                tr = pe(lambda e, k=k, t=t: e.transpose(psum[:, i, k * P:(k + 1) * P], hT3[:, t, :], ident[:, :]),
                        [attn_out[t // TPB]] + free)
            k, tfree = tmp_ring.take()
            yield
            cp = act(lambda e: e.copy(T(k)[:, :], bank(i)), [tr] + tfree)
            psum_ring.leave(i, [cp])
            yield
            yield from room(psum_ring, spare_banks)
            j, free = psum_ring.take()
            pr = mm(bank(j), wo[:, :], T(k)[:, :], after=[cp, late_in] + free)
            yield from room(tmp_ring, 1)
            k2, tfree2 = tmp_ring.take()
            for h in range(2):
                b = 2 * n + h
                sc = act(lambda e, b=b, h=h: e.activation(
                    T(k2)[:, h * S:(h + 1) * S], psum[:, j, h * S:(h + 1) * S], ACT.Identity,
                    bias=small[:, 0, 0, b:b + 1], scale=modT[:, 0, 2, b:b + 1]), [pr, bo_ready] + tfree2)
                yield
            tmp_ring.leave(k, [pr])
            psum_ring.leave(j, [sc])
            yield from room(psum_ring, spare_banks)
            tr, ad = add_back(n, T(k2)[:, :], [sc])
            tmp_ring.leave(k2, [tr])
            x1[2 * n] = x1[2 * n + 1] = ad

        xpT = big1[:, 0:TOK]
        fvec = sb("fvec", [P, LANES, 4, TPB])
        xp_ready = {}
        FS = 1.0 / float(np.sqrt(C))
        att_done = {}
        def mixture_attention(b):
            bs = slice(b * S, (b + 1) * S)
            hr = yield from normalise(b, (0, 1))
            yield
            yield from room(psum_ring, spare_banks)
            i, free = psum_ring.take()
            for w in range(2):
                last = mm(psum[:, i, w * S:(w + 1) * S], fw[:, w, :], hT[:, bs], after=[hr] + free)
            yield from room(tmp_ring, 1)
            kq, f1 = tmp_ring.take()
            act(lambda e, kq=kq, i=i: e.activation(T(kq)[:, 0:S], psum[:, i, 0:S], ACT.Identity,
                                                   bias=col("L0_ffn_bq")), [last] + f1)
            qk = act(lambda e, kq=kq, i=i: e.activation(T(kq)[:, S:2 * S], psum[:, i, S:2 * S], ACT.Identity,
                                                        bias=col("L0_ffn_bk")))
            psum_ring.leave(i, [qk])
            yield
            yield from room(psum_ring, spare_banks)
            i, free = psum_ring.take()
            for n in range(TPB):
                last = mm(psum[:, i, n * C:(n + 1) * C], hT[:, b * S + n * P:b * S + (n + 1) * P], fw[:, 2, :],
                          after=[hr] + free)
            yield from room(tmp_ring, 1)
            kv, f2 = tmp_ring.take()
            vt = T(kv)[:, 0:TPB * C].rearrange("p (t c) -> p t c", c=C)
            yield
            vr = dve(lambda e, vt=vt, i=i: e.tensor_tensor(
                vt, psum[:, i, 0:TPB * C].rearrange("p (t c) -> p t c", c=C),
                row("L0_ffn_bv").unsqueeze(1).to_broadcast([P, TPB, C]), ALU.add), [last] + f2)
            psum_ring.leave(i, [vr])
            yield
            yield from room(psum_ring, spare_banks)
            i, free = psum_ring.take()
            for n in range(TPB):
                last = mm(psum[:, i, n * S:(n + 1) * S], T(kq)[:, n * P:(n + 1) * P], T(kq)[:, S:2 * S],
                          after=[qk] + free)
            tmp_ring.leave(kq, [last])
            fv = fvec[:, b % LANES, :, :]
            yield
            mx = dve(lambda e, fv=fv, i=i: e.tensor_reduce(
                fv[:, 0, :], bank(i).rearrange("p (t k) -> p t k", k=S), X_AXIS, ALU.max), [last])
            yield
            ng = dve(lambda e, fv=fv: e.tensor_scalar(fv[:, 1, :], fv[:, 0, :], -FS, None, ALU.mult), [mx])
            yield from room(tmp_ring, 1)
            kp, f3 = tmp_ring.take()
            for n in range(TPB):
                ex = act(lambda e, n=n, fv=fv, kp=kp, i=i: e.activation(
                    T(kp)[:, n * S:(n + 1) * S], psum[:, i, n * S:(n + 1) * S], ACT.Exp,
                    bias=fv[:, 1, n:n + 1], scale=FS, accum_out=fv[:, 2, n:n + 1]), [ng] + f3)
            psum_ring.leave(i, [ex])
            yield
            rc = dve(lambda e, fv=fv: e.reciprocal(fv[:, 3, :], fv[:, 2, :]), [ex])
            for n in range(TPB):
                sc = dve(lambda e, n=n, fv=fv, kp=kp: e.tensor_scalar(
                    T(kp)[:, n * S:(n + 1) * S], T(kp)[:, n * S:(n + 1) * S], fv[:, 3, n:n + 1], None,
                    ALU.mult), [rc])
            yield
            yield from room(psum_ring, spare_banks)
            i, free = psum_ring.take()
            for kb in range(TPB):
                for qb in range(TPB):
                    tr = pe(lambda e, kb=kb, qb=qb, kp=kp, i=i: e.transpose(
                        psum[:, i, kb * S + qb * P:kb * S + (qb + 1) * P],
                        T(kp)[:, qb * S + kb * P:qb * S + (kb + 1) * P], ident[:, :]), [sc] + free)
            tmp_ring.leave(kp, [tr])
            yield from room(tmp_ring, 1)
            kt, f4 = tmp_ring.take()
            yield
            cp = act(lambda e, kt=kt, i=i: e.copy(T(kt)[:, :], bank(i)), [tr] + f4)
            psum_ring.leave(i, [cp])
            yield
            yield from room(psum_ring, spare_banks)
            i, free = psum_ring.take()
            for kb in range(TPB):
                last = mm(psum[:, i, 0:S], vt[:, kb, :], T(kt)[:, kb * S:(kb + 1) * S], start=kb == 0,
                          stop=kb == TPB - 1, after=[cp, vr] + free)
            tmp_ring.leave(kt, [last])
            tmp_ring.leave(kv, [last])
            yield from room(tmp_ring, 1)
            ka, f5 = tmp_ring.take()
            yield
            cp = act(lambda e, ka=ka, i=i: e.copy(T(ka)[:, 0:S], psum[:, i, 0:S]), [last] + f5)
            psum_ring.leave(i, [cp])
            yield
            yield from room(psum_ring, spare_banks)
            i, free = psum_ring.take()
            last = mm(psum[:, i, 0:S], fw[:, 3, :], T(ka)[:, 0:S], after=[cp] + free)
            tmp_ring.leave(ka, [last])
            yield
            xp_ready[b] = dve(lambda e, bs=bs, i=i: e.scalar_tensor_tensor(
                xpT[:, bs], psum[:, i, 0:S], col("L0_ffn_bo"), hT[:, bs], ALU.add, ALU.add), [last] + weights_gone)
            psum_ring.leave(i, [xp_ready[b]])


        gates = sb("gates", [P, NT, NE])
        gmax = sb("gmax", [P, NT])
        def softmax8(logits, n, gm, src_i, last, bias):
            src = psum[:, src_i, 0:n * NE].rearrange("p (t e) -> p t e", e=NE)
            if bias is not None:
                s1 = dve(lambda e: e.tensor_tensor(logits, src, bias.unsqueeze(1).to_broadcast([P, n, NE]), ALU.add),
                         [last])
            else:
                s1 = dve(lambda e: e.tensor_copy(logits, src), [last])
            psum_ring.leave(src_i, [s1])
            wide = gm.unsqueeze(2).to_broadcast([P, n, NE])
            yield
            s2 = dve(lambda e: e.tensor_reduce(gm, logits, X_AXIS, ALU.max), [s1])
            yield
            s3 = dve(lambda e: e.tensor_tensor(logits, logits, wide, ALU.subtract), [s2])
            yield
            s4 = act(lambda e: e.activation(logits, logits, ACT.Exp), [s3])
            yield
            s5 = dve(lambda e: e.tensor_reduce(gm, logits, X_AXIS, ALU.add), [s4])
            yield
            s6 = dve(lambda e: e.reciprocal(gm, gm), [s5])
            yield
            return dve(lambda e: e.tensor_tensor(logits, logits, wide, ALU.mult), [s6])

        gates_ready = {}

        def mixture_gates(g):
            while (g + 1) * LG // TPB - 1 not in xp_ready:
                yield
            yield from room(psum_ring, spare_banks)
            i, free = psum_ring.take()
            for m in range(LG):
                t = g * LG + m
                last = mm(psum[:, i, m * NE:(m + 1) * NE], xpT[:, t * P:(t + 1) * P], wg[:, :],
                          after=[xp_ready[t // TPB]] + free)
            ts = slice(g * LG, (g + 1) * LG)
            r = yield from softmax8(gates[:, ts, :], LG, gmax[:, ts], i, last, row("L0_ffn_bg"))
            for t in range(g * LG, (g + 1) * LG):
                gates_ready[t] = r

        def add_mixed(n):
            while 2 * n + 1 not in xp_ready:
                yield
            yield
            yield from room(tmp_ring, 1)
            k, tfree = tmp_ring.take()
            for h in range(2):
                b = 2 * n + h
                sc = pool(lambda e, b=b, h=h: e.tensor_scalar(
                    T(k)[:, h * S:(h + 1) * S], xpT[:, b * S:(b + 1) * S], modT[:, 0, 5, b:b + 1], None, ALU.mult),
                    [xp_ready[b]] + tfree)
                yield
            yield
            tr, ad = add_back(n, T(k)[:, :], [sc])
            tmp_ring.leave(k, [tr])
            x1_mixed[2 * n] = x1_mixed[2 * n + 1] = ad

        x1_mixed = {}
        y = hT3
        gT = sb("gT", [NE, 2, CHUNK])
        gT_free = [[], []]
        y_ready = {}

        def start_sums(n):
            while CT * n + CT - 1 not in gates_ready:
                yield
            yield from room(psum_ring, spare_banks)
            i, free = psum_ring.take()
            for k in range(CT):
                t = CT * n + k
                tr = pe(lambda e, k=k, t=t: e.transpose(psum[0:NE, i, k * P:(k + 1) * P], gates[:, t, :],
                                                        ident[:, :]), [gates_ready[t]] + free)
            yield
            g = gT[:, n % 2, :]
            cp = act(lambda e: e.copy(g, psum[0:NE, i, :]), [tr] + gT_free[n % 2])
            psum_ring.leave(i, [cp])
            yield
            yield from room(psum_ring, spare_banks)
            j, free = psum_ring.take()
            for k in range(CT):
                last = mm(psum[:, j, k * C:(k + 1) * C], g[:, k * P:(k + 1) * P], b2[:, :], after=[cp, late_in] + free)
            gT_free[n % 2] = [last]
            yield
            cp = act(lambda e: e.copy(hT[:, n * CHUNK:(n + 1) * CHUNK], bank(j)), [last] + chunk_read(n))
            psum_ring.leave(j, [cp])
            for k in range(CT):
                y_ready[CT * n + k] = cp

        def chunk_read(n):
            return [xp_ready[2 * n], xp_ready[2 * n + 1]]

        order = []
        for g in range(NT // LG):
            chunks = range(g * LG // CT, (g + 1) * LG // CT)
            order += [project_out(n) for n in chunks] + [statistics((0, 1), g, x1)]
            order += [mixture_attention(b) for b in range(g * LG // TPB, (g + 1) * LG // TPB)]
            order += [mixture_gates(g)] + [task(n) for n in chunks for task in (add_mixed, start_sums)]
        per = len(order) * LG // NT
        first = Lanes(order[:per], LANES)
        ahead = Lanes(order[per:], LANES)
        spare_banks = 1
        weights_gone = []
        for k in range(8, 10):
            tmp_ring.leave(k, [gated[NT - 1]])
        for i in range(2):
            free = p_ring.lend(i)
            for k in (2 * i, 2 * i + 1):
                tmp_ring.leave(k, free)


        for _ in range(LEAD):
            advance_max()
        max_rows(0)
        rows_done = 1
        EARLY_TURNS = 4
        DELAY = 2
        waiting = []
        for e in range(6 * B):
            b, u = divmod(e, 6)
            advance_max()
            if u == 3 and background:
                st, dst, src = background.pop(0)
                landed[st] = load(st, dst, src, [e2])
            if rows_done < B and (m_next >= 6 * (rows_done + 1) + 1 or m_next == 6 * B):
                max_rows(rows_done)
                rows_done += 1
            for done in list(turn):
                turn_batch(done)
            if m_next == 6 * B and rows_done == B and not weights_gone:
                i, free = pair.take()
                for k in (2 * i, 2 * i + 1):
                    psum_ring.leave(k, free)
                weights_gone += p_ring.lend(4)
            if weights_gone:
                for _ in range(EARLY_TURNS):
                    first.advance()
            if len(waiting) == DELAY:
                unit = waiting.pop(0)
                lv = value_unit(unit)
            waiting.append(exp_unit(b, u))
            if u == 5 and b + QR < B:
                stack_free[b % QR] = [waiting[-1][-1]]
                stack(b + QR)
        for unit in waiting:
            va_read = value_unit(unit)
        turn_batch(B - 1)
        ew_in = landed[s_ew]
        answers_zero = routed_empty = fills_in = landed[s_fill]
        while pair.free:
            i, free = pair.take()
            for k in (2 * i, 2 * i + 1):
                psum_ring.leave(k, free)
        for k in (6, 7):
            psum_ring.leave(k, o_free)
        spare_banks = 3
        for i in range(2, 4):
            free = p_ring.lend(i)
            for k in (2 * i, 2 * i + 1):
                tmp_ring.leave(k, free)
        w_raw = big1[:, TOK:TOK + 5 * C].rearrange("p (g c) -> p g c", c=C)
        s_raw = stream("weights1")
        load(s_raw, w_raw[:, 0:3, :], a["L1_attn_qkv_w"].rearrange("(g p) c -> p g c", p=P), [va_read])
        load(s_raw, w_raw[:, 3, :], a["L1_attn_p1_w"])
        w_raw_in = load(s_raw, w_raw[:, 4, :], a["L1_attn_p2_w"])

        hid = big2[:, 0:2 * FC * CHUNK].rearrange("p (r f t) -> p r f t", r=2, f=FC)
        hid_ring = Ring([])
        for r in range(2):
            hid_ring.leave(r, [va_read])

        behind = Lanes([], 1)

        def pace():
            ahead.advance()
            behind.advance()

        w1_ready, w1_read = {}, {}
        parts_ring = Ring(range(2))

        def w1_part(which, e_):
            at = 2 * (e_ % 2)
            return (q_stack, k_stack)[which][e_ // 2][:, at:at + 2, :].rearrange("p a t -> p (a t)")

        def split_w1(e_, ready):
            hi, lo, w = w1_part(0, e_), w1_part(1, e_), ew1[:, e_, :]
            h = act(lambda e: e.copy(hi, w), ready)
            l = dve(lambda e: e.tensor_tensor(lo, w, hi.bitcast(F32), ALU.subtract), [h] + ready)
            w1_ready[e_] = [h, l]

        def split_x(src, ready):
            k, free = parts_ring.take()
            hi, lo = parts[2 * k], parts[2 * k + 1]
            h = act(lambda e: e.copy(hi[:, :], src), ready + free)
            l = dve(lambda e: e.tensor_tensor(lo[:, :], src, hi[:, :].bitcast(F32), ALU.subtract), [h] + free)
            return k, [h, l]

        def up(e_, xk, x_ready, func):
            r, hfree = hid_ring.take()
            done = []
            for f in range(FC):
                i, free = psum_ring.take()
                fs = slice(f * P, (f + 1) * P)
                for n, (wp, xp) in enumerate(((0, 0), (0, 1), (1, 0))):
                    last = mm(bank(i), w1_part(wp, e_)[:, fs], parts[2 * xk + xp][:, :], start=n == 0, stop=n == 2,
                              after=x_ready + free + w1_ready[e_])
                done.append(func(i, r, f, e_, last, hfree))
                pace()
            w1_read[e_] = last
            return r, done

        def down(e_, r, done):
            i, free = psum_ring.take()
            for k in range(CT):
                for f in range(FC):
                    last = mm(psum[:, i, k * C:(k + 1) * C], hid[:, r, f, k * P:(k + 1) * P], ew2[:, e_, f, :],
                              start=f == 0, stop=f == FC - 1, after=done + free)
                pace()
            hid_ring.leave(r, [last])
            return i, last

        def relu(i, r, f, e_, last, hfree):
            s = act(lambda e: e.activation(hid[:, r, f, :], bank(i), ACT.Relu,
                                           bias=col("L0_ffn_b1", e_ * FC + f)), [last] + hfree)
            psum_ring.leave(i, [s])
            return s


        def mix(n, e_, i, last):
            for k in range(CT):
                t = CT * n + k
                s = dve(lambda e, k=k, t=t: e.scalar_tensor_tensor(
                    y[:, t, :], psum[:, i, k * C:(k + 1) * C], gates[:, t, e_:e_ + 1], y[:, t, :], ALU.mult, ALU.add),
                    [last, y_ready[t]])
                y_ready[t] = s
            psum_ring.leave(i, [s])

        x2 = {}

        def add_gated(n):
            while n not in sums_ready:
                yield
            for h in range(2):
                b = 2 * n + h
                ts = slice(TPB * b, TPB * (b + 1))
                yield from room(tmp_ring, 1)
                k, tfree = tmp_ring.take()
                t3 = T(k)[:, 0:TPB * C].rearrange("p (t c) -> p t c", c=C)
                m = pool(lambda e, ts=ts, t3=t3, b=b: e.tensor_tensor(
                    t3, y[:, ts, :], gb_tok[:, b, :].unsqueeze(1).to_broadcast([P, TPB, C]), ALU.mult),
                    sums_ready[n] + tfree + [gates_tok])
                yield
                x2[b] = dve(lambda e, ts=ts, t3=t3: e.tensor_tensor(x[:, ts, :], x[:, ts, :], t3, ALU.add),
                            [m, x1_mixed[b]])
                tmp_ring.leave(k, [x2[b]])

        for g in range(5):
            i, free = psum_ring.take()
            tr = pe(lambda e, g=g, i=i: e.transpose(psum[:, i, 0:C], w_raw[:, g, :], ident[:, :]), [w_raw_in] + free)
            wt = dve(lambda e, g=g, i=i: e.tensor_copy(w_t[:, g, :], psum[:, i, 0:C]), [tr])
            psum_ring.leave(i, [wt])
        G2 = 2 * HEADS
        cen = sb("cen", [P, G2])

        def centre(t, ready):
            t3 = t.rearrange("p (g d) -> p g d", d=HD)
            s1 = dve(lambda e: e.tensor_reduce(cen[:, :], t3, X_AXIS, ALU.add), ready)
            s2 = dve(lambda e: e.tensor_scalar(cen[:, :], cen[:, :], 1.0 / HD, None, ALU.mult), [s1])
            return dve(lambda e: e.tensor_tensor(t3, t3, cen[:, :].unsqueeze(2).to_broadcast([P, G2, HD]),
                                                 ALU.subtract), [s2])

        wkv = w_t[:, 1:3, :].rearrange("p g c -> p (g c)")
        wkv_ready = centre(wkv, [wt])
        bkv = rows[:, ROWS["L1_attn_qkv_b"][0] + C:ROWS["L1_attn_qkv_b"][0] + 3 * C]
        bkv_ready = centre(bkv, [wkv_ready])
        temp_blk, bias_blk = wqk[:, 0, :], wqk[:, 1, :]
        tcol = sb("tcol", [P, 1])
        s_blk = stream("blocks")
        z6 = pool(lambda e: e.memset(temp_blk[:, :], 1.0 / S), [va_read])
        z7 = pool(lambda e: e.memset(bias_blk[:, :], 0.0), [va_read])
        for h in range(HEADS):
            hs = slice(h * HD, (h + 1) * HD)
            load(s_blk, tcol[hs, :], a["L1_attn_temperature"][h, :, :].to_broadcast([HD, 1]))
            blk_in = load(s_blk, bias_blk[hs, hs], a["L1_attn_attn_bias"][h, :, :], [z7])
        t3 = temp_blk[:, :].rearrange("p (h d) -> p h d", d=HD)
        z8 = select(t3, [[-HD, HEADS], [0, HD]], 1, 0, 0.0, ALU.is_ge, [z6])
        z9 = select(t3, [[HD, HEADS], [0, HD]], -1, HD - 1, 0.0, ALU.is_ge, [z8])
        blk_ready = dve(lambda e: e.tensor_scalar(temp_blk[:, :], temp_blk[:, :], tcol[:, 0:1], None, ALU.mult),
                        [z9, blk_in])
        gam = sb("gam", [P, G2, HD])
        bet = sb("bet", [P, G2, HD])
        for half, nm in ((0, "kn"), (1, "vn")):
            for dst, wh in ((gam, "g"), (bet, "b")):
                affine = pool(lambda e, half=half, dst=dst, nm=nm, wh=wh: e.tensor_copy(
                    dst[:, half * HEADS:(half + 1) * HEADS, :],
                    row(f"L1_attn_{nm}_{wh}").unsqueeze(1).to_broadcast([P, HEADS, HD])), [rows_in])
        p2_ready = gated_bias(1, 2, "L1_attn_p2_b", 0)

        var, vrs = (sb(name, [P, LANES, TPB * G2]) for name in ("var", "vrs"))
        x3 = {}

        def linear_attention(b):
            bs = slice(b * S, (b + 1) * S)
            hr = yield from normalise(b, (1, 0))
            yield
            yield from room(psum_ring, 3)
            i, free = psum_ring.take()
            last = mm(psum[:, i, 0:S], w_t[:, 0, :], hT[:, bs], after=[hr, wt] + free)
            yield from room(tmp_ring, 1)
            kq, f1 = tmp_ring.take()
            yield
            qs = act(lambda e, kq=kq, i=i: e.activation(T(kq)[:, 0:S], psum[:, i, 0:S], ACT.Identity,
                                                        bias=col("L1_attn_qkv_b")), [last] + f1)
            psum_ring.leave(i, [qs])
            yield
            yield from room(psum_ring, 3)
            i, free = psum_ring.take()
            for n in range(TPB):
                last = mm(psum[:, i, n * 2 * C:(n + 1) * 2 * C], hT[:, b * S + n * P:b * S + (n + 1) * P], wkv,
                          after=[hr, wkv_ready] + free)
            yield from room(tmp_ring, 1)
            kk, f2 = tmp_ring.take()
            t2 = T(kk)[:, :].rearrange("p (t n) -> p t n", n=2 * C)
            yield
            kvb = dve(lambda e, t2=t2, i=i: e.tensor_tensor(
                t2, bank(i).rearrange("p (t n) -> p t n", n=2 * C), bkv.unsqueeze(1).to_broadcast([P, TPB, 2 * C]),
                ALU.add), [last, bkv_ready] + f2)
            psum_ring.leave(i, [kvb])
            yield from room(tmp_ring, 1)
            ks, f3 = tmp_ring.take()
            yield
            sq = act(lambda e, ks=ks, kk=kk: e.activation(T(ks)[:, :], T(kk)[:, :], ACT.Square), [kvb] + f3)
            vv = var[:, b % LANES, :]
            yield
            s1 = dve(lambda e, ks=ks, vv=vv: e.tensor_reduce(
                vv, T(ks)[:, :].rearrange("p (g d) -> p g d", d=HD), X_AXIS, ALU.add), [sq])
            yield
            s2 = dve(lambda e, vv=vv: e.tensor_scalar(vv, vv, 1.0 / HD, EPS, ALU.mult, ALU.add), [s1])
            vr_ = vrs[:, b % LANES, :]
            s3 = yield from rsqrt(vr_, vv, T(ks)[:, 0:TPB * G2], [s2])
            tmp_ring.leave(ks, [s3])
            kg = T(kk)[:, :].rearrange("p (g d) -> p g d", d=HD)
            yield
            s4 = dve(lambda e, kg=kg, vr_=vr_: e.tensor_tensor(
                kg, kg, vr_.unsqueeze(2).to_broadcast([P, TPB * G2, HD]), ALU.mult), [s3])
            g2 = gam[:, :, :].rearrange("p g d -> p (g d)").unsqueeze(1).to_broadcast([P, TPB, 2 * C])
            be2 = bet[:, :, :].rearrange("p g d -> p (g d)").unsqueeze(1).to_broadcast([P, TPB, 2 * C])
            yield
            s5 = pool(lambda e, t2=t2, g2=g2: e.tensor_tensor(t2, t2, g2, ALU.mult), [s4, affine])
            yield
            s6 = pool(lambda e, t2=t2, be2=be2: e.tensor_tensor(t2, t2, be2, ALU.add), [s5])
            yield
            yield from room(psum_ring, 3)
            i, free = psum_ring.take()
            for n in range(TPB):
                last = mm(psum[:, i, 0:C], t2[:, n, 0:C], t2[:, n, C:2 * C], start=n == 0, stop=n == TPB - 1,
                          after=[s6] + free)
            tmp_ring.leave(kk, [last])
            yield from room(tmp_ring, 1)
            kb_, f4 = tmp_ring.take()
            yield
            s7 = dve(lambda e, kb_=kb_, i=i: e.tensor_tensor(T(kb_)[:, 0:C], psum[:, i, 0:C], temp_blk[:, :],
                                                             ALU.mult), [last, blk_ready] + f4)
            psum_ring.leave(i, [s7])
            yield
            s8 = dve(lambda e, kb_=kb_: e.tensor_tensor(T(kb_)[:, 0:C], T(kb_)[:, 0:C], bias_blk[:, :],
                                                        ALU.add), [s7])
            yield
            yield from room(psum_ring, 3)
            i, free = psum_ring.take()
            last = mm(psum[:, i, 0:S], T(kb_)[:, 0:C], T(kq)[:, 0:S], after=[s8, qs] + free)
            tmp_ring.leave(kb_, [last])
            tmp_ring.leave(kq, [last])
            yield from room(tmp_ring, 1)
            ka, f5 = tmp_ring.take()
            yield
            at = dve(lambda e, ka=ka, i=i, bs=bs: e.tensor_tensor(T(ka)[:, 0:S], psum[:, i, 0:S], hT[:, bs],
                                                                  ALU.add), [last] + f5)
            psum_ring.leave(i, [at])
            yield
            yield from room(psum_ring, 3)
            i, free = psum_ring.take()
            last = mm(psum[:, i, 0:S], w_t[:, 3, :], T(ka)[:, 0:S], after=[at] + free)
            tmp_ring.leave(ka, [last])
            yield from room(tmp_ring, 1)
            kh, f6 = tmp_ring.take()
            yield
            ge = act(lambda e, kh=kh, i=i: e.activation(T(kh)[:, 0:S], psum[:, i, 0:S], ACT.Gelu,
                                                        bias=col("L1_attn_p1_b")), [last] + f6)
            psum_ring.leave(i, [ge])
            yield
            yield from room(psum_ring, 3)
            i, free = psum_ring.take()
            last = mm(psum[:, i, 0:S], w_t[:, 4, :], T(kh)[:, 0:S], after=[ge] + free)
            tmp_ring.leave(kh, [last])
            yield from room(tmp_ring, 1)
            ko, f7 = tmp_ring.take()
            yield
            o1 = dve(lambda e, ko=ko, i=i, bs=bs: e.tensor_tensor(T(ko)[:, 0:S], psum[:, i, 0:S], hT[:, bs],
                                                                  ALU.add), [last] + f7)
            psum_ring.leave(i, [o1])
            yield
            o2 = act(lambda e, ko=ko, b=b: e.activation(
                T(ko)[:, 0:S], T(ko)[:, 0:S], ACT.Identity, bias=small[:, 1, 0, b:b + 1],
                scale=modT[:, 1, 2, b:b + 1]), [o1, p2_ready])
            yield
            yield from room(psum_ring, 3)
            i, free = psum_ring.take()
            for n in range(TPB):
                tr = pe(lambda e, n=n, ko=ko, i=i: e.transpose(psum[:, i, n * P:(n + 1) * P],
                                                              T(ko)[:, n * P:(n + 1) * P], ident[:, :]),
                        [o2] + free)
            tmp_ring.leave(ko, [tr])
            ts = slice(TPB * b, TPB * (b + 1))
            yield
            x3[b] = dve(lambda e, ts=ts, i=i: e.tensor_tensor(
                x[:, ts, :], x[:, ts, :], psum[:, i, 0:S].rearrange("p (t c) -> p t c", c=C), ALU.add), [tr])
            psum_ring.leave(i, [x3[b]])

        RG = LG
        sc = sb("scores", [P, NT, NE])
        desc = sb("desc", [P, NE])
        capbase = sb("capbase", [P, NE])
        taken = sb("taken", [P, NE])
        for e_ in range(NE):
            pool(lambda e, e_=e_: e.memset(desc[:, e_:e_ + 1], float(NE - e_)))
            pool(lambda e, e_=e_: e.memset(capbase[:, e_:e_ + 1], float(CAP * e_)))
        pool(lambda e: e.memset(taken[:, :], 0.0))
        dest = sb("dest", [P, TOPK, NT], I32)
        tables = pool(lambda e: e.iota(dest[:, :, :], pattern=[[TOK, TOPK], [P, NT]], base=0, channel_multiplier=1))
        best = sb("best", [P, RG])
        TAB = TOK + 5 * C + 2 * CHUNK

        def carve(n):
            return big1[:, TAB + n * RG * NE:TAB + (n + 1) * RG * NE]

        pick = [carve(k).rearrange("p (t e) -> p t e", e=NE) for k in range(TOPK)]
        left = carve(2).rearrange("p (t e) -> p t e", e=NE)
        tot, run, keep = (carve(k).rearrange("p (e t) -> p e t", t=RG) for k in (3, 4, 5))
        k1 = pool(lambda e: e.memset(keep, 1.0), [w_raw_in])
        keep_ready = pool(lambda e: e.memset(keep[:, :, 0:1], 0.0), [k1])
        slot_f, rank_f, wts = (dst_[:, :, k * TOPK:(k + 1) * TOPK].rearrange("p t k -> p k t") for k in range(3))
        slot_i = sb("slot_i", [P, TOPK, NT], I32)
        sel = sb("sel", [P, NE, RG], BF16)
        ROWS_AT = 2 * FC * CHUNK
        rows_buf = big2[:, ROWS_AT:ROWS_AT + 2 * TPB * TOPK * ROW].rearrange(
            "p (r t k n) -> p r t k n", r=2, t=TPB, k=TOPK)
        s_sc = [stream(f"scatter{i}") for i in range(2)]
        rows_sent = [[va_read], [va_read]]
        routed_groups, h4 = set(), {}

        def over(t):
            return t.unsqueeze(2).to_broadcast([P, RG, NE])

        def wide(t):
            return t[:, :].unsqueeze(1).to_broadcast([P, RG, NE])

        def route(g):
            ts = slice(g * RG, (g + 1) * RG)
            while g and g - 1 not in routed_groups:
                yield
            yield from statistics((1, 1), g, x3)
            for b in range(g * RG // TPB, (g + 1) * RG // TPB):
                h4[b] = yield from normalise(b, (1, 1))
                yield
            yield from room(psum_ring, 3)
            i, free = psum_ring.take()
            for m in range(RG):
                t = g * RG + m
                last = mm(psum[:, i, m * NE:(m + 1) * NE], hT[:, t * P:(t + 1) * P], wr[:, :],
                          after=[h4[t // TPB]] + free)
            s_ = sc[:, ts, :]
            scored = yield from softmax8(s_, RG, gmax[:, ts], i, last, None)
            yield
            ready = dve(lambda e: e.tensor_copy(left, s_), [scored])
            for k in range(TOPK):
                pk, w = pick[k], wts[:, k, ts]
                yield
                r1 = dve(lambda e, w=w: e.tensor_reduce(w, left, X_AXIS, ALU.max), [ready])
                yield
                r2 = dve(lambda e, pk=pk, w=w: e.tensor_tensor(pk, left, over(w), ALU.is_equal), [r1])
                yield
                r3 = dve(lambda e, pk=pk: e.tensor_tensor(pk, pk, wide(desc), ALU.mult), [r2, tables])
                yield
                r4 = dve(lambda e, pk=pk: e.tensor_reduce(best[:, :], pk, X_AXIS, ALU.max), [r3])
                yield
                r5 = dve(lambda e, pk=pk: e.tensor_tensor(pk, pk, over(best[:, :]), ALU.is_equal), [r4])
                yield
                ready = dve(lambda e, pk=pk: e.scalar_tensor_tensor(left, pk, -2.0, left, ALU.mult, ALU.add), [r5])
            yield
            sl = dve(lambda e: e.tensor_tensor(sel[:, :, :].rearrange("p e t -> p t e"), pick[0], pick[1], ALU.add),
                     [ready])
            yield
            yield from room(psum_ring, 3)
            iw, free1 = psum_ring.take()
            yield from room(psum_ring, 3)
            it, free2 = psum_ring.take()
            flat = sel[:, :, :].rearrange("p e t -> p (e t)")
            mw = mm(psum[:, iw, 0:NE * RG], before[:, :], flat, after=[sl, counters] + free1)
            mt = mm(psum[:, it, 0:NE * RG], ones_b[:, :], flat, after=free2)
            yield
            c1 = dve(lambda e: e.tensor_copy(tot, psum[:, it, 0:NE * RG].rearrange("p (e t) -> p e t", t=RG)), [mt])
            psum_ring.leave(it, [c1])
            yield
            c2 = dve(lambda e: e.tensor_tensor_scan(
                run.rearrange("p e t -> p (e t)"), keep.rearrange("p e t -> p (e t)"),
                tot.rearrange("p e t -> p (e t)"), 0.0, ALU.mult, ALU.add), [c1, keep_ready])
            yield
            c3 = dve(lambda e: e.tensor_tensor(tot, run, tot, ALU.subtract), [c2])
            yield
            c4 = dve(lambda e: e.tensor_tensor(tot, tot, taken[:, :].unsqueeze(2).to_broadcast([P, NE, RG]), ALU.add),
                     [c3])
            yield
            c5 = dve(lambda e: e.tensor_tensor(
                tot, psum[:, iw, 0:NE * RG].rearrange("p (e t) -> p e t", t=RG), tot, ALU.add), [c4, mw])
            psum_ring.leave(iw, [c5])
            c6 = dve(lambda e: e.tensor_tensor(taken[:, :], taken[:, :], run[:, :, RG - 1], ALU.add), [c4])
            rank = tot.rearrange("p e t -> p t e")
            for k in range(TOPK):
                sf, rf = slot_f[:, k, ts], rank_f[:, k, ts]
                yield
                d1 = dve(lambda e, k=k: e.tensor_tensor(left, pick[k], rank, ALU.mult), [c5])
                yield
                d2 = dve(lambda e, rf=rf: e.tensor_reduce(rf, left, X_AXIS, ALU.add), [d1])
                yield
                d3 = dve(lambda e, k=k: e.tensor_tensor(left, pick[k], wide(capbase), ALU.mult), [d2])
                yield
                d4 = dve(lambda e, sf=sf: e.tensor_reduce(sf, left, X_AXIS, ALU.add), [d3])
                yield
                d5 = dve(lambda e, sf=sf, rf=rf: e.tensor_tensor(sf, sf, rf, ALU.add), [d4])
                d6 = dve(lambda e, rf=rf: e.tensor_scalar(rf, rf, float(CAP), float(SLOTS), ALU.is_ge, ALU.mult), [d5])
                yield
                d7 = dve(lambda e, sf=sf, rf=rf: e.tensor_tensor(sf, sf, rf, ALU.add), [d6])
                yield
                slots = dve(lambda e, sf=sf, k=k: e.tensor_copy(slot_i[:, k, ts], sf), [d7, c6])
            routed_groups.add(g)
            for b in range(g * RG // TPB, (g + 1) * RG // TPB):
                r = b % 2
                bt = slice(TPB * b, TPB * (b + 1))
                yield
                m1 = dve(lambda e, r=r, bt=bt: e.tensor_copy(
                    rows_buf[:, r, :, :, C], dest[:, :, bt].rearrange("p k t -> p t k")), [tables] + rows_sent[r])
                m2 = dve(lambda e, r=r, bt=bt: e.tensor_copy(
                    rows_buf[:, r, :, :, C + 1], wts[:, :, bt].rearrange("p k t -> p t k")), rows_sent[r])
                yield from room(psum_ring, 3)
                i, free = psum_ring.take()
                for m in range(TPB):
                    t = TPB * b + m
                    tr = pe(lambda e, m=m, t=t, i=i: e.transpose(psum[:, i, m * P:(m + 1) * P],
                                                                hT[:, t * P:(t + 1) * P], ident[:, :]),
                            [h4[b]] + free)
                yield
                src = psum[:, i, 0:S].rearrange("p (t c) -> p t c", c=C)
                ca = act(lambda e, r=r, src=src: e.copy(rows_buf[:, r, :, 0, 0:C], src), [tr] + rows_sent[r])
                yield
                cb = dve(lambda e, r=r, src=src: e.tensor_copy(rows_buf[:, r, :, 1, 0:C], src), [ca] + rows_sent[r])
                psum_ring.leave(i, [cb])
                for m in range(TPB):
                    t = TPB * b + m
                    for k in range(TOPK):
                        d = q.dma("gpsimd", s_sc[r], lambda e, k=k, t=t, m=m, r=r: e.indirect_dma_start(
                            out=routed, out_offset=bass.IndirectOffsetOnAxis(ap=slot_i[:, k, t:t + 1], axis=0),
                            in_=rows_buf[:, r, m, k, :], in_offset=None, bounds_check=SLOTS - 1,
                            oob_is_err=False), [ca, cb, m1, m2, slots, routed_empty])
                    yield
                rows_sent[r] = [d]
                h4_read[0] = tr

        h4_read = [None]

        sums_ready = {}
        order = []
        for t in with_statistics((1, 0), linear_attention, x2):
            if t.__name__ == "linear_attention":
                b = sum(o.__name__ == "linear_attention" for o in order)
                order.append(t)
                if (b + 1) * TPB % RG == 0:
                    order.append(route(b * TPB // RG))
            else:
                order += [add_gated(n) for n in range(sum(o.__name__ == "add_gated" for o in order),
                                                      NCH)][:LG // CT]
                order.append(t)
        behind = Lanes(order, 5)
        pending = None
        SPLIT_AHEAD = 2

        def settle():
            pn, pe_, pr, pdone = pending
            i, last = down(pe_, pr, pdone)
            mix(pn, pe_, i, last)
            if pe_ == NE - 1:
                sums_ready[pn] = [y_ready[CT * pn + k] for k in range(CT)]
            return last

        def chunk_emitted(n):
            return CT * n + CT - 1 in y_ready and 2 * n + 1 in x1_mixed

        def split_chunk(n):
            return split_x(xpT[:, n * CHUNK:(n + 1) * CHUNK], [xp_ready[2 * n], xp_ready[2 * n + 1]])

        next_x = None
        for n in range(NCH):
            while not chunk_emitted(n):
                first.advance()
                ahead.advance()
            xk, x_ready = next_x or split_chunk(n)
            next_x = None
            if n == 0:
                for e_ in range(SPLIT_AHEAD):
                    split_w1(e_, [ew_in, va_read])
            for e_ in range(NE):
                if n == 0 and e_ + SPLIT_AHEAD < NE:
                    split_w1(e_ + SPLIT_AHEAD, [ew_in, va_read])
                r, done = up(e_, xk, x_ready, relu)
                if e_ == NE - 2 and n + 1 < NCH and 2 * n + 3 in xp_ready:
                    next_x = split_chunk(n + 1)
                if pending:
                    last_l0 = settle()
                if n == NCH - 1:
                    split_w1(e_, [ew1_in, w1_read[e_]])
                pending = (n, e_, r, done)
            if n == 0:
                s_ew2 = stream("experts1")
                ew1_in = load(s_ew2, ew1[:, :, :], a["L1_ffn_w1"].rearrange("e p f -> p e f"),
                              w1_ready[NE - 1] + w1_ready[NE - 2])
                gates_tok = spread_gates(0, [part3_filled, fills_in])
            parts_ring.leave(xk, [w1_read[NE - 1]])
        last_l0 = settle()
        s_ew3 = stream("experts1_second")
        ew2_read = load(s_ew3, ew2[:, :, :, :], a["L1_ffn_w2"].rearrange("e (k p) c -> p e k c", p=P), [last_l0])
        ew2_in = {e_: ew2_read for e_ in range(NE)}
        while behind.advance():
            pass
        all_sent = rows_sent[0] + rows_sent[1]

        UNITS = SLOTS // CHUNK
        RINGS = 4
        xb = big1[:, 0:RINGS * CT * ROW].rearrange("p (r n c) -> p r n c", r=RINGS, c=ROW)
        ans_buf = hT[:, 0:RINGS * CHUNK].rearrange("p (r n c) -> p r n c", r=RINGS, c=C)
        to = sb("to", [P, RINGS, CT], I32)
        s_xb = [stream(f"xb{i}") for i in range(RINGS)]
        s_out = [stream(f"ans{i}") for i in range(RINGS)]
        routed_v = routed.rearrange("(u n p) c -> u p n c", p=P, n=CT)
        xb_left = [[] for _ in range(RINGS)]
        ans_sent = [[] for _ in range(RINGS)]
        xb_in = {}

        def fetch(unit):
            k = unit % RINGS
            xb_in[unit] = load(s_xb[k], xb[:, k, :, :], routed_v[unit], all_sent + xb_left[k])

        def feature_major(unit):
            k = unit % RINGS
            i, free = psum_ring.take()
            for m in range(CT):
                tr = pe(lambda e, m=m: e.transpose(psum[:, i, m * P:(m + 1) * P], xb[:, k, m, 0:C], ident[:, :]),
                        [xb_in[unit]] + free)
            kx, made = split_x(bank(i), [tr])
            psum_ring.leave(i, made)
            return kx, made

        def gelu(i, r, f, e_, last, hfree):
            s = act(lambda e: e.activation(hid[:, r, f, :], bank(i), ACT.Gelu_apprx_tanh), [last] + hfree)
            psum_ring.leave(i, [s])
            return s

        def answer(unit, r, done):
            k = unit % RINGS
            i, last = down(unit * CHUNK // CAP, r, done)
            to_in = dve(lambda e: e.tensor_copy(to[:, k, :], xb[:, k, :, C]), [xb_in[unit]] + ans_sent[k])
            for m in range(CT):
                s = dve(lambda e, m=m: e.tensor_scalar(ans_buf[:, k, m, :], psum[:, i, m * C:(m + 1) * C],
                                                       xb[:, k, m, C + 1:C + 2], None, ALU.mult),
                        [last, rows_read] + ans_sent[k])
            psum_ring.leave(i, [s])
            for m in range(CT):
                d = q.dma("gpsimd", s_out[k], lambda e, m=m: e.indirect_dma_start(
                    out=answers, out_offset=bass.IndirectOffsetOnAxis(ap=to[:, k, m:m + 1], axis=0),
                    in_=ans_buf[:, k, m, :], in_offset=None, bounds_check=TOPK * TOK - 1, oob_is_err=False),
                    [s, to_in, answers_zero])
            ans_sent[k] = [d]
            xb_left[k] = [s]

        rows_read = h4_read[0]
        AHEAD = 2
        for unit in range(AHEAD):
            fetch(unit)
        ready_x = feature_major(0)
        pending = None
        for unit in range(UNITS):
            if unit + AHEAD < UNITS:
                fetch(unit + AHEAD)
            kx, made = ready_x
            if unit + 1 < UNITS:
                ready_x = feature_major(unit + 1)
            r, done = up(unit * CHUNK // CAP, kx, made, gelu)
            parts_ring.leave(kx, [w1_read[unit * CHUNK // CAP]])
            if unit == 1:
                gates_tok = spread_gates(1, [x2[b] for b in range(B)])
                biased = []
                for b in range(B):
                    k, tfree = tmp_ring.take()
                    m = pool(lambda e, k=k, b=b: e.tensor_tensor(T(k)[:, 0:C], gb_tok[:, b, :], row("L1_ffn_bias"), ALU.mult),
                             tfree + [gates_tok])
                    biased.append(pool(lambda e, k=k, b=b: e.tensor_tensor(
                        x[:, TPB * b:TPB * (b + 1), :], x[:, TPB * b:TPB * (b + 1), :],
                        T(k)[:, 0:C].unsqueeze(1).to_broadcast([P, TPB, C]), ALU.add), [m, x3[b]]))
                    tmp_ring.leave(k, [biased[-1]])
                biased = biased[-1:]
            if pending:
                answer(*pending)
            pending = (unit, r, done)
        answer(*pending)

        out_v = out.rearrange("b (t p) c -> p (b t) c", p=P)
        s_y = [stream(f"yin{i}") for i in range(4)]
        s_res = stream("result")
        ans_v = answers.rearrange("(k n p) c -> k p n c", k=TOPK, p=P)
        YR = 4
        yb = [t[:, h * 2 * CHUNK:(h + 1) * 2 * CHUNK].rearrange("p (k t c) -> p k t c", k=TOPK, c=C)
              for t in (big1, hT) for h in range(YR // 2)]
        yfree = [[] for _ in range(YR)]
        s_last = [d for sent in ans_sent for d in sent]
        arrived = {}

        def fetch_answers(n):
            for k in range(TOPK):
                arrived[n] = load(s_y[n % YR], yb[n % YR][:, k, :, :], ans_v[k, :, CT * n:CT * (n + 1), :],
                                  s_last + yfree[n % YR])

        for n in range(YR):
            fetch_answers(n)
        for n in range(NCH):
            r = n % YR
            ts = slice(CT * n, CT * (n + 1))
            both = yb[r][:, 0, :, :]
            s1 = dve(lambda e, r=r, both=both: e.tensor_tensor(both, both, yb[r][:, 1, :, :], ALU.add), [arrived[n]])
            m = dve(lambda e, n=n, both=both: e.tensor_tensor(
                both.rearrange("p (b t) c -> p b t c", t=TPB), both.rearrange("p (b t) c -> p b t c", t=TPB),
                gb_tok[:, 2 * n:2 * n + 2, :].unsqueeze(2).to_broadcast([P, 2, TPB, C]), ALU.mult), [s1, gates_tok])
            ad = dve(lambda e, ts=ts, both=both: e.tensor_tensor(x[:, ts, :], x[:, ts, :], both, ALU.add),
                     [m] + biased)
            yfree[r] = [ad]
            if n + YR < NCH:
                fetch_answers(n + YR)
            res = load(s_res, out_v[:, ts, :], x[:, ts, :], [ad])

        q.number()
        block = ctx.enter_context(nc.Block())

        @block.sync
        def _(eng):
            q.play("sync", eng)
            for st in [s_res, s_fill] + s_part + s_sc + s_out:
                eng.wait_ge(st.sem, st.count)

        @block.tensor
        def _(eng):
            q.play("tensor", eng)

        @block.vector
        def _(eng):
            q.play("vector", eng)

        @block.scalar
        def _(eng):
            q.play("scalar", eng)

        @block.gpsimd
        def _(eng):
            q.play("gpsimd", eng)


def kernel(**inputs):
    import concourse.bacc as bacc
    from concourse.bass_utils import run_bass_kernel_spmd

    nc = bacc.Bacc("TRN2", target_bir_lowering=False, num_devices=1)
    arrays, aps = {}, {}
    for name, value in inputs.items():
        v = np.ascontiguousarray(value)
        arrays[f"in_{name}"] = v
        aps[name] = nc.dram_tensor(f"in_{name}", v.shape, mybir.dt.from_np(v.dtype), kind="ExternalInput").ap()
    out = nc.dram_tensor("out", (B, S, C), F32, kind="ExternalOutput").ap()
    build(nc, aps, out)
    r = run_bass_kernel_spmd(nc, [arrays], core_ids=[0])
    return r.results[0]["out"]
```
